# Optimizing a Trainium2 kernel written in Bass

```python
import numpy as np
import jax
import jax.numpy as jnp

def _softmax(x, axis=-1):
    return jax.nn.softmax(x, axis=axis)

def _gelu(x):
    return jax.nn.gelu(x, approximate=True)

def _silu(x):
    return jax.nn.silu(x)

def _sigmoid(x):
    return jax.nn.sigmoid(x)

def _layernorm(x, axis=-1, eps=1e-05):
    m = jnp.mean(x, axis=axis, keepdims=True)
    v = jnp.var(x, axis=axis, keepdims=True)
    return (x - m) / jnp.sqrt(v + eps)

def _scatter_add(tgt, idx, src, axis=0):
    return tgt.at[idx].add(src)

def _segment_sum(src, seg, n):
    return jax.ops.segment_sum(src, seg, n)
kernel_name = 'mk_metaformer_d4_conv_nchw512_r4_eb0edb'

def setup_inputs(seed: int=0):
    np.random.seed(seed)
    _w = jnp.asarray

    def _rec_inputs():
        import jax
        import jax.numpy as jnp
        _gk = jax.random.key(seed)
        x = -0.0003929 + 0.9999 * jax.random.normal(jax.random.fold_in(_gk, 1), (8, 128, 16, 16), jnp.float32)
        return x
    x = _rec_inputs()

    def _L0_conv_setup():
        import jax, jax.numpy as jnp
        from jax import lax
        import numpy as np
        UP = 2
        DOWN = 2
        PADDING = (11, 10, 11, 10)
        GAIN = float(np.sqrt(2.0))
        SLOPE = 0.2
        CLAMP = 256.0
        UP_TAPS = 12
        IN_CUTOFF = 8.0
        OUT_CUTOFF = 8.0
        IN_HALF_WIDTH = 6.0
        OUT_HALF_WIDTH = 6.0
        TEMP_FS = 32.0

        def _design_lowpass(numtaps, cutoff, width, fs):
            nyq = fs / 2.0
            atten = 2.285 * (numtaps - 1) * np.pi * (width / nyq) + 7.95
            if atten > 50.0:
                beta = 0.1102 * (atten - 8.7)
            elif atten > 21.0:
                beta = 0.5842 * (atten - 21.0) ** 0.4 + 0.07886 * (atten - 21.0)
            else:
                beta = 0.0
            m = np.arange(numtaps) - (numtaps - 1) / 2.0
            c = cutoff / nyq
            h = c * np.sinc(c * m)
            h = h * np.kaiser(numtaps, beta)
            h = h / np.sum(h)
            return h.astype(np.float32)

        def _upfirdn2d_sep(x, f, up, down, pad, gain):
            N, C, H, W = x.shape
            fr = f[::-1].astype(x.dtype)
            kH = fr.reshape(1, 1, -1, 1)
            kW = fr.reshape(1, 1, 1, -1)
            px0, px1, py0, py1 = pad
            xr = x.reshape(N * C, 1, H, W)
            xr = lax.conv_general_dilated(xr, kH, window_strides=(down, 1), padding=((py0, py1 + up - 1), (0, 0)), lhs_dilation=(up, 1))
            xr = lax.conv_general_dilated(xr, kW, window_strides=(1, down), padding=((0, 0), (px0, px1 + up - 1)), lhs_dilation=(1, up))
            Ho, Wo = (xr.shape[2], xr.shape[3])
            return xr.reshape(N, C, Ho, Wo) * gain
        key = jax.random.key(seed)
        k1, k2 = jax.random.split(key)
        x = jax.random.normal(k1, (8, 128, 16, 16), dtype=jnp.float32)
        bias = jax.random.normal(k2, (128,), dtype=jnp.float32) * 0.1
        up_filter = jnp.asarray(_design_lowpass(UP_TAPS, IN_CUTOFF, IN_HALF_WIDTH * 2, TEMP_FS))
        down_filter = jnp.asarray(_design_lowpass(UP_TAPS, OUT_CUTOFF, OUT_HALF_WIDTH * 2, TEMP_FS))
        return {'x': x, 'bias': bias, 'up_filter': up_filter, 'down_filter': down_filter}
    _L0_conv_all = _L0_conv_setup()
    _L0_conv_in = {k: v for k, v in _L0_conv_all.items() if k in ('bias', 'up_filter', 'down_filter')}
    del _L0_conv_all

    def _L0_ffn_setup():
        import jax, jax.numpy as jnp
        import numpy as np
        B, L, D, H, E, K = (8, 2048, 128, 512, 8, 2)
        SCALE = 0.02
        key = jax.random.key(seed)
        ks = jax.random.split(key, 6)
        return {'x': jax.random.normal(ks[0], (B, L, D), dtype=jnp.float32), 'Wg': jax.random.normal(ks[1], (D, E), dtype=jnp.float32) * SCALE, 'W1': jax.random.normal(ks[2], (E, D, H), dtype=jnp.float32) * SCALE, 'b1': jax.random.normal(ks[3], (E, H), dtype=jnp.float32) * SCALE, 'W2': jax.random.normal(ks[4], (E, H, D), dtype=jnp.float32) * SCALE, 'b2': jax.random.normal(ks[5], (E, D), dtype=jnp.float32) * SCALE}
    _L0_ffn_all = _L0_ffn_setup()
    _L0_ffn_in = {k: v for k, v in _L0_ffn_all.items() if k in ('Wg', 'W1', 'b1', 'W2', 'b2')}
    del _L0_ffn_all

    def _L1_conv_setup():
        import jax, jax.numpy as jnp
        import numpy as np
        DIM = 8
        EPS_ATT = 1e-15
        BN_EPS = 1e-05

        def conv2d(x, w, groups=1, padding=0):
            return jax.lax.conv_general_dilated(x, w, window_strides=(1, 1), padding=[(padding, padding), (padding, padding)], dimension_numbers=('NCHW', 'OIHW', 'NCHW'), feature_group_count=groups)
        key = jax.random.key(seed)
        ks = jax.random.split(key, 8)
        B, C, H, W = (8, 128, 16, 16)
        TD = 128
        s = lambda k, shape, fan: jax.random.normal(k, shape, jnp.float32) * (1.0 / np.sqrt(fan))
        return {'x': jax.random.normal(ks[0], (B, C, H, W), jnp.float32), 'qkv_w': s(ks[1], (3 * TD, C, 1, 1), C), 'agg_dw_w': s(ks[2], (3 * TD, 1, 5, 5), 25), 'agg_pw_w': s(ks[3], (3 * TD, 3 * TD // (3 * 16), 1, 1), 8), 'proj_w': s(ks[4], (C, 2 * TD, 1, 1), 2 * TD), 'bn_gamma': jnp.ones((C,), jnp.float32), 'bn_beta': jnp.zeros((C,), jnp.float32), 'bn_mean': jax.random.normal(ks[5], (C,), jnp.float32) * 0.1, 'bn_var': jax.random.uniform(ks[6], (C,), jnp.float32, 0.5, 1.5)}
    _L1_conv_all = _L1_conv_setup()
    _L1_conv_in = {k: v for k, v in _L1_conv_all.items() if k in ('qkv_w', 'agg_dw_w', 'agg_pw_w', 'proj_w', 'bn_gamma', 'bn_beta', 'bn_mean', 'bn_var')}
    del _L1_conv_all

    def _L1_ffn_setup():
        import jax, jax.numpy as jnp
        import numpy as np
        B, C, IN_LEN, OUT_LEN, E, TOP_K, N_I = (1, 2048, 128, 128, 8, 2, 16)
        key = jax.random.key(seed)
        ks = jax.random.split(key, 8)
        w = lambda k, shape, sc=0.02: jax.random.normal(k, shape, dtype=jnp.float32) * sc
        return {'x': jax.random.normal(ks[0], (B, C, IN_LEN), dtype=jnp.float32), 'Ins_tk': jax.random.normal(ks[1], (B, N_I, OUT_LEN), dtype=jnp.float32), 'gate_w': w(ks[2], (IN_LEN, E)), 'expert_w': w(ks[3], (E, IN_LEN, OUT_LEN)), 'expert_b': jnp.zeros((E, OUT_LEN), dtype=jnp.float32), 'gamma_w': w(ks[4], (E, OUT_LEN)), 'beta_w': w(ks[5], (E, OUT_LEN, OUT_LEN)), 'rmod_w': w(ks[6], (OUT_LEN, E))}
    _L1_ffn_all = _L1_ffn_setup()
    _L1_ffn_in = {k: v for k, v in _L1_ffn_all.items() if k in ('Ins_tk', 'gate_w', 'expert_w', 'expert_b', 'gamma_w', 'beta_w', 'rmod_w')}
    del _L1_ffn_all

    def _L2_conv_setup():
        import jax, jax.numpy as jnp
        import numpy as np
        from jax import lax
        DIM = 128
        ORDER = 3
        DIMS = [DIM // 2 ** i for i in range(ORDER)][::-1]
        SUMD = sum(DIMS)
        SCALE = 1.0

        def conv1x1(x, w, b):
            return jnp.einsum('oc,bchw->bohw', w, x) + b[None, :, None, None]

        def dwconv7(x, w, b):
            y = lax.conv_general_dilated(x, w, window_strides=(1, 1), padding=((3, 3), (3, 3)), dimension_numbers=('NCHW', 'OIHW', 'NCHW'), feature_group_count=x.shape[1])
            return y + b[None, :, None, None]
        key = jax.random.key(seed)
        ks = jax.random.split(key, 12)
        s = 0.02
        return {'x': jax.random.normal(ks[0], (4, DIM, 32, 32), jnp.float32), 'w_in': jax.random.normal(ks[1], (2 * DIM, DIM), jnp.float32) * s, 'b_in': jnp.zeros((2 * DIM,), jnp.float32), 'dw_w': jax.random.normal(ks[2], (SUMD, 1, 7, 7), jnp.float32) * s, 'dw_b': jnp.zeros((SUMD,), jnp.float32), 'pw0_w': jax.random.normal(ks[3], (DIMS[1], DIMS[0]), jnp.float32) * s, 'pw0_b': jnp.zeros((DIMS[1],), jnp.float32), 'pw1_w': jax.random.normal(ks[4], (DIMS[2], DIMS[1]), jnp.float32) * s, 'pw1_b': jnp.zeros((DIMS[2],), jnp.float32), 'w_out': jax.random.normal(ks[5], (DIM, DIM), jnp.float32) * s, 'b_out': jnp.zeros((DIM,), jnp.float32)}
    _L2_conv_all = _L2_conv_setup()
    _L2_conv_in = {k: v for k, v in _L2_conv_all.items() if k in ('w_in', 'b_in', 'dw_w', 'dw_b', 'pw0_w', 'pw0_b', 'pw1_w', 'pw1_b', 'w_out', 'b_out')}
    del _L2_conv_all

    def _L2_ffn_setup():
        import jax, jax.numpy as jnp
        import numpy as np
        from jax import lax
        N, M, DIM, HEADS, TOPK = (4, 512, 128, 8, 16)

        def _split_heads(t, h):
            n, m, c = t.shape
            return t.reshape(n, m, h, c // h).transpose(0, 2, 1, 3).reshape(n * h, m, c // h)
        key = jax.random.key(seed)
        ks = jax.random.split(key, 7)
        f = lambda k, s, sc=1.0: jax.random.normal(k, s, dtype=jnp.float32) * sc
        return {'x': f(ks[0], (N, M, DIM)), 'pos_w': f(ks[1], (DIM, 1, 3), 0.1), 'pos_b': f(ks[2], (DIM,), 0.02), 'qkv_w': f(ks[3], (3 * DIM, DIM), 0.02), 'qkv_b': f(ks[4], (3 * DIM,), 0.02), 'wo_w': f(ks[5], (DIM, DIM), 0.02), 'wo_b': f(ks[6], (DIM,), 0.02)}
    _L2_ffn_all = _L2_ffn_setup()
    _L2_ffn_in = {k: v for k, v in _L2_ffn_all.items() if k in ('pos_w', 'pos_b', 'qkv_w', 'qkv_b', 'wo_w', 'wo_b')}
    del _L2_ffn_all

    def _L3_conv_setup():
        import jax, jax.numpy as jnp
        import numpy as np
        OPT_SCALE_4BIT = 2.513930578568423
        N_LEVELS = 16
        TRUST = OPT_SCALE_4BIT / (N_LEVELS - 1)
        LHD = 6
        HD = 1 << LHD

        def _hadamard_matrix(lhd):
            h = np.array([[1.0]], dtype=np.float32)
            for _ in range(lhd):
                h = np.block([[h, h], [h, -h]])
            return jnp.asarray(h * 2.0 ** (-lhd / 2), dtype=jnp.float32)
        key = jax.random.key(seed)
        x = jax.random.normal(key, (16, 128, 56, 56), dtype=jnp.float32)
        aux_matrix = _hadamard_matrix(LHD)
        return {'x': x, 'aux_matrix': aux_matrix}
    _L3_conv_all = _L3_conv_setup()
    _L3_conv_in = {k: v for k, v in _L3_conv_all.items() if k in ('aux_matrix',)}
    del _L3_conv_all

    def _L3_ffn_setup():
        import jax, jax.numpy as jnp
        import numpy as np
        B, T, D = (4, 256, 128)
        E, TOP_K, H = (8, 2, 64)
        key = jax.random.key(seed)
        ks = jax.random.split(key, 8)
        s = 0.02
        return {'x': jax.random.normal(ks[0], (B, T, D), dtype=jnp.float32), 'router': jax.random.normal(ks[1], (D, E), dtype=jnp.float32) * s, 'shared_gate': jax.random.normal(ks[2], (D, H), dtype=jnp.float32) * s, 'shared_up': jax.random.normal(ks[3], (D, H), dtype=jnp.float32) * s, 'shared_down': jax.random.normal(ks[4], (H, D), dtype=jnp.float32) * s, 'W_gate': jax.random.normal(ks[5], (E, D, H), dtype=jnp.float32) * s, 'W_up': jax.random.normal(ks[6], (E, D, H), dtype=jnp.float32) * s, 'W_down': jax.random.normal(ks[7], (E, H, D), dtype=jnp.float32) * s}
    _L3_ffn_all = _L3_ffn_setup()
    _L3_ffn_in = {k: v for k, v in _L3_ffn_all.items() if k in ('router', 'shared_gate', 'shared_up', 'shared_down', 'W_gate', 'W_up', 'W_down')}
    del _L3_ffn_all
    return {'x': x, 'L0_conv_bias': _L0_conv_in['bias'], 'L0_conv_up_filter': _L0_conv_in['up_filter'], 'L0_conv_down_filter': _L0_conv_in['down_filter'], 'L0_ffn_Wg': _L0_ffn_in['Wg'], 'L0_ffn_W1': _L0_ffn_in['W1'], 'L0_ffn_b1': _L0_ffn_in['b1'], 'L0_ffn_W2': _L0_ffn_in['W2'], 'L0_ffn_b2': _L0_ffn_in['b2'], 'L1_conv_qkv_w': _L1_conv_in['qkv_w'], 'L1_conv_agg_dw_w': _L1_conv_in['agg_dw_w'], 'L1_conv_agg_pw_w': _L1_conv_in['agg_pw_w'], 'L1_conv_proj_w': _L1_conv_in['proj_w'], 'L1_conv_bn_gamma': _L1_conv_in['bn_gamma'], 'L1_conv_bn_beta': _L1_conv_in['bn_beta'], 'L1_conv_bn_mean': _L1_conv_in['bn_mean'], 'L1_conv_bn_var': _L1_conv_in['bn_var'], 'L1_ffn_Ins_tk': _L1_ffn_in['Ins_tk'], 'L1_ffn_gate_w': _L1_ffn_in['gate_w'], 'L1_ffn_expert_w': _L1_ffn_in['expert_w'], 'L1_ffn_expert_b': _L1_ffn_in['expert_b'], 'L1_ffn_gamma_w': _L1_ffn_in['gamma_w'], 'L1_ffn_beta_w': _L1_ffn_in['beta_w'], 'L1_ffn_rmod_w': _L1_ffn_in['rmod_w'], 'L2_conv_w_in': _L2_conv_in['w_in'], 'L2_conv_b_in': _L2_conv_in['b_in'], 'L2_conv_dw_w': _L2_conv_in['dw_w'], 'L2_conv_dw_b': _L2_conv_in['dw_b'], 'L2_conv_pw0_w': _L2_conv_in['pw0_w'], 'L2_conv_pw0_b': _L2_conv_in['pw0_b'], 'L2_conv_pw1_w': _L2_conv_in['pw1_w'], 'L2_conv_pw1_b': _L2_conv_in['pw1_b'], 'L2_conv_w_out': _L2_conv_in['w_out'], 'L2_conv_b_out': _L2_conv_in['b_out'], 'L2_ffn_pos_w': _L2_ffn_in['pos_w'], 'L2_ffn_pos_b': _L2_ffn_in['pos_b'], 'L2_ffn_qkv_w': _L2_ffn_in['qkv_w'], 'L2_ffn_qkv_b': _L2_ffn_in['qkv_b'], 'L2_ffn_wo_w': _L2_ffn_in['wo_w'], 'L2_ffn_wo_b': _L2_ffn_in['wo_b'], 'L3_conv_aux_matrix': _L3_conv_in['aux_matrix'], 'L3_ffn_router': _L3_ffn_in['router'], 'L3_ffn_shared_gate': _L3_ffn_in['shared_gate'], 'L3_ffn_shared_up': _L3_ffn_in['shared_up'], 'L3_ffn_shared_down': _L3_ffn_in['shared_down'], 'L3_ffn_W_gate': _L3_ffn_in['W_gate'], 'L3_ffn_W_up': _L3_ffn_in['W_up'], 'L3_ffn_W_down': _L3_ffn_in['W_down']}

def reference(x, L0_conv_bias, L0_conv_up_filter, L0_conv_down_filter, L0_ffn_Wg, L0_ffn_W1, L0_ffn_b1, L0_ffn_W2, L0_ffn_b2, L1_conv_qkv_w, L1_conv_agg_dw_w, L1_conv_agg_pw_w, L1_conv_proj_w, L1_conv_bn_gamma, L1_conv_bn_beta, L1_conv_bn_mean, L1_conv_bn_var, L1_ffn_Ins_tk, L1_ffn_gate_w, L1_ffn_expert_w, L1_ffn_expert_b, L1_ffn_gamma_w, L1_ffn_beta_w, L1_ffn_rmod_w, L2_conv_w_in, L2_conv_b_in, L2_conv_dw_w, L2_conv_dw_b, L2_conv_pw0_w, L2_conv_pw0_b, L2_conv_pw1_w, L2_conv_pw1_b, L2_conv_w_out, L2_conv_b_out, L2_ffn_pos_w, L2_ffn_pos_b, L2_ffn_qkv_w, L2_ffn_qkv_b, L2_ffn_wo_w, L2_ffn_wo_b, L3_conv_aux_matrix, L3_ffn_router, L3_ffn_shared_gate, L3_ffn_shared_up, L3_ffn_shared_down, L3_ffn_W_gate, L3_ffn_W_up, L3_ffn_W_down):
    import jax
    import jax.numpy as jnp

    def _L0_conv_ref(x, bias, up_filter, down_filter):
        import jax, jax.numpy as jnp
        from jax import lax
        import numpy as np
        UP = 2
        DOWN = 2
        PADDING = (11, 10, 11, 10)
        GAIN = float(np.sqrt(2.0))
        SLOPE = 0.2
        CLAMP = 256.0
        UP_TAPS = 12
        IN_CUTOFF = 8.0
        OUT_CUTOFF = 8.0
        IN_HALF_WIDTH = 6.0
        OUT_HALF_WIDTH = 6.0
        TEMP_FS = 32.0

        def _design_lowpass(numtaps, cutoff, width, fs):
            nyq = fs / 2.0
            atten = 2.285 * (numtaps - 1) * np.pi * (width / nyq) + 7.95
            if atten > 50.0:
                beta = 0.1102 * (atten - 8.7)
            elif atten > 21.0:
                beta = 0.5842 * (atten - 21.0) ** 0.4 + 0.07886 * (atten - 21.0)
            else:
                beta = 0.0
            m = np.arange(numtaps) - (numtaps - 1) / 2.0
            c = cutoff / nyq
            h = c * np.sinc(c * m)
            h = h * np.kaiser(numtaps, beta)
            h = h / np.sum(h)
            return h.astype(np.float32)

        def _upfirdn2d_sep(x, f, up, down, pad, gain):
            N, C, H, W = x.shape
            fr = f[::-1].astype(x.dtype)
            kH = fr.reshape(1, 1, -1, 1)
            kW = fr.reshape(1, 1, 1, -1)
            px0, px1, py0, py1 = pad
            xr = x.reshape(N * C, 1, H, W)
            xr = lax.conv_general_dilated(xr, kH, window_strides=(down, 1), padding=((py0, py1 + up - 1), (0, 0)), lhs_dilation=(up, 1))
            xr = lax.conv_general_dilated(xr, kW, window_strides=(1, down), padding=((0, 0), (px0, px1 + up - 1)), lhs_dilation=(1, up))
            Ho, Wo = (xr.shape[2], xr.shape[3])
            return xr.reshape(N, C, Ho, Wo) * gain
        y = _upfirdn2d_sep(x, up_filter, UP, 1, PADDING, float(UP * UP))
        y = y + bias[None, :, None, None]
        y = jnp.where(y >= 0, y, y * SLOPE) * GAIN
        y = jnp.clip(y, -CLAMP, CLAMP)
        y = _upfirdn2d_sep(y, down_filter, 1, DOWN, (0, 0, 0, 0), 1.0)
        return y

    def _L0_ffn_ref(x, Wg, W1, b1, W2, b2):
        import jax, jax.numpy as jnp
        import numpy as np
        B, L, D, H, E, K = (8, 2048, 128, 512, 8, 2)
        SCALE = 0.02
        b, l, d = x.shape
        xt = x.reshape(-1, d)
        T = xt.shape[0]
        gate = jax.nn.softmax(xt @ Wg, axis=-1)
        topv, topi = jax.lax.top_k(gate, K)
        topv = topv / (jnp.sum(topv, axis=-1, keepdims=True) + 1e-06)
        scores = jnp.zeros((T, E), dtype=xt.dtype).at[jnp.arange(T)[:, None], topi].set(topv)
        out = jnp.zeros_like(xt)
        for e in range(E):
            h = jax.nn.gelu(xt @ W1[e] + b1[e], approximate=False)
            ye = h @ W2[e] + b2[e]
            out = out + ye * scores[:, e:e + 1]
        return out.reshape(b, l, d)

    def _L1_conv_ref(x, qkv_w, agg_dw_w, agg_pw_w, proj_w, bn_gamma, bn_beta, bn_mean, bn_var):
        import jax, jax.numpy as jnp
        import numpy as np
        DIM = 8
        EPS_ATT = 1e-15
        BN_EPS = 1e-05

        def conv2d(x, w, groups=1, padding=0):
            return jax.lax.conv_general_dilated(x, w, window_strides=(1, 1), padding=[(padding, padding), (padding, padding)], dimension_numbers=('NCHW', 'OIHW', 'NCHW'), feature_group_count=groups)
        B, _, H, W = x.shape
        qkv = conv2d(x, qkv_w)
        dw_groups = agg_dw_w.shape[0]
        pw_groups = qkv.shape[1] // agg_pw_w.shape[1]
        agg = conv2d(qkv, agg_dw_w, groups=dw_groups, padding=2)
        agg = conv2d(agg, agg_pw_w, groups=pw_groups)
        ms = jnp.concatenate([qkv, agg], axis=1)
        n_h = ms.shape[1] // (3 * DIM)
        t = ms.reshape(B, n_h, 3 * DIM, H * W).transpose(0, 1, 3, 2)
        q = jax.nn.relu(t[..., :DIM])
        k = jax.nn.relu(t[..., DIM:2 * DIM])
        v = t[..., 2 * DIM:]
        v = jnp.concatenate([v, jnp.ones(v.shape[:-1] + (1,), v.dtype)], axis=-1)
        kv = jnp.einsum('bhnd,bhne->bhde', k, v)
        out = jnp.einsum('bhnd,bhde->bhne', q, kv)
        out = out[..., :-1] / (out[..., -1:] + EPS_ATT)
        out = out.transpose(0, 1, 3, 2).reshape(B, n_h * DIM, H, W)
        out = conv2d(out, proj_w)
        inv = jax.lax.rsqrt(bn_var + BN_EPS) * bn_gamma
        out = out * inv[:, None, None] + (bn_beta - bn_mean * inv)[:, None, None]
        return out

    def _L1_ffn_ref(x, Ins_tk, gate_w, expert_w, expert_b, gamma_w, beta_w, rmod_w):
        import jax, jax.numpy as jnp
        import numpy as np
        B, C, IN_LEN, OUT_LEN, E, TOP_K, N_I = (1, 2048, 128, 128, 8, 2, 16)
        Bx, Cx, L = x.shape
        xf = x.reshape(-1, L)
        ins = Ins_tk[0]
        router_gamma = jnp.mean(ins @ rmod_w, axis=0)
        logits = xf @ gate_w + router_gamma
        probs = jax.nn.softmax(logits.astype(jnp.float32), axis=-1)
        rw, sel = jax.lax.top_k(probs, TOP_K)
        combine = jnp.sum(jax.nn.one_hot(sel, E, dtype=rw.dtype) * rw[..., None], axis=1)
        gam = jnp.mean(ins @ gamma_w.T, axis=0)
        bet = jnp.einsum('nh,ehd->ed', ins, beta_w) / N_I
        eo = jnp.einsum('nl,eld->end', xf, expert_w) + expert_b[:, None, :]
        mod = gam[:, None, None] * eo + bet[:, None, :]
        out = jnp.einsum('ne,end->nd', combine, mod)
        return out.reshape(Bx, Cx, OUT_LEN)

    def _L2_conv_ref(x, w_in, b_in, dw_w, dw_b, pw0_w, pw0_b, pw1_w, pw1_b, w_out, b_out):
        import jax, jax.numpy as jnp
        import numpy as np
        from jax import lax
        DIM = 128
        ORDER = 3
        DIMS = [DIM // 2 ** i for i in range(ORDER)][::-1]
        SUMD = sum(DIMS)
        SCALE = 1.0

        def conv1x1(x, w, b):
            return jnp.einsum('oc,bchw->bohw', w, x) + b[None, :, None, None]

        def dwconv7(x, w, b):
            y = lax.conv_general_dilated(x, w, window_strides=(1, 1), padding=((3, 3), (3, 3)), dimension_numbers=('NCHW', 'OIHW', 'NCHW'), feature_group_count=x.shape[1])
            return y + b[None, :, None, None]
        fused = conv1x1(x, w_in, b_in)
        pwa = fused[:, :DIMS[0]]
        abc = fused[:, DIMS[0]:]
        dw_abc = dwconv7(abc, dw_w, dw_b) * SCALE
        dw0 = dw_abc[:, :DIMS[0]]
        dw1 = dw_abc[:, DIMS[0]:DIMS[0] + DIMS[1]]
        dw2 = dw_abc[:, DIMS[0] + DIMS[1]:]
        h = pwa * dw0
        h = conv1x1(h, pw0_w, pw0_b) * dw1
        h = conv1x1(h, pw1_w, pw1_b) * dw2
        return conv1x1(h, w_out, b_out)

    def _L2_ffn_ref(x, pos_w, pos_b, qkv_w, qkv_b, wo_w, wo_b):
        import jax, jax.numpy as jnp
        import numpy as np
        from jax import lax
        N, M, DIM, HEADS, TOPK = (4, 512, 128, 8, 16)

        def _split_heads(t, h):
            n, m, c = t.shape
            return t.reshape(n, m, h, c // h).transpose(0, 2, 1, 3).reshape(n * h, m, c // h)
        n, m, c = x.shape
        h = HEADS
        scale = c ** (-0.5)
        pos = lax.conv_general_dilated(x.transpose(0, 2, 1), pos_w, window_strides=(1,), padding=[(1, 1)], feature_group_count=c, dimension_numbers=('NCH', 'OIH', 'NCH'))
        x = x + (pos + pos_b[None, :, None]).transpose(0, 2, 1)
        qkv = x @ qkv_w.T + qkv_b
        q, k, v = jnp.split(qkv, [c, 2 * c], axis=-1)
        q = _split_heads(q, h)
        k = _split_heads(k, h)
        v = _split_heads(v, h)
        qd = lax.stop_gradient(q)
        kd = lax.stop_gradient(k)
        logits = jnp.einsum('bmd,bpd->bmp', qd * scale, kd)
        _, idx = lax.top_k(logits, TOPK)
        gather = jax.vmap(lambda t, i: t[i])
        k_sel = gather(k, idx)
        v_sel = gather(v, idx)
        attn = jax.nn.softmax(jnp.einsum('bmd,bmkd->bmk', q * scale, k_sel), axis=-1)
        out = jnp.einsum('bmk,bmkd->bmd', attn, v_sel)
        d = c // h
        out = out.reshape(n, h, m, d).transpose(0, 2, 1, 3).reshape(n, m, c)
        return out @ wo_w.T + wo_b

    def _L3_conv_ref(x, aux_matrix):
        import jax, jax.numpy as jnp
        import numpy as np
        OPT_SCALE_4BIT = 2.513930578568423
        N_LEVELS = 16
        TRUST = OPT_SCALE_4BIT / (N_LEVELS - 1)
        LHD = 6
        HD = 1 << LHD

        def _hadamard_matrix(lhd):
            h = np.array([[1.0]], dtype=np.float32)
            for _ in range(lhd):
                h = np.block([[h, h], [h, -h]])
            return jnp.asarray(h * 2.0 ** (-lhd / 2), dtype=jnp.float32)
        B, C, H, W = x.shape
        hd = aux_matrix.shape[0]
        xm = jnp.moveaxis(x, 1, -1)
        xh = jnp.einsum('bhwgd,de->bhwge', xm.reshape(B, H, W, C // hd, hd), aux_matrix)
        x_had = jnp.moveaxis(xh.reshape(B, H, W, C), -1, 1)
        xs = jax.lax.stop_gradient(x_had)
        std = jnp.sqrt(jnp.mean(xs * xs, axis=(-1, -2, -3), keepdims=True))
        scale = OPT_SCALE_4BIT * std + 1e-08
        step = 2.0 * scale / (N_LEVELS - 1)
        x_clip = jnp.clip(xs, -scale, scale)
        temp = jnp.round(x_clip / step + 0.5)
        xq = temp * step - step * 0.5
        mask = (jnp.abs(xq - xs) <= std * TRUST).astype(x.dtype)
        grad_flow = x_had * mask
        return grad_flow + jax.lax.stop_gradient(xq - grad_flow)

    def _L3_ffn_ref(x, router, shared_gate, shared_up, shared_down, W_gate, W_up, W_down):
        import jax, jax.numpy as jnp
        import numpy as np
        B, T, D = (4, 256, 128)
        E, TOP_K, H = (8, 2, 64)
        b, t, d = x.shape
        n = b * t
        x_flat = x.reshape(n, d)
        shared_out = jax.nn.silu(x_flat @ shared_gate) * (x_flat @ shared_up) @ shared_down
        probs = jax.nn.softmax(x_flat @ router, axis=-1)
        topk_scores, topk_idx = jax.lax.top_k(probs, TOP_K)
        combine = jnp.zeros((n, E), dtype=x.dtype)
        combine = combine.at[jnp.arange(n)[:, None], topk_idx].set(topk_scores)
        gate = jax.nn.silu(jnp.einsum('nd,edh->enh', x_flat, W_gate))
        up = jnp.einsum('nd,edh->enh', x_flat, W_up)
        y = jnp.einsum('enh,ehd->end', gate * up, W_down)
        routed_out = jnp.einsum('ne,end->nd', combine, y)
        return (shared_out + routed_out).reshape(b, t, d)

    def _gn(v, G=32, eps=1e-05):
        B_, C_, H_, W_ = v.shape
        g = v.reshape(B_, G, C_ // G, H_, W_)
        m = jnp.mean(g, axis=(2, 3, 4), keepdims=True)
        s = jnp.var(g, axis=(2, 3, 4), keepdims=True)
        return ((g - m) / jnp.sqrt(s + eps)).reshape(v.shape)

    def _ln_c(v, eps=1e-06):
        m = jnp.mean(v, axis=1, keepdims=True)
        s = jnp.var(v, axis=1, keepdims=True)
        return (v - m) / jnp.sqrt(s + eps)

    def _ln_t(v, eps=1e-05):
        m = jnp.mean(v, axis=-1, keepdims=True)
        s = jnp.var(v, axis=-1, keepdims=True)
        return (v - m) / jnp.sqrt(s + eps)

    def _to_tokens(v):
        B_, C_, H_, W_ = v.shape
        return v.reshape(B_, C_, H_ * W_).transpose(0, 2, 1)

    def _from_tokens(t, like):
        B_, C_, H_, W_ = like.shape
        return t.transpose(0, 2, 1).reshape(B_, C_, H_, W_)
    x = x + _L0_conv_ref(_ln_c(x), L0_conv_bias, L0_conv_up_filter, L0_conv_down_filter)
    t = _to_tokens(x)
    t = t + _L0_ffn_ref(_ln_t(t), L0_ffn_Wg, L0_ffn_W1, L0_ffn_b1, L0_ffn_W2, L0_ffn_b2)
    x = _from_tokens(t, x)
    x = x + _L1_conv_ref(_ln_c(x), L1_conv_qkv_w, L1_conv_agg_dw_w, L1_conv_agg_pw_w, L1_conv_proj_w, L1_conv_bn_gamma, L1_conv_bn_beta, L1_conv_bn_mean, L1_conv_bn_var)
    t = _to_tokens(x)
    t = t + _L1_ffn_ref(_ln_t(t), L1_ffn_Ins_tk, L1_ffn_gate_w, L1_ffn_expert_w, L1_ffn_expert_b, L1_ffn_gamma_w, L1_ffn_beta_w, L1_ffn_rmod_w)
    x = _from_tokens(t, x)
    x = x + _L2_conv_ref(_ln_c(x), L2_conv_w_in, L2_conv_b_in, L2_conv_dw_w, L2_conv_dw_b, L2_conv_pw0_w, L2_conv_pw0_b, L2_conv_pw1_w, L2_conv_pw1_b, L2_conv_w_out, L2_conv_b_out)
    t = _to_tokens(x)
    t = t + _L2_ffn_ref(_ln_t(t), L2_ffn_pos_w, L2_ffn_pos_b, L2_ffn_qkv_w, L2_ffn_qkv_b, L2_ffn_wo_w, L2_ffn_wo_b)
    x = _from_tokens(t, x)
    x = x + _L3_conv_ref(_ln_c(x), L3_conv_aux_matrix)
    t = _to_tokens(x)
    t = t + _L3_ffn_ref(_ln_t(t), L3_ffn_router, L3_ffn_shared_gate, L3_ffn_shared_up, L3_ffn_shared_down, L3_ffn_W_gate, L3_ffn_W_up, L3_ffn_W_down)
    x = _from_tokens(t, x)
    return x

_drawn_inputs = setup_inputs


def setup_inputs(seed=0):
    import zlib

    import numpy as np

    out = dict(_drawn_inputs(seed))
    spreads = {'L1_conv_bn_gamma': (1.0, 0.2),
     'L1_conv_bn_beta': (0.0, 0.1),
     'L1_ffn_expert_b': (0.0, 0.8),
     'L2_conv_b_in': (0.0, 0.8),
     'L2_conv_dw_b': (0.0, 0.743),
     'L2_conv_pw0_b': (0.0, 0.8),
     'L2_conv_pw1_b': (0.0, 0.718),
     'L2_conv_b_out': (0.0, 0.8)}
    factors = {'L0_ffn_b1': 5.141,
     'L1_ffn_gate_w': 2.931,
     'L1_ffn_expert_w': 6.524,
     'L1_ffn_gamma_w': 7.247,
     'L1_ffn_beta_w': 2.682,
     'L1_ffn_rmod_w': 5.43,
     'L2_conv_w_in': 8.0,
     'L2_conv_dw_w': 8.0,
     'L2_conv_pw0_w': 8.0,
     'L2_conv_pw1_w': 8.0,
     'L2_conv_w_out': 5.887,
     'L2_ffn_pos_w': 29.048,
     'L2_ffn_pos_b': 53.544,
     'L2_ffn_qkv_b': 33.376,
     'L3_ffn_router': 8.0,
     'L3_ffn_shared_gate': 8.0,
     'L3_ffn_shared_up': 8.0,
     'L3_ffn_shared_down': 8.0,
     'L3_ffn_W_gate': 8.0,
     'L3_ffn_W_up': 8.0,
     'L3_ffn_W_down': 8.0,
     'L0_ffn_b2': 2.716,
     'L2_ffn_qkv_w': 8.0,
     'L2_ffn_wo_w': 8.0,
     'L2_ffn_wo_b': 64.0}
    for name, (base, spread) in spreads.items():
        noise = np.random.default_rng([zlib.crc32(name.encode()), seed]).standard_normal(out[name].shape)
        drawn = base * np.exp(spread * noise) if base else spread * noise
        out[name] = jnp.asarray(drawn.astype(out[name].dtype))
    for name, factor in factors.items():
        out[name] = (out[name] * factor).astype(out[name].dtype)
    return out
```

```python
import numpy as np
import concourse.bass as bass
from concourse import mybir
from contextlib import ExitStack

B, C, HW = 8, 128, 256
SIDE = 16
P = 128
SLOTS = 2
IMGS = 2
PASSES = B // (SLOTS * IMGS)
TILES = IMGS * HW // P
N = IMGS * HW
E = 8
HID = 512
TAPS = 12
UP = 42
ROWS_M = 3
M_UP = UP // ROWS_M
PM = ROWS_M * UP

def _up_halves(m):
    lo, hi = max(0, -(-(ROWS_M * m - 11) // 2)), min(SIDE - 1, (ROWS_M * m + 2) // 2)
    return [h for h in (0, 1) if lo <= 8 * h + 7 and hi >= 8 * h]
UP_PARTS = [(m, h) for m in range(M_UP) for h in _up_halves(m)]
DOWN_PARTS = [(h, k) for h in (0, 1) for k in range(M_UP)
              if ROWS_M * k + 2 >= 16 * h and ROWS_M * k <= 16 * h + 14 + 11]

L1_TAPS, L1_PAD, L1_W = 25, 2, 20
L2_TAPS, L2_PAD, L2_W = 49, 3, 22
L1_DVE = 14
L2_DVE = 24
HEADS, HD = 8, 16
LN_EPS = [1e-6, 1e-5] * 4
NEG = -3.0e38


def metaformer(nc, a, stop=99):
    F32 = mybir.dt.float32
    BF16 = mybir.dt.bfloat16
    ALU = mybir.AluOpType
    ACT = mybir.ActivationFunctionType
    AX = mybir.AxisListType

    ctx = ExitStack()
    with ctx:
        def sb(name, shape, dt=F32):
            return ctx.enter_context(nc.sbuf_tensor(name, shape, dt))

        def S(name):
            return ctx.enter_context(nc.semaphore(name))

        M = [ctx.enter_context(nc.psum_tensor(f"M{i}", [P, 512], F32)) for i in range(6)]
        TR = [ctx.enter_context(nc.psum_tensor(f"TR{i}", [P, 512], F32)) for i in range(2)]

        w = {}
        def load(name, shape, dt=F32):
            w[name] = sb("w_" + name, shape, dt)
            return w[name]
        wsrc = []
        def weight(name, shape, dt=F32):
            t = load(name, shape, dt)
            v = t[:] if len(shape) == 2 else t[:]
            wsrc.append((v, a[name]))
            return t
        ident = weight("ident", [P, P])
        NMASK_U = (2 * UP + UP) * TAPS
        NMASK_D = (len(DOWN_PARTS) * 8 + SIDE) * TAPS
        taps = weight("taps", [P, 2 * TAPS])
        conv_bias = weight("conv_bias", [P, C])
        Wg0 = weight("Wg0", [P, E])
        pick = weight("pick", [P, E])
        W1 = weight("W1", [P, E, HID])
        b1 = weight("b1", [P, E * 4])
        W2 = weight("W2", [P, E, 4, C])
        b2 = weight("b2", [E, C])
        Wqkv1 = weight("Wqkv1", [P, 3, P])
        dw1 = weight("dw1", [P, 3, L1_TAPS])
        pw1T = weight("pw1T", [P, 3, P])
        proj = weight("proj", [P, 2, C])
        headmask1 = weight("headmask1", [P, P])
        bn = weight("bn", [P, 4])
        ins = weight("ins", [P, 16])
        modw = weight("modw", [P, 16])
        exp_bT = weight("exp_bT", [P, E])
        Wg1 = weight("Wg1", [P, E])
        Wexp = weight("Wexp", [P, E, C])
        Win = weight("Win", [P, 256])
        bin_ = weight("bin", [P, 2])
        bpa = weight("bpa", [P, 1])
        dw2 = weight("dw2", [P, 2, L2_TAPS])
        dwb2 = weight("dwb2", [P, 2])
        pwT0 = weight("pwT0", [P, 64])
        pwb0 = weight("pwb0", [P, 1])
        pwT1 = weight("pwT1", [P, P])
        pwb1 = weight("pwb1", [P, 1])
        Wout = weight("Wout", [P, C])
        bout = weight("bout", [P, C])
        posw = weight("posw", [P, 4])
        Wqkv2 = weight("Wqkv2", [P, 3, C])
        bqk = weight("bqk", [P, 2])
        bv = weight("bv", [P, C])
        headmask2 = weight("headmask2", [P, HEADS])
        Wo = weight("Wo", [P, C])
        bo = weight("bo", [P, C])
        Whad = weight("Whad", [P, P])
        Wg3 = weight("Wg3", [P, E])
        Wgate = weight("Wgate", [P, 5, P])
        Wup = weight("Wup", [P, 5, P])
        Wdown = weight("Wdown", [P, 5, C])
        sel3 = weight("sel3", [E, 4, P])

        ones = sb("ones", [P, P])
        mhalf = sb("mhalf", [P, TILES])
        phalf = sb("phalf", [P, 2])
        upw = sb("upw", [P, len(UP_PARTS), PM])
        downw = sb("downw", [P, len(DOWN_PARTS), P])
        upA = sb("upA", [P, 2, UP])
        upB = sb("upB", [P, UP])
        dnA = sb("dnA", [P, len(DOWN_PARTS), 8])
        dnB = sb("dnB", [P, SIDE])
        w5 = sb("w5", [P, 3, L1_TAPS - L1_DVE, P])
        w7 = sb("w7", [P, 2, L2_TAPS - L2_DVE, P])
        bncol = sb("bncol", [P, 4])
        bndiag = sb("bndiag", [P, 2, P])
        bnrow = sb("bnrow", [P, 2, C])
        inssum = sb("inssum", [P, 1])
        modr = sb("modr", [16, 16])
        sixteenth = sb("sixteenth", [16, P])
        modb = sb("modb", [P, 16])
        btd = sb("btd", [P, E])
        bt = sb("bt", [E, C])

        X = [sb(f"X{s}", [P, TILES, C]) for s in range(SLOTS)]
        XT = [sb(f"XT{s}", [P, TILES, C]) for s in range(SLOTS)]
        XN = [sb(f"XN{s}", [P, N]) for s in range(SLOTS)]
        XC = [XN[s][:].rearrange("p (b n) -> p b n", b=IMGS) for s in range(SLOTS)]
        lnst = [sb(f"lnst{s}", [P, TILES, 6]) for s in range(SLOTS)]
        lnmv = [sb(f"lnmv{s}", [P, TILES, 2]) for s in range(SLOTS)]
        lnve = [sb(f"lnve{s}", [P, TILES]) for s in range(SLOTS)]
        lnrs = [sb(f"lnrs{s}", [P, TILES]) for s in range(SLOTS)]
        rt = [sb(f"rt{s}", [P, 8, TILES, E]) for s in range(SLOTS)]
        rs1 = [sb(f"rs1{s}", [P, 8, TILES]) for s in range(SLOTS)]
        comb = [sb(f"comb{s}", [P, TILES, E]) for s in range(SLOTS)]
        combT = [sb(f"combT{s}", [E, N]) for s in range(SLOTS)]

        ARENA = 60 * 256
        arena = sb("arena", [P, ARENA])
        at_ = [0]
        def piece(n, shape_str=None, **kw):
            o = at_[0]
            at_[0] += n
            assert at_[0] <= ARENA, at_[0]
            v = arena[:, o:o + n]
            return v.rearrange(shape_str, **kw) if shape_str else v
        Y = [piece(M_UP * 256, "p (m n) -> p m n", m=M_UP) for s in range(SLOTS)]
        Z = [piece(512) for _ in range(3)]
        Zb = [piece(512) for _ in range(3)]
        masks = arena[:, 0:NMASK_U + NMASK_D]
        mprod = arena[:, 4096:4096 + NMASK_D]
        assert NMASK_U + NMASK_D <= 4096
        beta_w = arena[:, 8192:8192 + E * C].rearrange("p (e c) -> p e c", e=E)
        wsrc.append((beta_w, a["beta_w"]))
        at_[0] = 0
        H = [[piece(512) for _ in range(4)] for _ in range(2)]
        at_[0] = 0
        P5 = [[piece(IMGS * L1_W * L1_W, "p (b y x) -> p b y x", b=IMGS, y=L1_W) for _ in range(3)]
              for _ in range(SLOTS)]
        A5 = [piece(512, "p (b y x) -> p b y x", b=IMGS, y=SIDE) for _ in range(2)]
        Q1 = [piece(512) for _ in range(SLOTS)]
        Q2 = [piece(512) for _ in range(SLOTS)]
        KVC = [[piece(512) for _ in range(2)] for _ in range(SLOTS)]
        KV = [[piece(TILES * 260, "p (t c) -> p t c", t=TILES) for _ in range(2)] for _ in range(SLOTS)]
        KM = [piece(2 * IMGS * 144, "p (g j c) -> p g j c", g=2, j=IMGS) for _ in range(SLOTS)]
        end_c = at_[0]
        OTk = [[P5[s][g].rearrange("p b y x -> p (b y x)")[:, 0:512] for g in range(2)] for s in range(SLOTS)]
        OC = [[KVC[s][g] for g in range(2)] for s in range(SLOTS)]
        DEN = [sb(f"DEN{s}", [P, 4, 16 * 2]) for s in range(SLOTS)]
        at_[0] = 0
        P7 = [[piece(IMGS * L2_W * L2_W, "p (b y x) -> p b y x", b=IMGS, y=L2_W) for _ in range(2)]
              for _ in range(SLOTS)]
        A7 = [piece(512, "p (b y x) -> p b y x", b=IMGS, y=SIDE) for _ in range(2)]
        PA = [piece(512) for _ in range(SLOTS)]
        D7 = [[piece(512) for _ in range(2)] for _ in range(SLOTS)]
        G0 = [piece(512) for _ in range(SLOTS)]
        G1 = [piece(512) for _ in range(SLOTS)]
        G2 = [piece(512) for _ in range(SLOTS)]
        at_[0] = 0
        XP = piece(512)
        Qc = [piece(512) for _ in range(SLOTS)]
        Kc = [piece(512) for _ in range(SLOTS)]
        Vh = [piece(TILES * HEADS * 32, "p (t h c) -> p t h c", t=TILES, h=HEADS) for _ in range(SLOTS)]
        QM = [piece(512) for _ in range(3)]
        LG = [piece(512) for _ in range(3)]
        REP = [piece(512) for _ in range(2)]
        E1 = [piece(512) for _ in range(2)]
        E2 = [piece(512) for _ in range(2)]
        PR = [piece(512) for _ in range(2)]
        PT = [piece(512) for _ in range(5)]
        PO = [piece(512) for _ in range(2)]
        OT = [XT[s][:].rearrange("p t (h d) -> p t h d", h=HEADS) for s in range(SLOTS)]
        OCf = [XN[s][:] for s in range(SLOTS)]
        UNITS = SLOTS * HEADS * IMGS
        top8 = [sb(f"top8_{i}", [P, 2, 16]) for i in range(4)]
        nmx = [sb(f"nmx{i}", [P, 2]) for i in range(4)]
        rdn = sb("rdn", [P, 2, TILES, 4])
        at_[0] = 0
        HS = [piece(512) for _ in range(SLOTS)]
        HQ = [piece(512) for _ in range(SLOTS)]
        H1 = [piece(512) for _ in range(SLOTS)]
        H2 = [piece(512) for _ in range(SLOTS)]
        H3 = [piece(512) for _ in range(SLOTS)]
        hst = [sb(f"hst{s}", [P, 9, IMGS]) for s in range(SLOTS)]
        at_[0] = 0
        SG = [piece(512) for _ in range(2)]
        GU = [[piece(512) for _ in range(5)] for _ in range(SLOTS)]

        weights_in = S("weights_in")
        masks_in = S("masks_in")
        consts = S("consts")
        dve_setup = S("dve_setup")
        pe_setup = S("pe_setup")
        act_setup = S("act_setup")
        pool_setup = S("pool_setup")
        setup_done = S("setup_done")
        dve_step = S("dve_step")
        act_step = S("act_step")
        pool_step = S("pool_step")
        pass_end = S("pass_end")
        pass_go = {n: S("go_" + n) for n in ("pe", "act", "dve", "pool")}
        borders5 = S("borders5")
        borders7 = S("borders7")
        v_ones = S("v_ones")
        lg_copied = S("lg_copied")
        x_loaded = [S(f"x_loaded{s}") for s in range(SLOTS)]
        x_turned = S("x_turned")
        x_in = S("x_in")
        ln_var = S("ln_var")
        ln_rstd = S("ln_rstd")
        xt_ready = S("xt_ready")
        xt_turned = S("xt_turned")
        xn_ready = S("xn_ready")
        up_done = S("up_done")
        up_biased = S("up_biased")
        up_leaky = S("up_leaky")
        up_gained = S("up_gained")
        up_clipped = S("up_clipped")
        down_done = S("down_done")
        x_after_conv = S("x_after_conv")
        logits_done = S("logits_done")
        router_shifted = S("router_shifted")
        router_exp = S("router_exp")
        comb_ready = S("comb_ready")
        comb_turned = S("comb_turned")
        combT_ready = S("combT_ready")
        ffn_up_done = S("ffn_up_done")
        ffn_gelu_done = S("ffn_gelu_done")
        ffn_down_done = S("ffn_down_done")
        ffn_added = S("ffn_added")
        qkv_done = S("qkv_done")
        qkv_padded = S("qkv_padded")
        kvpx_done = S("kvpx_done")
        kvpx_k = S("kvpx_k")
        kvpx_v = S("kvpx_v")
        dw5_acc = S("dw5_acc")
        dw5_done = S("dw5_done")
        dw5_out = S("dw5_out")
        agg_turned = S("agg_turned")
        agg_px = S("agg_px")
        kv_done = S("kv_done")
        kv_masked = S("kv_masked")
        num_done = S("num_done")
        num_scaled = S("num_scaled")
        o_turned = S("o_turned")
        o_ready = S("o_ready")
        proj_done = S("proj_done")
        x_shifted = S("x_shifted")
        x_added = S("x_added")
        eo_done = S("eo_done")
        eo_added = S("eo_added")
        eb_done = S("eb_done")
        fused_done = S("fused_done")
        fused_padded = S("fused_padded")
        dw7_acc = S("dw7_acc")
        dw7_done = S("dw7_done")
        dw7_out = S("dw7_out")
        g0_ready = S("g0_ready")
        pw0_done = S("pw0_done")
        g1_ready = S("g1_ready")
        pw1_done = S("pw1_done")
        g2_ready = S("g2_ready")
        out2_done = S("out2_done")
        x_after_l2 = S("x_after_l2")
        xp_ready = S("xp_ready")
        qk_done = S("qk_done")
        qk_ready = S("qk_ready")
        v_ready = S("v_ready")
        qm_ready = S("qm_ready")
        lg_done = S("lg_done")
        lg_max = S("lg_max")
        lg_exp = S("lg_exp")
        rep_ready = S("rep_ready")
        rep_exp = S("rep_exp")
        pr_ready = S("pr_ready")
        pt_done = S("pt_done")
        pt_ready = S("pt_ready")
        pv_done = S("pv_done")
        po_ready = S("po_ready")
        po_turned = S("po_turned")
        ot_ready = S("ot_ready")
        ot_turned = S("ot_turned")
        oc_ready = S("oc_ready")
        wo_done = S("wo_done")
        x_after_attn = S("x_after_attn")
        had_done = S("had_done")
        had_copied = S("had_copied")
        had_sq = S("had_sq")
        ss_done = S("ss_done")
        ms_ready = S("ms_ready")
        std_ready = S("std_ready")
        x_after_had = S("x_after_had")
        gate_done = S("gate_done")
        upp_done = S("upp_done")
        silu_done = S("silu_done")
        gu_ready = S("gu_ready")
        cb_done = S("cb_done")
        gus_ready = S("gus_ready")
        moe_done = S("moe_done")
        x_final = S("x_final")
        xf_turned = S("xf_turned")
        xf_ready = S("xf_ready")
        stored = S("stored")

        NW = len(wsrc)
        pass_sems = range(borders5.num, stored.num + 1)

        def next_pass(eng, name):
            eng.drain().then_inc(pass_end, 1)
            eng.wait_ge(pass_go[name], 1)
            eng.sem_clear(pass_go[name])
        block = ctx.enter_context(nc.Block())

        def ln_index(n, s):
            return 2 * n + s + 1

        @block.sync
        def _(sp):
            sp.dma_start(masks, a["masks"]).then_inc(masks_in, 16)
            for dst, src in wsrc:
                sp.dma_start(dst, src).then_inc(weights_in, 16)
            with sp.Fori(0, PASSES) as p:
                for s in range(SLOTS):
                    src = a["x"][:, bass.ds((p * SLOTS + s) * IMGS, IMGS), :]
                    sp.dma_start(XC[s], src).then_inc(x_loaded[s], 16)
                for s in range(SLOTS):
                    sp.wait_ge(xf_ready, s + 1)
                    dst = a["out"][:, bass.ds((p * SLOTS + s) * IMGS, IMGS), :]
                    sp.dma_start(dst, XC[s]).then_inc(stored, 16)
                sp.wait_ge(stored, 32)
                sp.wait_ge(pass_end, 4)
                sp.sem_clear(pass_sems)
                sp.sem_clear(pass_end)
                for g in pass_go.values():
                    sp.sem_inc(g, 1)

        @block.gpsimd
        def _(pool):
            def link(ins):
                steps[0] += 1
                ins.then_inc(pool_step, 1)
                pool.wait_ge(pool_step, steps[0])
            steps = [0]
            g = nc.gpsimd
            g.memset(ones[:], 1.0).then_inc(consts, 1)
            g.memset(mhalf[:], -0.5).then_inc(consts, 1)
            g.memset(phalf[:], 0.5).then_inc(consts, 1)
            g.memset(sixteenth[:], 1.0 / 16).then_inc(consts, 1)
            pool.wait_ge(weights_in, 16 * NW)
            link(g.tensor_scalar(bncol[:, 0:1], bn[:, 3:4], 1e-5, None, ALU.add))
            pool.wait_ge(consts, 4)
            link(g.tensor_tensor(bncol[:, 1:2], bncol[:, 0:1], mhalf[:, 0:1], ALU.pow))
            g.tensor_tensor(bncol[:, 2:3], bncol[:, 1:2], bn[:, 0:1], ALU.mult).then_inc(pool_setup, 1)
            for i in range(3):
                for t in range(L1_TAPS - L1_DVE):
                    g.tensor_scalar(w5[:, i, t, :], pw1T[:, i, :], dw1[:, i, L1_DVE + t:L1_DVE + t + 1],
                                    None, ALU.mult)
            for i in range(2):
                for t in range(L2_TAPS - L2_DVE):
                    last = g.tensor_scalar(w7[:, i, t, :], ident[:], dw2[:, i, L2_DVE + t:L2_DVE + t + 1],
                                           None, ALU.mult)
            last.then_inc(pool_setup, 1)
            pool.wait_ge(dve_setup, 2)

            def ln_pow(p, n, slots=range(SLOTS)):
                for s in slots:
                    pool.wait_ge(ln_var, ln_index(n, s))
                    g.tensor_tensor(lnrs[s][:], lnve[s][:], mhalf[:], ALU.pow).then_inc(ln_rstd, 1)

            def new_steps():
                if steps[0]:
                    pool.wait_ge(pool_step, steps[0])
                pool.sem_clear(pool_step)
                steps[0] = 0

            new_steps()
            with pool.Fori(0, PASSES) as p:
                ln_pow(p, 0)
                for s in range(SLOTS):
                    for m in range(7):
                        k = 7 * s + m + 1
                        pool.wait_ge(up_gained, k)
                        g.tensor_scalar(Y[s][0:PM, 2 * m:2 * m + 2, :],
                                        Zb[(7 * s + m) % 3][0:PM, :].rearrange("p (m n) -> p m n", m=2),
                                        256.0, -256.0, ALU.min, ALU.max).then_inc(up_clipped, 1)
                if stop >= 1:
                    ln_pow(p, 1)
                if stop >= 2:
                    ln_pow(p, 2, [0])
                    pool.wait_ge(ffn_added, 17)
                    for s in range(SLOTS):
                        for i in range(3):
                            g.memset(P5[s][i][:], 0.0)
                        for gg in range(2):
                            last = g.memset(KV[s][gg][:, :, 256:257], 1.0)
                    last.then_inc(borders5, 1)
                    ln_pow(p, 2, [1])
                    for s in range(SLOTS):
                        pool.wait_ge(xt_ready, ln_index(2, s))
                        for t in range(TILES):
                            last = g.tensor_tensor(X[s][:, t, :], X[s][:, t, :], bnrow[:, 1, :], ALU.add)
                        last.then_inc(x_shifted, 1)
                if stop >= 3:
                    ln_pow(p, 3)
                if stop >= 4:
                    ln_pow(p, 4)
                    pool.wait_ge(x_added, 2)
                    for s in range(SLOTS):
                        for i in range(2):
                            last = g.memset(P7[s][i][:], 0.0)
                    last.then_inc(borders7, 1)
                if stop >= 5:
                    ln_pow(p, 5)
                    for s in range(SLOTS):
                        pool.wait_ge(xt_ready, ln_index(5, s))
                        for t in range(TILES):
                            last = g.tensor_tensor(X[s][:, t, :], X[s][:, t, :], bo[:], ALU.add)
                        last.then_inc(x_shifted, 1)
                    pool.wait_ge(x_after_l2, 2)
                    for s in range(SLOTS):
                        link(g.memset(Vh[s], 0.0))
                        last = g.memset(Vh[s][:, :, :, HD:HD + 1], 1.0)
                    last.then_inc(v_ones, 1)

                    def mask_queries(hh):
                        s, h = divmod(hh, HEADS)
                        if h == 0:
                            pool.wait_ge(qk_ready, 2 * s + 1)
                        if hh >= 3:
                            pool.wait_ge(lg_done, 2 * (hh - 3) + 2)
                        g.tensor_scalar(QM[hh % 3], Qc[s], headmask2[:, h:h + 1], float(C) ** -0.5,
                                        ALU.mult, ALU.mult).then_inc(qm_ready, 1)
                    mask_queries(0)
                    mask_queries(1)
                    for c in range(UNITS):
                        if c % 2 == 0 and c // 2 + 2 < SLOTS * HEADS:
                            mask_queries(c // 2 + 2)
                        pool.wait_ge(rep_exp, c + 1)
                        if c >= 2:
                            pool.wait_ge(pt_done, c - 1)
                        g.tensor_tensor(PR[c % 2], E1[c % 2], E2[c % 2], ALU.subtract).then_inc(pr_ready, 1)
                        if c == 27 and stop >= 6:
                            ln_pow(p, 6, [0])
                    if stop >= 6:
                        ln_pow(p, 6, [1])
                if stop >= 6:
                    for s in range(SLOTS):
                        pool.wait_ge(ms_ready, s + 1)
                        g.tensor_tensor(hst[s][:, 2, :], hst[s][:, 1, :], phalf[:], ALU.pow)\
                         .then_inc(std_ready, 1)
                        if stop >= 7:
                            ln_pow(p, 7, [s])
                new_steps()
                next_pass(pool, "pool")

        @block.scalar
        def _(act):
            A = nc.scalar.activation
            pool_base = 0
            act.wait_ge(pe_setup, 1)
            A(modr[:], TR[0][0:16, 0:16], ACT.Copy).then_inc(act_setup, 1)
            act.wait_ge(pe_setup, 3)
            A(modb[:], TR[1][:, 0:16], ACT.Copy).then_inc(act_setup, 1)
            act.wait_ge(pe_setup, 5)
            A(bnrow[:].rearrange("p g c -> p (g c)"), M[0][:, 0:256], ACT.Copy).then_inc(act_setup, 1)
            act.wait_ge(pe_setup, 4)
            A(bt[:], M[1][0:E, 0:C], ACT.Copy).then_inc(act_setup, 1)

            def ln_copy(p, n, s):
                act.wait_ge(xt_turned, ln_index(n, s) - 2)
                A(XN[s][:], TR[s][:], ACT.Copy).then_inc(xn_ready, 1)

            def router_act(p, r, s):
                act.wait_ge(router_shifted, 2 * r + s + 1)
                A(rt[s][:, 1], rt[s][:, 0], ACT.Exp).then_inc(router_exp, 1)

            def comb_copy(p, r, s):
                act.wait_ge(comb_turned, 2 * r + s + 1)
                A(combT[s][:], TR[s][0:E, :], ACT.Copy).then_inc(combT_ready, 1)

            with act.Fori(0, PASSES) as p:
                for s in range(SLOTS):
                    act.wait_ge(x_turned, s + 1)
                    A(X[s][:].rearrange("p t c -> p (t c)"), TR[s][:], ACT.Copy).then_inc(x_in, 1)
                for s in range(SLOTS):
                    for m in range(7):
                        c = 7 * s + m
                        act.wait_ge(up_leaky, c + 1)
                        if c >= 3:
                            act.wait_ge(up_clipped, c - 2)
                        A(Zb[c % 3][0:PM, :], Z[c % 3][0:PM, :], ACT.Copy, scale=float(np.sqrt(2.0)))\
                            .then_inc(up_gained, 1)
                if stop >= 1:
                    for s in range(SLOTS):
                        ln_copy(p, 1, s)
                        router_act(p, 0, s)
                    for s in range(SLOTS):
                        for i in range(32):
                            c = 32 * s + i
                            e = c // 4
                            act.wait_ge(ffn_up_done, c + 1)
                            if e >= 2:
                                act.wait_ge(ffn_down_done, (e - 2) + 1 + (1 if e - 2 >= 8 else 0))
                            A(H[e % 2][i % 4], M[c % 3][:], ACT.Gelu, bias=b1[:, i:i + 1])\
                                .then_inc(ffn_gelu_done, 1)
                        comb_copy(p, 0, s)
                if stop >= 2:
                    act.wait_ge(borders5, 1)
                    for s in range(SLOTS):
                        ln_copy(p, 2, s)
                    for s in range(SLOTS):
                        for i in range(3):
                            k = 3 * s + i + 1
                            act.wait_ge(qkv_done, k)
                            if i == 0:
                                A(Q1[s], M[0][:], ACT.Relu)
                            A(P5[s][i][:, :, L1_PAD:L1_PAD + SIDE, L1_PAD:L1_PAD + SIDE],
                              M[i][:].rearrange("p (b y x) -> p b y x", b=IMGS, y=SIDE),
                              ACT.Copy).then_inc(qkv_padded, 1)
                        for h in range(2):
                            act.wait_ge(kvpx_done, 2 * s + h + 1)
                            src = M[3 + h][:].rearrange("p (t c) -> p t c", t=2)
                            A(KV[s][0][:, 2 * h:2 * h + 2, 0:128], src[:, :, 0:128], ACT.Relu)\
                                .then_inc(kvpx_k, 1)
                            A(KV[s][0][:, 2 * h:2 * h + 2, 128:256], src[:, :, 128:256], ACT.Copy)\
                                .then_inc(kvpx_v, 1)
                    for s in range(SLOTS):
                        for i in range(3):
                            k = 3 * s + i + 1
                            act.wait_ge(dw5_done, k)
                            dst = [Q2[s], KVC[s][0], KVC[s][1]][i]
                            A(dst, M[[5, 0, 1][i]][:], ACT.Copy if i == 2 else ACT.Relu).then_inc(dw5_out, 1)
                    for s in range(SLOTS):
                        for g in range(2):
                            act.wait_ge(agg_turned, 2 * s + g + 1)
                            A(KV[s][1][:, :, 128 * g:128 * g + 128],
                              M[2 + g][:].rearrange("p (t c) -> p t c", t=TILES), ACT.Copy)\
                                .then_inc(agg_px, 1)
                    for s in range(SLOTS):
                        for g in range(2):
                            act.wait_ge(o_turned, 2 * s + g + 1)
                            A(OC[s][g], M[4 + g][:], ACT.Copy).then_inc(o_ready, 1)
                if stop >= 3:
                    for s in range(SLOTS):
                        ln_copy(p, 3, s)
                        router_act(p, 1, s)
                    for s in range(SLOTS):
                        comb_copy(p, 1, s)
                if stop >= 4:
                    act.wait_ge(borders7, 1)
                    for s in range(SLOTS):
                        ln_copy(p, 4, s)
                    for s in range(SLOTS):
                        for i in range(2):
                            act.wait_ge(fused_done, 3 * s + i + 1)
                            n = P if i == 0 else 96
                            A(P7[s][i][0:n, :, L2_PAD:L2_PAD + SIDE, L2_PAD:L2_PAD + SIDE],
                              M[4 + i][0:n, :].rearrange("p (b y x) -> p b y x", b=IMGS, y=SIDE),
                              ACT.Identity, bias=bin_[0:n, i:i + 1]).then_inc(fused_padded, 1)
                        act.wait_ge(fused_done, 3 * s + 3)
                        A(PA[s][64:96, :], M[3][64:96, :], ACT.Identity, bias=bpa[64:96, :])\
                            .then_inc(fused_padded, 1)
                    for s in range(SLOTS):
                        for i in range(2):
                            act.wait_ge(dw7_done, 2 * s + i + 1)
                            n = P if i == 1 else 96
                            A(D7[s][i][0:n, :], M[i][0:n, :], ACT.Identity, bias=dwb2[0:n, 1 - i:2 - i])\
                                .then_inc(dw7_out, 1)
                if stop >= 5:
                    for s in range(SLOTS):
                        ln_copy(p, 5, s)

                    def project_copy(s, i):
                        act.wait_ge(qk_done, 3 * s + i + 1)
                        A([Qc, Kc][i][s], M[2][:], ACT.Identity, bias=bqk[:, i:i + 1]).then_inc(qk_ready, 1)

                    def lg_copy(c):
                        act.wait_ge(lg_done, c + 1)
                        if c >= 3:
                            act.wait_ge(rep_ready, c - 2)
                        A(LG[c % 3], M[c % 2][:], ACT.Copy).then_inc(lg_copied, 1)

                    def pt_copy(c):
                        act.wait_ge(pt_done, c + 1)
                        if c >= 5:
                            act.wait_ge(pv_done, (c - 5) // 4 + 1)
                        A(PT[c % 5], M[3 + c % 2][:], ACT.Copy).then_inc(pt_ready, 1)

                    def po_copy(s, g):
                        act.wait_ge(pv_done, 4 * s + 2 * g + 2)
                        if s == 1:
                            act.wait_ge(po_turned, g + 1)
                        A(PO[g], [M[5], TR[s]][g][:], ACT.Copy).then_inc(po_ready, 1)

                    def oc_copy(s):
                        act.wait_ge(ot_turned, s + 1)
                        A(OCf[s], M[2][:], ACT.Copy).then_inc(oc_ready, 1)
                    project_copy(0, 0)
                    project_copy(0, 1)
                    lg_copy(0)
                    for c in range(UNITS):
                        if c + 1 < UNITS:
                            lg_copy(c + 1)
                        act.wait_ge(lg_max, c + 1)
                        if c >= 2:
                            act.wait_ge(pr_ready, c - 1)
                        for q in range(2):
                            A(E1[c % 2][:, q * 256:q * 256 + 256], LG[c % 3][:, q * 256:q * 256 + 256],
                              ACT.Exp, bias=nmx[c % 4][:, q:q + 1])
                        act.wait_ge(rep_ready, c + 1)
                        for q in range(2):
                            last = A(E2[c % 2][:, q * 256:q * 256 + 256], REP[c % 2][:, q * 256:q * 256 + 256],
                                     ACT.Exp, bias=nmx[c % 4][:, q:q + 1])
                        last.then_inc(rep_exp, 1)
                        if c >= 1:
                            pt_copy(c - 1)
                        if c in (8, 9):
                            project_copy(1, c - 8)
                        if c == 9:
                            po_copy(0, 0)
                        if c == 17:
                            po_copy(0, 1)
                        if c == 23:
                            oc_copy(0)
                        if c == 25:
                            po_copy(1, 0)
                    pt_copy(UNITS - 1)
                    po_copy(1, 1)
                    oc_copy(1)
                if stop >= 6:
                    for s in range(SLOTS):
                        ln_copy(p, 6, s)
                    for s in range(SLOTS):
                        act.wait_ge(had_done, s + 1)
                        A(HS[s], M[2 + s][:], ACT.Copy).then_inc(had_copied, 1)
                        for j in range(IMGS):
                            last = A(HQ[s][:, 256 * j:256 * j + 256], M[2 + s][:, 256 * j:256 * j + 256],
                                     ACT.Square, accum_out=hst[s][:, 0, j:j + 1])
                        last.then_inc(had_sq, 1)
                if stop >= 7:
                    for s in range(SLOTS):
                        ln_copy(p, 7, s)
                        router_act(p, 2, s)
                    for s in range(SLOTS):
                        for i in range(5):
                            c = 5 * s + i
                            n = P if i < 4 else 64
                            act.wait_ge(gate_done, c + 1)
                            if c >= 2:
                                act.wait_ge(gu_ready, c - 1)
                            A(SG[c % 2][0:n, :], M[c % 2][0:n, :], ACT.Silu).then_inc(silu_done, 1)
                        comb_copy(p, 2, s)
                for s in range(SLOTS):
                    act.wait_ge(xf_turned, s + 1)
                    A(XC[s].rearrange("p b n -> p (b n)"), TR[s][:], ACT.Copy).then_inc(xf_ready, 1)
                next_pass(act, "act")

        @block.vector
        def _(dve):
            v = nc.vector
            steps = [0]

            def link(ins):
                steps[0] += 1
                ins.then_inc(dve_step, 1)
                dve.wait_ge(dve_step, steps[0])

            def mark(ins):
                steps[0] += 1
                ins.then_inc(dve_step, 1)
                return steps[0]

            def after(k):
                dve.wait_ge(dve_step, k)

            dve.wait_ge(masks_in, 16)
            dve.wait_ge(weights_in, 16 * NW)
            for lo, dst, n, f in ((0, upA[:].rearrange("p h y -> p (h y)"), 2 * UP, 0),
                                  (2 * UP, upB[:], UP, 0),
                                  (3 * UP, dnA[:].rearrange("p k j -> p (k j)"), 8 * len(DOWN_PARTS), 1),
                                  (3 * UP + 8 * len(DOWN_PARTS), dnB[:], SIDE, 1)):
                src = masks[:, lo * TAPS:(lo + n) * TAPS].rearrange("p (n t) -> p n t", t=TAPS)
                tp = taps[:, f * TAPS:(f + 1) * TAPS].unsqueeze(1).to_broadcast([P, n, TAPS])
                prod = mprod[:, 0:n * TAPS].rearrange("p (n t) -> p n t", t=TAPS)
                link(v.tensor_tensor(prod, src, tp, ALU.mult))
                link(v.tensor_reduce(dst, prod, AX.X, ALU.add))
            link(v.tensor_scalar(upB[:], upB[:], 4.0, None, ALU.mult))
            for i, (m, h) in enumerate(UP_PARTS):
                v.tensor_tensor(upw[:, i, :].rearrange("p (r x) -> p r x", r=ROWS_M),
                                upA[:, h, ROWS_M * m:ROWS_M * m + ROWS_M].unsqueeze(2).to_broadcast([P, ROWS_M, UP]),
                                upB[:].unsqueeze(1).to_broadcast([P, ROWS_M, UP]), ALU.mult)
            for i in range(len(DOWN_PARTS)):
                last = v.tensor_tensor(downw[:, i, :].rearrange("p (j x) -> p j x", j=8),
                                       dnA[:, i, :].unsqueeze(2).to_broadcast([P, 8, SIDE]),
                                       dnB[:].unsqueeze(1).to_broadcast([P, 8, SIDE]), ALU.mult)
            last.then_inc(dve_setup, 2)
            link(v.tensor_reduce(inssum[:], ins[:], AX.X, ALU.add))
            dve.wait_ge(pool_setup, 1)
            link(v.tensor_tensor(bncol[:, 3:4], bn[:, 2:3], bncol[:, 2:3], ALU.mult))
            link(v.tensor_tensor(bncol[:, 0:1], bn[:, 1:2], bncol[:, 3:4], ALU.subtract))
            v.tensor_scalar(bndiag[:, 0, :], ident[:], bncol[:, 2:3], None, ALU.mult)
            v.tensor_scalar(bndiag[:, 1, :], ident[:], bncol[:, 0:1], None, ALU.mult).then_inc(dve_setup, 1)
            dve.wait_ge(pe_setup, 3)
            dve.wait_ge(act_setup, 2)
            link(v.tensor_scalar(btd[:], M[2][:, 0:E], 1.0 / 16, None, ALU.mult))
            link(v.tensor_tensor(exp_bT[:], exp_bT[:], modb[:, 8:16], ALU.mult))
            v.tensor_tensor(btd[:], btd[:], exp_bT[:], ALU.add).then_inc(dve_setup, 1)

            def ln_stats(n, s):
                for t in range(TILES):
                    k = mark(v.bn_stats(lnst[s][:, t, :], X[s][:, t, :]))
                for t in range(TILES):
                    after(k - TILES + 1 + t)
                    k2 = mark(v.bn_aggr(lnmv[s][:, t, :], lnst[s][:, t, :]))
                after(k2)
                v.tensor_scalar(lnve[s][:], lnmv[s][:, :, 1], LN_EPS[n], None, ALU.add).then_inc(ln_var, 1)

            def ln_apply(n, s):
                dve.wait_ge(ln_rstd, ln_index(n, s))
                for t in range(TILES):
                    last = v.tensor_scalar(XT[s][:, t, :], X[s][:, t, :], lnmv[s][:, t, 0:1], lnrs[s][:, t:t + 1],
                                           ALU.subtract, ALU.mult)
                last.then_inc(xt_ready, 1)

            def layernorm(p, n, s):
                ln_stats(n, s)
                ln_apply(n, s)

            def router(p, r, s, gamma=None, renorm=False):
                R = [rt[s][:, i] for i in range(8)]
                q = [rs1[s][:, i] for i in range(8)]
                wide = lambda t: t.unsqueeze(2).to_broadcast([P, TILES, E])
                pk = pick[:].unsqueeze(1).to_broadcast([P, TILES, E])
                dve.wait_ge(logits_done, 2 * r + s + 1)
                lg = TR[s][:, 0:TILES * E].rearrange("p (t e) -> p t e", t=TILES)
                if gamma is None:
                    link(v.tensor_copy(R[2], lg))
                else:
                    link(v.tensor_tensor(R[2], lg, gamma.unsqueeze(1).to_broadcast([P, TILES, E]), ALU.add))
                link(v.tensor_reduce(q[0], R[2], AX.X, ALU.max))
                v.tensor_tensor(R[0], R[2], wide(q[0]), ALU.subtract).then_inc(router_shifted, 1)
                dve.wait_ge(router_exp, 2 * r + s + 1)
                link(v.tensor_reduce(q[1], R[1], AX.X, ALU.add))
                link(v.reciprocal(q[2], q[1]))
                link(v.tensor_tensor(R[3], R[1], wide(q[2]), ALU.mult))
                src = R[3]
                for i in range(2):
                    link(v.tensor_reduce(q[3 + i], src, AX.X, ALU.max))
                    link(v.tensor_tensor(R[4], src, wide(q[3 + i]), ALU.is_equal))
                    link(v.tensor_tensor(R[4], R[4], pk, ALU.mult))
                    link(v.tensor_reduce(q[5], R[4], AX.X, ALU.max))
                    link(v.tensor_tensor(R[5 + i], R[4], wide(q[5]), ALU.is_equal))
                    if i == 0:
                        link(v.scalar_tensor_tensor(R[7], R[5], -2.0, R[3], ALU.mult, ALU.add))
                        src = R[7]
                link(v.tensor_tensor(R[5], R[5], R[6], ALU.add))
                if renorm:
                    link(v.tensor_tensor(q[6], q[3], q[4], ALU.add))
                    link(v.tensor_scalar(q[6], q[6], 1e-6, None, ALU.add))
                    link(v.reciprocal(q[7], q[6]))
                    link(v.tensor_tensor(R[3], R[3], wide(q[7]), ALU.mult))
                v.tensor_tensor(comb[s][:], R[3], R[5], ALU.mult).then_inc(comb_ready, 1)

            def new_steps():
                if steps[0]:
                    after(steps[0])
                dve.sem_clear(dve_step)
                steps[0] = 0

            new_steps()
            with dve.Fori(0, PASSES) as p:
                for s in range(SLOTS):
                    dve.wait_ge(x_in, s + 1)
                    layernorm(p, 0, s)
                for s in range(SLOTS):
                    for m in range(7):
                        c = 7 * s + m
                        dve.wait_ge(up_done, c + 1)
                        if c >= 3:
                            dve.wait_ge(up_gained, c - 2)
                        v.tensor_tensor(Z[c % 3][0:PM, :].rearrange("p (k c) -> p k c", k=4),
                                        M[c % 3][0:PM, :].rearrange("p (k c) -> p k c", k=4),
                                        conv_bias[0:PM, :].unsqueeze(1).to_broadcast([PM, 4, C]),
                                        ALU.add).then_inc(up_biased, 1)
                        dve.wait_ge(up_biased, c + 1)
                        v.scalar_tensor_tensor(Z[c % 3][0:PM, :], Z[c % 3][0:PM, :], 0.2, Z[c % 3][0:PM, :],
                                               ALU.mult, ALU.max).then_inc(up_leaky, 1)
                for s in range(SLOTS):
                    dve.wait_ge(down_done, s + 1)
                    xv = X[s][:].rearrange("p (j h) c -> p h j c", h=2)
                    v.tensor_tensor(xv, xv, M[3 + s][:].rearrange("p (h j c) -> p h j c", h=2, j=IMGS),
                                    ALU.add).then_inc(x_after_conv, 1)
                    dve.wait_ge(x_after_conv, s + 1)
                    if stop >= 1:
                        layernorm(p, 1, s)
                if stop >= 1:
                    for s in range(SLOTS):
                        router(p, 0, s, renorm=True)
                    for s in range(SLOTS):
                        for e in range(E + 1):
                            c = 9 * s + e
                            dve.wait_ge(ffn_down_done, c + 1)
                            if e > 0:
                                dve.wait_ge(ffn_added, c)
                            else:
                                dve.wait_ge(comb_ready, s + 1)
                            if e < E:
                                bank = M[[3, 5][(8 * s + e) % 2]]
                                for t in range(TILES):
                                    last = v.scalar_tensor_tensor(X[s][:, t, :], bank[:, t * C:t * C + C],
                                                                  comb[s][:, t, e:e + 1], X[s][:, t, :],
                                                                  ALU.mult, ALU.add)
                            else:
                                last = v.tensor_tensor(X[s][:].rearrange("p t c -> p (t c)"),
                                                       X[s][:].rearrange("p t c -> p (t c)"), M[4][:], ALU.add)
                            last.then_inc(ffn_added, 1)
                        if stop >= 2:
                            dve.wait_ge(ffn_added, 9 * s + 9)
                            layernorm(p, 2, s)
                if stop >= 2:
                    for s in range(SLOTS):
                        for i in range(3):
                            k = 3 * s + i + 1
                            dve.wait_ge(qkv_padded, k)
                            if k > 2:
                                dve.wait_ge(dw5_done, k - 2)
                            for t in range(L1_DVE):
                                dy, dx = divmod(t, 5)
                                for b in range(IMGS):
                                    win = P5[s][i][:, b, dy:dy + SIDE, dx:dx + SIDE]
                                    acc = A5[k % 2][:, b]
                                    if t == 0:
                                        kk = mark(v.tensor_scalar(acc, win, dw1[:, i, 0:1], None, ALU.mult))
                                    else:
                                        after(kk - 1)
                                        ins_ = v.scalar_tensor_tensor(acc, win, dw1[:, i, t:t + 1], acc,
                                                                      ALU.mult, ALU.add)
                                        if t < L1_DVE - 1:
                                            kk = mark(ins_)
                                        elif b == 0:
                                            kk = mark(ins_)
                                        else:
                                            ins_.then_inc(dw5_acc, 1)
                    for s in range(SLOTS):
                        for g in range(2):
                            dve.wait_ge(kv_done, 2 * s + g + 1)
                            for j in range(IMGS):
                                v.tensor_tensor(KM[s][:, g, j, 0:128], M[4 + g][:, 129 * j:129 * j + 128],
                                                headmask1[:], ALU.mult)
                                last = v.tensor_scalar(KM[s][:, g, j, 128:144],
                                                       headmask1[:, 0:128:8], M[4 + g][:, 129 * j + 128:129 * j + 129],
                                                       None, ALU.mult)
                            last.then_inc(kv_masked, 1)
                    for s in range(SLOTS):
                        for i in range(4):
                            g, h = divmod(i, 2)
                            dve.wait_ge(num_done, 4 * s + i + 1)
                            src = M[i][:, 0:288].rearrange("p (t c) -> p t c", t=2)
                            den = DEN[s][:, i, :].rearrange("p (t h) -> p t h", t=2)
                            link(v.tensor_scalar(den, src[:, :, 128:144], 1e-15, None, ALU.add))
                            link(v.reciprocal(den, den))
                            v.tensor_tensor(OTk[s][g][:, 256 * h:256 * h + 256].rearrange("p (t h d) -> p t h d", t=2, h=16),
                                            src[:, :, 0:128].rearrange("p t (h d) -> p t h d", h=16),
                                            den.unsqueeze(3).to_broadcast([P, 2, 16, 8]), ALU.mult)\
                             .then_inc(num_scaled, 1)
                    for s in range(SLOTS):
                        dve.wait_ge(proj_done, s + 1)
                        link(v.tensor_tensor(XT[s][:], TR[s][:].rearrange("p (t c) -> p t c", t=TILES),
                                             bnrow[:, 0, :].unsqueeze(1).to_broadcast([P, TILES, C]), ALU.mult))
                        dve.wait_ge(x_shifted, s + 1)
                        v.tensor_tensor(X[s][:], X[s][:], XT[s][:], ALU.add).then_inc(x_added, 1)
                        dve.wait_ge(x_added, s + 1)
                        if stop >= 3:
                            layernorm(p, 3, s)
                if stop >= 3:
                    for s in range(SLOTS):
                        router(p, 1, s, gamma=modb[:, 0:8])
                        dve.wait_ge(comb_ready, 3 + s)
                        link(v.tensor_tensor(rt[s][:, 0], comb[s][:],
                                             modb[:, 8:16].unsqueeze(1).to_broadcast([P, TILES, E]), ALU.mult))
                    for s in range(SLOTS):
                        for t in range(TILES):
                            for h in range(2):
                                c = 8 * s + 2 * t + h
                                dve.wait_ge(eo_done, c + 1)
                                for e in range(4):
                                    link(v.scalar_tensor_tensor(X[s][:, t, :], M[c % 3][:, e * C:e * C + C],
                                                                rt[s][:, 0, t, 4 * h + e:4 * h + e + 1],
                                                                X[s][:, t, :], ALU.mult, ALU.add))
                                v.nop().then_inc(eo_added, 1)
                        dve.wait_ge(eb_done, s + 1)
                        xf = X[s][:].rearrange("p t c -> p (t c)")
                        link(v.tensor_tensor(xf, xf, M[3][:], ALU.add))
                        v.nop().then_inc(x_shifted, 0) if False else None
                        if stop >= 4:
                            layernorm(p, 4, s)
                if stop >= 4:
                    for s in range(SLOTS):
                        for i in range(2):
                            n = P if i == 1 else 96
                            k = 2 * s + i + 1
                            dve.wait_ge(fused_padded, 3 * s + 2)
                            if k > 2:
                                dve.wait_ge(dw7_done, k - 2)
                            for t in range(L2_DVE):
                                dy, dx = divmod(t, 7)
                                for b in range(IMGS):
                                    win = P7[s][1 - i][0:n, b, dy:dy + SIDE, dx:dx + SIDE]
                                    acc = A7[k % 2][0:n, b]
                                    if t == 0:
                                        kk = mark(v.tensor_scalar(acc, win, dw2[0:n, 1 - i, 0:1], None, ALU.mult))
                                    else:
                                        after(kk - 1)
                                        ins_ = v.scalar_tensor_tensor(acc, win, dw2[0:n, 1 - i, t:t + 1], acc,
                                                                      ALU.mult, ALU.add)
                                        if t < L2_DVE - 1 or b == 0:
                                            kk = mark(ins_)
                                        else:
                                            ins_.then_inc(dw7_acc, 1)
                    for s in range(SLOTS):
                        dve.wait_ge(dw7_out, 2 * s + 1)
                        dve.wait_ge(fused_padded, 3 * s + 3)
                        v.tensor_tensor(G0[s][64:96, :], PA[s][64:96, :], D7[s][0][64:96, :], ALU.mult)\
                         .then_inc(g0_ready, 1)
                    for s in range(SLOTS):
                        dve.wait_ge(pw0_done, s + 1)
                        v.scalar_tensor_tensor(G1[s][0:64, :], M[4][0:64, :], pwb0[0:64, :], D7[s][0][0:64, :],
                                               ALU.add, ALU.mult).then_inc(g1_ready, 1)
                    for s in range(SLOTS):
                        dve.wait_ge(pw1_done, s + 1)
                        dve.wait_ge(dw7_out, 2 * s + 2)
                        v.scalar_tensor_tensor(G2[s], M[5][:], pwb1[:], D7[s][1], ALU.add, ALU.mult)\
                         .then_inc(g2_ready, 1)
                    for s in range(SLOTS):
                        dve.wait_ge(out2_done, s + 1)
                        link(v.tensor_tensor(X[s][:], X[s][:], TR[s][:].rearrange("p (t c) -> p t c", t=TILES), ALU.add))
                        v.tensor_tensor(X[s][:], X[s][:], bout[:].unsqueeze(1).to_broadcast([P, TILES, C]), ALU.add)\
                         .then_inc(x_after_l2, 1)
                        dve.wait_ge(x_after_l2, s + 1)
                        if stop >= 5:
                            layernorm(p, 5, s)
                if stop >= 5:

                    def positions(s):
                        dve.wait_ge(xn_ready, ln_index(5, s) - 2)
                        if s == 1:
                            dve.wait_ge(qk_done, 3)
                        xn3 = XN[s][:].rearrange("p (b m) -> p b m", b=IMGS)
                        xq3 = XP.rearrange("p (b m) -> p b m", b=IMGS)
                        link(v.tensor_scalar(XP, XN[s][:], posw[:, 1:2], posw[:, 3:4], ALU.mult, ALU.add))
                        link(v.scalar_tensor_tensor(xq3[:, :, 1:HW], xn3[:, :, 0:HW - 1], posw[:, 0:1],
                                                    xq3[:, :, 1:HW], ALU.mult, ALU.add))
                        link(v.scalar_tensor_tensor(xq3[:, :, 0:HW - 1], xn3[:, :, 1:HW], posw[:, 2:3],
                                                    xq3[:, :, 0:HW - 1], ALU.mult, ALU.add))
                        v.tensor_tensor(XP, XP, XN[s][:], ALU.add).then_inc(xp_ready, 1)

                    def values(s):
                        dve.wait_ge(qk_done, 3 * s + 3)
                        dve.wait_ge(v_ones, 1)
                        v.tensor_tensor(Vh[s][:, :, :, 0:HD],
                                        M[2][:].rearrange("p (t h d) -> p t h d", t=TILES, h=HEADS),
                                        bv[:].rearrange("p (h d) -> p h d", h=HEADS).unsqueeze(1)
                                        .to_broadcast([P, TILES, HEADS, HD]), ALU.add).then_inc(v_ready, 1)

                    def divide(s, g):
                        dve.wait_ge(po_turned, 2 * s + g + 1)
                        src = M[2][:].rearrange("p (t h c) -> p t h c", t=TILES, h=4)
                        link(v.reciprocal(rdn[:, g], src[:, :, :, HD]))
                        v.tensor_tensor(OT[s][:, :, 4 * g:4 * g + 4, :], src[:, :, :, 0:HD],
                                        rdn[:, g].unsqueeze(3).to_broadcast([P, TILES, 4, HD]), ALU.mult)\
                         .then_inc(ot_ready, 1)

                    def add_attention(s):
                        dve.wait_ge(wo_done, s + 1)
                        dve.wait_ge(x_shifted, 3 + s)
                        xf = X[s][:].rearrange("p t c -> p (t c)")
                        v.tensor_tensor(xf, xf, M[2][:], ALU.add).then_inc(x_after_attn, 1)
                        dve.wait_ge(x_after_attn, s + 1)
                    positions(0)
                    values(0)
                    for c in range(UNITS):
                        if c == 6:
                            positions(1)
                        if c == 12:
                            values(1)
                        if c == 21:
                            divide(0, 0)
                        if c == 23:
                            divide(0, 1)
                        if c == 27:
                            add_attention(0)
                            if stop >= 6:
                                ln_stats(6, 0)
                        if c == 30 and stop >= 6:
                            ln_apply(6, 0)
                        lg = [LG[c % 3][:, q * 256:q * 256 + 256] for q in range(2)]
                        rp = [REP[c % 2][:, q * 256:q * 256 + 256] for q in range(2)]
                        t8 = top8[c % 4]
                        dve.wait_ge(lg_copied, c + 1)
                        k = [mark(v.max(t8[:, q, 0:8], lg[q])) for q in range(2)]
                        after(k[1])
                        v.tensor_scalar(nmx[c % 4][:], t8[:, :, 0], -1.0, None, ALU.mult).then_inc(lg_max, 1)
                        if c >= 2:
                            dve.wait_ge(rep_exp, c - 1)
                        k = [mark(v.match_replace(rp[q], t8[:, q, 0:8], lg[q], NEG)) for q in range(2)]
                        k2 = []
                        for q in range(2):
                            after(k[q])
                            k2.append(mark(v.max(t8[:, q, 8:16], rp[q])))
                        for q in range(2):
                            after(k2[q])
                            last = v.match_replace(rp[q], t8[:, q, 8:16], rp[q], NEG)
                        last.then_inc(rep_ready, 1)
                    divide(1, 0)
                    divide(1, 1)
                    add_attention(1)
                    if stop >= 6:
                        layernorm(p, 6, 1)
                if stop >= 6:
                    for s in range(SLOTS):
                        q = [hst[s][:, i, :] for i in range(9)]
                        dve.wait_ge(ss_done, s + 1)
                        v.tensor_scalar(q[1], M[4][:, 2 * s:2 * s + 2], 1.0 / (C * HW), None, ALU.mult)\
                         .then_inc(ms_ready, 1)
                        dve.wait_ge(std_ready, s + 1)
                        link(v.tensor_scalar(q[3], q[2], 2.513930578568423, 1e-8, ALU.mult, ALU.add))
                        link(v.tensor_scalar(q[4], q[3], 2.0 / 15.0, None, ALU.mult))
                        link(v.reciprocal(q[5], q[4]))
                        link(v.tensor_scalar(q[6], q[4], 0.5, None, ALU.mult))
                        link(v.tensor_scalar(q[7], q[3], -1.0, None, ALU.mult))
                        link(v.tensor_scalar(q[8], q[2], 2.513930578568423 / 15.0, None, ALU.mult))
                        MAGIC = 1.5 * 2.0 ** 23
                        dve.wait_ge(had_copied, s + 1)

                        def both(dst, src, s1, s2, o1, o2):
                            for j in range(IMGS):
                                c_ = lambda i: q[i][:, j:j + 1] if isinstance(i, int) else i
                                k = mark(v.tensor_scalar(dst[:, 256 * j:256 * j + 256], src[:, 256 * j:256 * j + 256],
                                                         c_(s1), c_(s2), o1, o2))
                            after(k)
                        both(H1[s], HS[s], 3, 7, ALU.min, ALU.max)
                        for j in range(IMGS):
                            k = mark(v.tensor_scalar(H1[s][:, 256 * j:256 * j + 256], H1[s][:, 256 * j:256 * j + 256],
                                                     q[5][:, j:j + 1], None, ALU.mult))
                        after(k)
                        link(v.tensor_scalar(H1[s], H1[s], 0.5, MAGIC, ALU.add, ALU.add))
                        link(v.tensor_scalar(H1[s], H1[s], -MAGIC, None, ALU.add))
                        both(H1[s], H1[s], 4, 6, ALU.mult, ALU.subtract)
                        link(v.tensor_tensor(H2[s], H1[s], HS[s], ALU.subtract))
                        link(v.scalar_tensor_tensor(H2[s], H2[s], -1.0, H2[s], ALU.mult, ALU.max))
                        for j in range(IMGS):
                            k = mark(v.tensor_scalar(H2[s][:, 256 * j:256 * j + 256], H2[s][:, 256 * j:256 * j + 256],
                                                     q[8][:, j:j + 1], None, ALU.is_le))
                        after(k)
                        link(v.tensor_tensor(H2[s], HS[s], H2[s], ALU.mult))
                        link(v.tensor_tensor(H3[s], H1[s], H2[s], ALU.subtract))
                        link(v.tensor_tensor(H3[s], H2[s], H3[s], ALU.add))
                        xf = X[s][:].rearrange("p t c -> p (t c)")
                        v.tensor_tensor(xf, xf, H3[s], ALU.add).then_inc(x_after_had, 1)
                        dve.wait_ge(x_after_had, s + 1)
                        if stop >= 7:
                            layernorm(p, 7, s)
                if stop >= 7:
                    for s in range(SLOTS):
                        router(p, 2, s)
                    for s in range(SLOTS):
                        for i in range(5):
                            c = 5 * s + i
                            n = P if i < 4 else 64
                            dve.wait_ge(silu_done, c + 1)
                            dve.wait_ge(upp_done, c + 1)
                            v.tensor_tensor(GU[s][i][0:n, :], SG[c % 2][0:n, :], M[2 + c % 2][0:n, :], ALU.mult)\
                             .then_inc(gu_ready, 1)
                        for i in range(4):
                            dve.wait_ge(cb_done, 4 * s + i + 1)
                            dve.wait_ge(gu_ready, 5 * s + 5)
                            v.tensor_tensor(GU[s][i], GU[s][i], M[4][:] if i % 2 == 0 else M[5][:], ALU.mult)\
                             .then_inc(gus_ready, 1)
                    for s in range(SLOTS):
                        dve.wait_ge(moe_done, s + 1)
                        xf = X[s][:].rearrange("p t c -> p (t c)")
                        v.tensor_tensor(xf, xf, M[s][:], ALU.add).then_inc(x_final, 1)
                else:
                    for s in range(SLOTS):
                        dve.drain()
                        link(v.tensor_copy(hst[s][:, 0, :], X[s][:, 0, 0:2]))
                        v.tensor_copy(X[s][:, 0, 0:2], hst[s][:, 0, :]).then_inc(x_final, 1)
                new_steps()
                next_pass(dve, "dve")

        @block.tensor
        def _(pe):
            mm = nc.tensor.matmul
            tr = nc.tensor.transpose
            pe.wait_ge(weights_in, 16 * NW)
            pe.wait_ge(consts, 4)
            mm(TR[0][0:16, 0:16], ins[:], modw[:], start=True, stop=True).then_inc(pe_setup, 1)
            pe.wait_ge(dve_setup, 3)
            for e in range(E):
                last = mm(M[2][:, e:e + 1], beta_w[:, e, :], inssum[:], start=True, stop=True)
            last.then_inc(pe_setup, 1)
            pe.wait_ge(act_setup, 1)
            mm(TR[1][:, 0:16], sixteenth[:], modr[:], start=True, stop=True).then_inc(pe_setup, 1)
            pe.wait_ge(dve_setup, 4)
            tr(M[1][0:E, 0:C], btd[:], ident[:]).then_inc(pe_setup, 1)
            mm(M[0][:, 0:256], ones[:], bndiag[:].rearrange("p g c -> p (g c)"), start=True, stop=True)\
                .then_inc(pe_setup, 1)
            pe.wait_ge(act_setup, 4)
            pe.wait_ge(pool_setup, 2)

            def turn(bank, src4, sig):
                for t in range(TILES):
                    last = tr(bank[:, t * P:t * P + P], src4(t), ident[:])
                last.then_inc(sig, 1)

            def ln_turn(p, n, s):
                pe.wait_ge(xt_ready, ln_index(n, s))
                turn(TR[s], lambda t: XT[s][:, t, :], xt_turned)

            def logits(p, r, n, s, Wg):
                pe.wait_ge(xn_ready, ln_index(n, s) - 2)
                for t in range(TILES):
                    last = mm(TR[s][:, t * E:t * E + E], XN[s][:, t * P:t * P + P], Wg[:], start=True, stop=True)
                last.then_inc(logits_done, 1)

            def comb_turn(p, r, s):
                pe.wait_ge(comb_ready, 2 * r + s + 1)
                for t in range(TILES):
                    last = tr(TR[s][0:E, t * P:t * P + P], comb[s][:, t, :], ident[:])
                last.then_inc(comb_turned, 1)

            with pe.Fori(0, PASSES) as p:
                for s in range(SLOTS):
                    pe.wait_ge(x_loaded[s], 16)
                    turn(TR[s], lambda t: XC[s][:, t // 2, (t % 2) * P:(t % 2) * P + P], x_turned)
                for s in range(SLOTS):
                    pe.wait_ge(xt_ready, ln_index(0, s))
                    xv = XT[s][:].rearrange("p (j h) c -> p h j c", h=2)
                    for m2 in range(7):
                        c = 7 * s + m2
                        if c >= 3:
                            pe.wait_ge(up_biased, c - 2)
                        for m in (2 * m2, 2 * m2 + 1):
                            parts = [i for i, (mm_, h) in enumerate(UP_PARTS) if mm_ == m]
                            for n_, i in enumerate(parts):
                                last = mm(M[c % 3][0:PM, (m % 2) * 256:(m % 2) * 256 + 256], upw[:, i, :],
                                          xv[:, UP_PARTS[i][1]], start=n_ == 0, stop=n_ == len(parts) - 1)
                        last.then_inc(up_done, 1)
                for s in range(SLOTS):
                    pe.wait_ge(up_clipped, 7 * s + 7)
                    for h in range(2):
                        parts = [i for i, (h_, k) in enumerate(DOWN_PARTS) if h_ == h]
                        for n_, i in enumerate(parts):
                            last = mm(M[3 + s][:, h * 256:h * 256 + 256], downw[0:PM, i, :],
                                      Y[s][0:PM, DOWN_PARTS[i][1], :], start=n_ == 0, stop=n_ == len(parts) - 1)
                    last.then_inc(down_done, 1)
                if stop >= 1:
                    for s in range(SLOTS):
                        ln_turn(p, 1, s)
                    for s in range(SLOTS):
                        logits(p, 0, 1, s, Wg0)
                    def ffn_up(s, e):
                        for hc in range(4):
                            c = 32 * s + 4 * e + hc
                            if c >= 3:
                                pe.wait_ge(ffn_gelu_done, c - 2)
                            mm(M[c % 3][:], W1[:, e, hc * P:hc * P + P], XN[s][:], start=True, stop=True)\
                                .then_inc(ffn_up_done, 1)

                    def ffn_down(s, e):
                        d = 8 * s + e
                        pe.wait_ge(ffn_gelu_done, 4 * d + 4)
                        if d >= 2:
                            prev = d - 2
                            pe.wait_ge(ffn_added, prev + 1 + (1 if prev >= 8 else 0))
                        for t in range(TILES):
                            for hc in range(4):
                                last = mm(M[[3, 5][d % 2]][:, t * C:t * C + C], H[d % 2][hc][:, t * P:t * P + P],
                                          W2[:, e, hc, :], start=hc == 0, stop=hc == 3)
                        last.then_inc(ffn_down_done, 1)
                    for s in range(SLOTS):
                        ffn_up(s, 0)
                        for e in range(E):
                            if e + 1 < E:
                                ffn_up(s, e + 1)
                            ffn_down(s, e)
                        comb_turn(p, 0, s)
                        pe.wait_ge(combT_ready, s + 1)
                        if s == 1:
                            pe.wait_ge(ffn_added, 9)
                        for t in range(TILES):
                            last = mm(M[4][:, t * C:t * C + C], combT[s][:, t * P:t * P + P], b2[:],
                                      start=True, stop=True)
                        last.then_inc(ffn_down_done, 1)
                if stop >= 2:
                    for s in range(SLOTS):
                        ln_turn(p, 2, s)
                    for s in range(SLOTS):
                        pe.wait_ge(xn_ready, ln_index(2, s) - 2)
                        for i in range(3):
                            if s == 1:
                                pe.wait_ge(qkv_padded, i + 1)
                            mm(M[i][:], Wqkv1[:, i, :], XN[s][:], start=True, stop=True).then_inc(qkv_done, 1)
                        pe.wait_ge(ffn_added, 18)
                        for h in range(2):
                            if s == 1:
                                pe.wait_ge(kvpx_v, h + 1)
                            for t in range(2 * h, 2 * h + 2):
                                last = mm(M[3 + h][:, (t % 2) * 256:(t % 2) * 256 + 256],
                                          XN[s][:, t * P:t * P + P], Wqkv1[:, 1:3, :].rearrange("p i c -> p (i c)"),
                                          start=True, stop=True)
                            last.then_inc(kvpx_done, 1)
                    for s in range(SLOTS):
                        for i in range(3):
                            k = 3 * s + i + 1
                            bank = M[[5, 0, 1][i]]
                            pe.wait_ge(qkv_padded, k if s == 1 else max(k, 3 + i))
                            if i > 0 and s == 0:
                                pe.wait_ge(qkv_padded, 3 + i)
                            if s == 1:
                                pe.wait_ge(dw5_out, i + 1)
                            for t in range(L1_DVE, L1_TAPS):
                                dy, dx = divmod(t, 5)
                                mm(bank[:].rearrange("p (b y x) -> p b y x", b=IMGS, y=SIDE),
                                   w5[:, i, t - L1_DVE, :], P5[s][i][:, :, dy:dy + SIDE, dx:dx + SIDE],
                                   start=t == L1_DVE, stop=False)
                            pe.wait_ge(dw5_acc, k)
                            mm(bank[:], pw1T[:, i, :], A5[k % 2].rearrange("p b y x -> p (b y x)"),
                               start=False, stop=True).then_inc(dw5_done, 1)
                    for s in range(SLOTS):
                        for g in range(2):
                            pe.wait_ge(dw5_out, 3 * s + g + 2)
                            if g == 0:
                                pe.wait_ge(qkv_padded, 6)
                            pe.wait_ge(kvpx_v, 4)
                            if s == 1:
                                pe.wait_ge(agg_px, g + 1)
                            turn(M[2 + g], lambda t: KVC[s][g][:, t * P:t * P + P], agg_turned)
                    for s in range(SLOTS):
                        for g in range(2):
                            if g == 1:
                                pe.wait_ge(agg_px, 2 * s + 2)
                                pe.wait_ge(dw5_out, 6)
                            if s == 1:
                                pe.wait_ge(kv_masked, g + 1)
                            for j in range(IMGS):
                                for h in range(2):
                                    t = 2 * j + h
                                    last = mm(M[4 + g][:, 129 * j:129 * j + 129], KV[s][g][:, t, 0:128],
                                              KV[s][g][:, t, 128:257], start=h == 0, stop=h == 1)
                            last.then_inc(kv_done, 1)
                    for s in range(SLOTS):
                        for i in range(4):
                            g, h = divmod(i, 2)
                            pe.wait_ge(kv_masked, 2 * s + g + 1)
                            if s == 0:
                                pe.wait_ge(agg_px, 4)
                            if s == 1:
                                pe.wait_ge(num_scaled, i + 1)
                            for t in range(2):
                                last = mm(M[i][:, 144 * t:144 * t + 144],
                                          [Q1, Q2][g][s][:, (2 * h + t) * P:(2 * h + t) * P + P],
                                          KM[s][:, g, h, :], start=True, stop=True)
                            last.then_inc(num_done, 1)
                    for s in range(SLOTS):
                        for g in range(2):
                            pe.wait_ge(num_scaled, 4 * s + 2 * g + 2)
                            pe.wait_ge(kv_masked, 4)
                            if s == 1:
                                pe.wait_ge(o_ready, g + 1)
                            turn(M[4 + g], lambda t: OTk[s][g][:, t * P:t * P + P], o_turned)
                    for s in range(SLOTS):
                        pe.wait_ge(o_ready, 2 * s + 2)
                        for t in range(TILES):
                            for g in range(2):
                                last = mm(TR[s][:, t * C:t * C + C], OC[s][g][:, t * P:t * P + P], proj[:, g, :],
                                          start=g == 0, stop=g == 1)
                        last.then_inc(proj_done, 1)
                if stop >= 3:
                    for s in range(SLOTS):
                        ln_turn(p, 3, s)
                    for s in range(SLOTS):
                        logits(p, 1, 3, s, Wg1)
                    for s in range(SLOTS):
                        for t in range(TILES):
                            for h in range(2):
                                c = 8 * s + 2 * t + h
                                if c >= 3:
                                    pe.wait_ge(eo_added, c - 2)
                                mm(M[c % 3][:], XN[s][:, t * P:t * P + P],
                                   Wexp[:, 4 * h:4 * h + 4, :].rearrange("p e c -> p (e c)"),
                                   start=True, stop=True).then_inc(eo_done, 1)
                        comb_turn(p, 1, s)
                        pe.wait_ge(combT_ready, 3 + s)
                        if s == 1 and stop >= 4:
                            pe.wait_ge(xt_ready, ln_index(4, 0))
                        for t in range(TILES):
                            last = mm(M[3][:, t * C:t * C + C], combT[s][:, t * P:t * P + P], bt[:],
                                      start=True, stop=True)
                        last.then_inc(eb_done, 1)
                if stop >= 4:
                    for s in range(SLOTS):
                        ln_turn(p, 4, s)
                    for s in range(SLOTS):
                        pe.wait_ge(xn_ready, ln_index(4, s) - 2)
                        for i in range(3):
                            if s == 1:
                                pe.wait_ge(fused_padded, i + 1)
                            out = [M[4][:], M[5][0:96, :], M[3][64:96, :]][i]
                            mm(out, [Win[:, 0:128], Win[:, 128:224], Win[:, 224:256]][i], XN[s][:],
                               start=True, stop=True).then_inc(fused_done, 1)
                    for s in range(SLOTS):
                        for i in range(2):
                            n = P if i == 1 else 96
                            k = 2 * s + i + 1
                            pe.wait_ge(fused_padded, 3 * s + 2)
                            if s == 1:
                                pe.wait_ge(dw7_out, i + 1)
                            bank = M[i][0:n, :]
                            for t in range(L2_DVE, L2_TAPS):
                                dy, dx = divmod(t, 7)
                                mm(bank.rearrange("p (b y x) -> p b y x", b=IMGS, y=SIDE),
                                   w7[0:n, 1 - i, t - L2_DVE, 0:n], P7[s][1 - i][0:n, :, dy:dy + SIDE, dx:dx + SIDE],
                                   start=t == L2_DVE, stop=False)
                            pe.wait_ge(dw7_acc, k)
                            mm(bank, ident[0:n, 0:n], A7[k % 2][0:n].rearrange("p b y x -> p (b y x)"),
                               start=False, stop=True).then_inc(dw7_done, 1)
                    for s in range(SLOTS):
                        pe.wait_ge(g0_ready, s + 1)
                        if s == 0:
                            pe.wait_ge(fused_padded, 6)
                        else:
                            pe.wait_ge(g1_ready, 1)
                        mm(M[4][0:64, :], pwT0[64:96, :], G0[s][64:96, :], start=True, stop=True)\
                            .then_inc(pw0_done, 1)
                    for s in range(SLOTS):
                        pe.wait_ge(g1_ready, s + 1)
                        if s == 1:
                            pe.wait_ge(g2_ready, 1)
                        mm(M[5][:], pwT1[0:64, :], G1[s][0:64, :], start=True, stop=True).then_inc(pw1_done, 1)
                    for s in range(SLOTS):
                        pe.wait_ge(g2_ready, s + 1)
                        for t in range(TILES):
                            last = mm(TR[s][:, t * C:t * C + C], G2[s][:, t * P:t * P + P], Wout[:],
                                      start=True, stop=True)
                        last.then_inc(out2_done, 1)
                if stop >= 5:
                    for s in range(SLOTS):
                        ln_turn(p, 5, s)
                    def project(s, i):
                        if i == 0:
                            pe.wait_ge(xp_ready, s + 1)
                            if s == 1:
                                pe.wait_ge(v_ready, 1)
                        else:
                            pe.wait_ge(qk_ready, 2 * s + i)
                        if i < 2:
                            mm(M[2][:], Wqkv2[:, i, :], XP, start=True, stop=True).then_inc(qk_done, 1)
                        else:
                            for t in range(TILES):
                                last = mm(M[2][:, t * C:t * C + C], XP[:, t * P:t * P + P], Wqkv2[:, 2, :],
                                          start=True, stop=True)
                            last.then_inc(qk_done, 1)

                    def lg(c):
                        hh, j = divmod(c, 2)
                        s = hh // HEADS
                        pe.wait_ge(qm_ready, hh + 1)
                        pe.wait_ge(qk_ready, 2 * s + 2)
                        if c >= 2:
                            pe.wait_ge(lg_copied, c - 1)
                        for q in range(2):
                            t = 2 * j + q
                            last = mm(M[c % 2][:, q * 256:q * 256 + 256],
                                      QM[hh % 3][:, t * P:t * P + P], Kc[s][:, j * 256:j * 256 + 256],
                                      start=True, stop=True)
                        last.then_inc(lg_done, 1)

                    def pv(gr):
                        s, g = gr // 4, gr // 2 % 2
                        pe.wait_ge(pt_ready, 4 * gr + 4)
                        pe.wait_ge(v_ready, s + 1)
                        if gr in (4, 5):
                            pe.wait_ge(po_ready, 1)
                        bank = [M[5], TR[s]][g]
                        for j in range(IMGS):
                            for kt in range(2):
                                for x in range(2):
                                    c = 4 * gr + 2 * x + j
                                    h = c // 2 % HEADS
                                    hq = h % 4
                                    last = mm(bank[32 * hq:32 * hq + 32, j * 256:j * 256 + 256],
                                              Vh[s][:, 2 * j + kt, h, :], PT[c % 5][:, kt * 256:kt * 256 + 256],
                                              start=kt == 0, stop=kt == 1)
                        last.then_inc(pv_done, 1)

                    def post(s, i):
                        if i < 2:
                            pe.wait_ge(po_ready, 2 * s + i + 1)
                            if i == 1:
                                pe.wait_ge(ot_ready, 2 * s + 1)
                            elif s == 0:
                                pe.wait_ge(v_ready, 2)
                            else:
                                pe.wait_ge(x_after_attn, 1)
                            turn(M[2], lambda t: PO[i][:, t * P:t * P + P], po_turned)
                        elif i == 2:
                            pe.wait_ge(ot_ready, 2 * s + 2)
                            turn(M[2], lambda t: OT[s][:, t].rearrange("p h d -> p (h d)"), ot_turned)
                        else:
                            pe.wait_ge(oc_ready, s + 1)
                            for t in range(TILES):
                                last = mm(M[2][:, t * C:t * C + C], OCf[s][:, t * P:t * P + P], Wo[:],
                                          start=True, stop=True)
                            last.then_inc(wo_done, 1)
                    for i in range(3):
                        project(0, i)
                    lg(0)
                    lg(1)
                    for c in range(UNITS):
                        if c + 2 < UNITS:
                            lg(c + 2)
                        pe.wait_ge(pr_ready, c + 1)
                        if c >= 2:
                            pe.wait_ge(pt_ready, c - 1)
                        for kt in range(2):
                            for q in range(2):
                                last = tr(M[3 + c % 2][:, kt * 256 + q * P:kt * 256 + q * P + P],
                                          PR[c % 2][:, q * 256 + kt * P:q * 256 + kt * P + P], ident[:])
                        last.then_inc(pt_done, 1)
                        if c % 4 == 0 and c > 0:
                            pv(c // 4 - 1)
                        if c in (7, 8, 9):
                            project(1, c - 7)
                        if c in (18, 20, 22, 24):
                            post(0, (c - 18) // 2)
                    pv(UNITS // 4 - 1)
                    for i in range(4):
                        post(1, i)
                if stop >= 6:
                    for s in range(SLOTS):
                        ln_turn(p, 6, s)
                    for s in range(SLOTS):
                        pe.wait_ge(xn_ready, ln_index(6, s) - 2)
                        pe.wait_ge(x_after_attn, 2)
                        for t in range(TILES):
                            last = mm(M[2 + s][:, t * C:t * C + C], XN[s][:, t * P:t * P + P], Whad[:],
                                      start=True, stop=True)
                        last.then_inc(had_done, 1)
                    for s in range(SLOTS):
                        pe.wait_ge(had_sq, s + 1)
                        if s == 1:
                            pe.wait_ge(ms_ready, 1)
                        mm(M[4][:, 2 * s:2 * s + 2], ones[:], hst[s][:, 0, :], start=True, stop=True)\
                            .then_inc(ss_done, 1)
                if stop >= 7:
                    for s in range(SLOTS):
                        ln_turn(p, 7, s)
                    for s in range(SLOTS):
                        logits(p, 2, 7, s, Wg3)
                    for s in range(SLOTS):
                        for i in range(5):
                            c = 5 * s + i
                            n = P if i < 4 else 64
                            if c >= 2:
                                pe.wait_ge(gu_ready, c - 1)
                            mm(M[c % 2][0:n, :], Wgate[:, i, 0:n], XN[s][:], start=True, stop=True)\
                                .then_inc(gate_done, 1)
                            mm(M[2 + c % 2][0:n, :], Wup[:, i, 0:n], XN[s][:], start=True, stop=True)\
                                .then_inc(upp_done, 1)
                        comb_turn(p, 2, s)
                        pe.wait_ge(combT_ready, 5 + s)
                        for i in range(4):
                            k = 4 * s + i
                            if k >= 2:
                                pe.wait_ge(gus_ready, k - 1)
                            mm(M[4 + i % 2][:], sel3[:, i, :], combT[s][:], start=True, stop=True)\
                                .then_inc(cb_done, 1)
                    for s in range(SLOTS):
                        pe.wait_ge(gus_ready, 4 * s + 4)
                        pe.wait_ge(gu_ready, 10)
                        for t in range(TILES):
                            for i in range(5):
                                n = P if i < 4 else 64
                                last = mm(M[s][:, t * C:t * C + C], GU[s][i][0:n, t * P:t * P + P],
                                          Wdown[0:n, i, :], start=i == 0, stop=i == 4)
                        last.then_inc(moe_done, 1)
                for s in range(SLOTS):
                    pe.wait_ge(x_final, s + 1)
                    turn(TR[s], lambda t: X[s][:, t, :], xf_turned)
                next_pass(pe, "pe")


def layout(inputs):
    f = {k: np.asarray(v) for k, v in inputs.items()}
    T = np.ascontiguousarray
    rep = lambda v: T(np.broadcast_to(np.asarray(v).reshape(1, -1), (P, np.asarray(v).size)))
    o = {}
    o["x"] = T(f["x"].reshape(B, C, HW).transpose(1, 0, 2))
    o["ident"] = np.eye(P, dtype=np.float32)
    o["taps"] = rep(np.concatenate([f["L0_conv_up_filter"], f["L0_conv_down_filter"]]))
    hh, ww = np.divmod(np.arange(P), SIDE)
    tp = np.arange(TAPS)
    y = np.arange(UP)
    mA = np.stack([(y[None, :] - 2 * (hh[:, None] + 8 * h))[:, :, None] == tp for h in (0, 1)], 1)
    mB = (y[None, :] - 2 * ww[:, None])[:, :, None] == tp
    r, xx = np.divmod(np.arange(P), UP)
    dA = np.stack([(11 - (ROWS_M * k + r[:, None] - 2 * (8 * h + np.arange(8)[None, :])))[:, :, None] == tp
                   for h, k in DOWN_PARTS], 1)
    dB = (11 - (xx[:, None] - 2 * np.arange(SIDE)[None, :]))[:, :, None] == tp
    o["masks"] = T(np.concatenate([m.reshape(P, -1) for m in (mA, mB, dA, dB)], 1).astype(np.float32))
    o["conv_bias"] = rep(f["L0_conv_bias"])
    o["Wg0"] = f["L0_ffn_Wg"]
    o["pick"] = rep(np.arange(E, 0, -1).astype(np.float32))
    o["W1"] = T(f["L0_ffn_W1"].transpose(1, 0, 2))
    o["b1"] = T(f["L0_ffn_b1"].reshape(E * 4, P).T)
    o["W2"] = T(f["L0_ffn_W2"].reshape(E, 4, P, C).transpose(2, 0, 1, 3))
    o["b2"] = f["L0_ffn_b2"]
    perm = (24 * np.arange(16)[None, :, None] + 8 * np.arange(3)[:, None, None] + np.arange(8)).reshape(3, P)
    o["Wqkv1"] = T(f["L1_conv_qkv_w"].reshape(384, C)[perm].transpose(2, 0, 1))
    o["dw1"] = T(f["L1_conv_agg_dw_w"].reshape(384, 25)[perm].transpose(1, 0, 2))
    pw = f["L1_conv_agg_pw_w"].reshape(384, 8)[perm]
    blk = np.zeros((P, 3, P), np.float32)
    co = np.arange(P)
    for ci in range(8):
        blk[8 * (co // 8) + ci, :, co] = pw[:, co, ci].T
    o["pw1T"] = blk
    o["proj"] = T(f["L1_conv_proj_w"].reshape(C, 2, P).transpose(2, 1, 0))
    o["headmask1"] = (co[:, None] // 8 == co[None, :] // 8).astype(np.float32)
    o["bn"] = T(np.stack([f["L1_conv_bn_gamma"], f["L1_conv_bn_beta"], f["L1_conv_bn_mean"], f["L1_conv_bn_var"]], 1))
    o["ins"] = T(f["L1_ffn_Ins_tk"][0].T)
    o["modw"] = T(np.concatenate([f["L1_ffn_rmod_w"], f["L1_ffn_gamma_w"].T], 1))
    o["beta_w"] = T(f["L1_ffn_beta_w"].transpose(1, 0, 2))
    o["exp_bT"] = T(f["L1_ffn_expert_b"].T)
    o["Wg1"] = f["L1_ffn_gate_w"]
    o["Wexp"] = T(f["L1_ffn_expert_w"].transpose(1, 0, 2))
    order = np.concatenate([np.arange(128, 256), np.arange(64, 128), np.arange(32, 64), np.arange(0, 32)])
    o["Win"] = T(f["L2_conv_w_in"][order].T)
    b = f["L2_conv_b_in"][order]
    pad = lambda v, lo=0: np.concatenate([np.zeros(lo, np.float32), v, np.zeros(P - lo - v.size, np.float32)])
    o["bin"] = T(np.stack([b[0:128], pad(b[128:224])], 1))
    o["bpa"] = pad(b[224:256], 64).reshape(P, 1)
    dorder = order[:224] - 32
    d = f["L2_conv_dw_w"].reshape(224, 49)[dorder]
    o["dw2"] = T(np.stack([d[0:128], np.concatenate([d[128:], np.zeros((32, 49), np.float32)])], 1))
    db = f["L2_conv_dw_b"][dorder]
    o["dwb2"] = T(np.stack([db[0:128], pad(db[128:])], 1))
    z = np.zeros((P, 64), np.float32)
    z[64:96] = f["L2_conv_pw0_w"].T
    o["pwT0"] = z
    o["pwb0"] = pad(f["L2_conv_pw0_b"]).reshape(P, 1)
    z = np.zeros((P, P), np.float32)
    z[0:64] = f["L2_conv_pw1_w"].T
    o["pwT1"] = z
    o["pwb1"] = f["L2_conv_pw1_b"].reshape(P, 1)
    o["Wout"] = T(f["L2_conv_w_out"].T)
    o["bout"] = rep(f["L2_conv_b_out"])
    o["posw"] = T(np.concatenate([f["L2_ffn_pos_w"].reshape(C, 3), f["L2_ffn_pos_b"].reshape(C, 1)], 1))
    o["Wqkv2"] = T(f["L2_ffn_qkv_w"].reshape(3, C, C).transpose(2, 0, 1))
    o["bqk"] = T(f["L2_ffn_qkv_b"][0:256].reshape(2, C).T)
    o["bv"] = rep(f["L2_ffn_qkv_b"][256:384])
    o["headmask2"] = (co[:, None] // HD == np.arange(HEADS)[None, :]).astype(np.float32)
    o["Wo"] = T(f["L2_ffn_wo_w"].T)
    o["bo"] = rep(f["L2_ffn_wo_b"])
    z = np.zeros((P, P), np.float32)
    z[0:64, 0:64] = f["L3_conv_aux_matrix"]
    z[64:, 64:] = f["L3_conv_aux_matrix"]
    o["Whad"] = z
    o["Wg3"] = f["L3_ffn_router"]

    def pairs(we, ws):
        z = np.zeros((P, 5, P), np.float32)
        z[:, 0:4] = we.reshape(4, 2, C, 64).transpose(2, 0, 1, 3).reshape(C, 4, P)
        z[:, 4, 0:64] = ws
        return z
    o["Wgate"] = pairs(f["L3_ffn_W_gate"], f["L3_ffn_shared_gate"])
    o["Wup"] = pairs(f["L3_ffn_W_up"], f["L3_ffn_shared_up"])
    z = np.zeros((P, 5, C), np.float32)
    z[:, 0:4] = f["L3_ffn_W_down"].reshape(4, P, C).transpose(1, 0, 2)
    z[0:64, 4] = f["L3_ffn_shared_down"]
    o["Wdown"] = z
    z = np.zeros((E, 4, P), np.float32)
    for e in range(E):
        z[e, e // 2, 64 * (e % 2):64 * (e % 2) + 64] = 1.0
    o["sel3"] = z
    return {k: np.ascontiguousarray(v) for k, v in o.items()}


def kernel(**inputs):
    import concourse.bacc as _bacc
    from concourse.bass_utils import run_bass_kernel_spmd as _run

    nc = _bacc.Bacc("TRN2", target_bir_lowering=False, num_devices=1)
    arrays, args = {}, {}
    for name, v in layout(inputs).items():
        arrays[f"in_{name}_dram"] = v
        args[name] = nc.dram_tensor(f"in_{name}_dram", v.shape, mybir.dt.from_np(v.dtype), kind="ExternalInput").ap()
    out = nc.dram_tensor("out_0_dram", (B, C, HW), mybir.dt.float32, kind="ExternalOutput").ap()
    args["out"] = out.rearrange("b c n -> c b n")
    metaformer(nc, args)
    r = _run(nc, [arrays], core_ids=[0])
    return r.results[0]["out_0_dram"].reshape(B, C, SIDE, SIDE)
```

```python
import numpy as np
import concourse.bass as bass
from concourse import mybir
from contextlib import ExitStack

B, C, HW = 8, 128, 256
SIDE = 16
P = 128
SLOTS = 2
IMGS = 2
PASSES = B // (SLOTS * IMGS)
TILES = IMGS * HW // P
N = IMGS * HW
E = 8
HID = 512
TAPS = 12
UP = 42
ROWS_M = 3
M_UP = UP // ROWS_M
PM = ROWS_M * UP

def _up_halves(m):
    lo, hi = max(0, -(-(ROWS_M * m - 11) // 2)), min(SIDE - 1, (ROWS_M * m + 2) // 2)
    return [h for h in (0, 1) if lo <= 8 * h + 7 and hi >= 8 * h]
UP_PARTS = [(m, h) for m in range(M_UP) for h in _up_halves(m)]
DOWN_PARTS = [(h, k) for h in (0, 1) for k in range(M_UP)
              if ROWS_M * k + 2 >= 16 * h and ROWS_M * k <= 16 * h + 14 + 11]

L1_TAPS, L1_PAD, L1_W = 25, 2, 20
L2_TAPS, L2_PAD, L2_W = 49, 3, 22
L1_DVE, L1_POOL = 10, 5
L2_DVE, L2_POOL = 19, 12
L1_PE, L2_PE = L1_TAPS - L1_DVE - L1_POOL, L2_TAPS - L2_DVE - L2_POOL
RING = 3
HEADS, HD = 8, 16
N_UP = 3 * UP
N_DN = 8 * len(DOWN_PARTS) + SIDE
PACKS = {
    "first": [("ident", (P,)), ("tap_no", (N_UP + N_DN,)), ("taps", (2 * TAPS,)), ("conv_bias", (C,)),
              ("bn", (4,)),
              ("ins", (16,)), ("modw", (16,)),
              ("exp_bT", (E,)), ("dw1", (3, L1_TAPS)),
              ("pw1T", (3, P)),
              ("dw2", (2, L2_TAPS))],
    "stage1": [("Wg0", (E,)), ("pick", (E,)),
               ("b1", (E * 4,)), ("b2T", (E,)), ("W1", (E, HID)), ("W2", (E, 4, C))],
    "later": [("Wqkv1", (3, P)),
              ("proj", (2, C)),
              ("headmask1", (P,)),
              ("Wg1", (E,)), ("Wexp", (E, C)),
              ("Win", (256,)),
              ("bin", (2,)), ("bpa", (1,)), ("dwb2", (2,)),
              ("pwT0", (64,)), ("pwb0", (1,)), ("pwT1", (P,)), ("pwb1", (1,)), ("Wout", (C,)), ("bout", (C,)),
              ("posw", (4,)),
              ("Wqkv2", (3, C)), ("bqk", (2,)), ("bv", (C,)), ("headmask2", (HEADS,)), ("Wo", (C,)), ("bo", (C,)),
              ("Whad", (P,)), ("Wg3", (E,)), ("Wgate", (5, P)), ("Wup", (5, P)), ("Wdown", (5, C))],
}
LN_EPS = [1e-6, 1e-5] * 4
NEG = -3.0e38


def metaformer(nc, a, stop=99):
    F32 = mybir.dt.float32
    BF16 = mybir.dt.bfloat16
    ALU = mybir.AluOpType
    ACT = mybir.ActivationFunctionType
    AX = mybir.AxisListType

    ctx = ExitStack()
    with ctx:
        def sb(name, shape, dt=F32):
            return ctx.enter_context(nc.sbuf_tensor(name, shape, dt))

        def S(name):
            return ctx.enter_context(nc.semaphore(name))

        M = [ctx.enter_context(nc.psum_tensor(f"M{i}", [P, 512], F32)) for i in range(6)]
        TR = [ctx.enter_context(nc.psum_tensor(f"TR{i}", [P, 512], F32)) for i in range(2)]

        W = {}
        packs = {}
        for pack, parts in PACKS.items():
            packs[pack] = sb("w_" + pack, [P, sum(int(np.prod(shape)) for _, shape in parts)])
            o = 0
            for name, shape in parts:
                n = int(np.prod(shape))
                W[name] = packs[pack][:, o:o + n]
                if len(shape) == 2:
                    W[name] = W[name].rearrange("p (a b) -> p a b", a=shape[0])
                if len(shape) == 3:
                    W[name] = W[name].rearrange("p (a b c) -> p a b c", a=shape[0], b=shape[1])
                o += n
        ident, taps, conv_bias = W["ident"], W["taps"], W["conv_bias"]
        pick, Wg0, b1, W1, W2 = W["pick"], W["Wg0"], W["b1"], W["W1"], W["W2"]
        Wqkv1, dw1, pw1T, proj, headmask1 = W["Wqkv1"], W["dw1"], W["pw1T"], W["proj"], W["headmask1"]
        bn, ins, modw, exp_bT = W["bn"], W["ins"], W["modw"], W["exp_bT"]
        Wg1, Wexp = W["Wg1"], W["Wexp"]
        Win, bin_, bpa, dw2, dwb2 = W["Win"], W["bin"], W["bpa"], W["dw2"], W["dwb2"]
        pwT0, pwb0, pwT1, pwb1, Wout, bout = (W[n] for n in ("pwT0", "pwb0", "pwT1", "pwb1", "Wout", "bout"))
        posw, Wqkv2, bqk, bv, headmask2 = W["posw"], W["Wqkv2"], W["bqk"], W["bv"], W["headmask2"]
        Wo, bo, Whad, Wg3 = W["Wo"], W["bo"], W["Whad"], W["Wg3"]
        Wgate, Wup, Wdown = W["Wgate"], W["Wup"], W["Wdown"]
        b2T = W["b2T"]

        ones = sb("ones", [P, P])
        mhalf = sb("mhalf", [P, TILES])
        phalf = sb("phalf", [P, 2])
        upw = sb("upw", [P, len(UP_PARTS), PM])
        downw = sb("downw", [P, len(DOWN_PARTS), P])
        filt = sb("filt", [P, N_UP + N_DN])
        upA = filt[:, 0:2 * UP].rearrange("p (h y) -> p h y", h=2)
        upB = filt[:, 2 * UP:N_UP]
        dnA = filt[:, N_UP:N_UP + 8 * len(DOWN_PARTS)].rearrange("p (k j) -> p k j", j=8)
        dnB = filt[:, N_UP + 8 * len(DOWN_PARTS):N_UP + N_DN]
        w5 = sb("w5", [P, 3, L1_PE, P])
        w7 = sb("w7", [P, 2, L2_PE, P])
        bncol = sb("bncol", [P, 4])
        bndiag = sb("bndiag", [P, 2, P])
        bnrow = sb("bnrow", [P, 2, C])
        inssum = sb("inssum", [P, 1])
        modr = sb("modr", [16, 16])
        sixteenth = sb("sixteenth", [16, P])
        modb = sb("modb", [P, 16])
        btd = sb("btd", [P, E])
        bt = sb("bt", [E, C])

        X = [sb(f"X{s}", [P, TILES, C]) for s in range(SLOTS)]
        XT = [sb(f"XT{s}", [P, TILES, C]) for s in range(SLOTS)]
        XN = [sb(f"XN{s}", [P, N]) for s in range(SLOTS)]
        XC = [XN[s][:].rearrange("p (b n) -> p b n", b=IMGS) for s in range(SLOTS)]
        lnst = [sb(f"lnst{s}", [P, TILES, 6]) for s in range(SLOTS)]
        lnmv = [sb(f"lnmv{s}", [P, TILES, 2]) for s in range(SLOTS)]
        lnve = [sb(f"lnve{s}", [P, TILES]) for s in range(SLOTS)]
        lnrs = [sb(f"lnrs{s}", [P, TILES]) for s in range(SLOTS)]
        rt = [sb(f"rt{s}", [P, 8, TILES, E]) for s in range(SLOTS)]
        rs1 = [sb(f"rs1{s}", [P, 8, TILES]) for s in range(SLOTS)]
        comb = [sb(f"comb{s}", [P, TILES, E]) for s in range(SLOTS)]
        combT = [sb(f"combT{s}", [E, N]) for s in range(SLOTS)]

        ARENA = 70 * 256 + 192
        arena = sb("arena", [P, ARENA])
        at_ = [0]
        def piece(n, shape_str=None, **kw):
            o = at_[0]
            at_[0] += n
            assert at_[0] <= ARENA, at_[0]
            v = arena[:, o:o + n]
            return v.rearrange(shape_str, **kw) if shape_str else v
        Y = [piece(M_UP * 256, "p (m n) -> p m n", m=M_UP) for s in range(SLOTS)]
        Z = [piece(512) for _ in range(3)]
        Zb = [piece(512) for _ in range(3)]
        picked = arena[:, 0:TAPS * (N_UP + N_DN)]
        beta_w = arena[:, 12288:12288 + E * C].rearrange("p (e c) -> p e c", e=E)
        at_[0] = 0
        H = [[piece(512) for _ in range(4)] for _ in range(2)]
        CB = [piece(E * N, "p (e n) -> p e n", e=E) for _ in range(SLOTS)]
        YS = [piece(512) for _ in range(2)]
        at_[0] = 0
        at_[0] = ARENA - SLOTS * 3 * IMGS * L1_W * L1_W
        P5 = [[piece(IMGS * L1_W * L1_W, "p (b y x) -> p b y x", b=IMGS, y=L1_W) for _ in range(3)]
              for _ in range(SLOTS)]
        at_[0] = 0
        A5 = [piece(512, "p (b y x) -> p b y x", b=IMGS, y=SIDE) for _ in range(2)]
        AP5 = [piece(512) for _ in range(2)]
        PROD5 = [piece(512) for _ in range(RING)]
        Q1 = [piece(512) for _ in range(SLOTS)]
        Q2 = [piece(512) for _ in range(SLOTS)]
        KVC = [[piece(512) for _ in range(2)] for _ in range(SLOTS)]
        KV = [[piece(TILES * 260, "p (t c) -> p t c", t=TILES) for _ in range(2)] for _ in range(SLOTS)]
        KM = [piece(2 * IMGS * 144, "p (g j c) -> p g j c", g=2, j=IMGS) for _ in range(SLOTS)]
        end_c = at_[0]
        OTk = [[P5[s][g].rearrange("p b y x -> p (b y x)")[:, 0:512] for g in range(2)] for s in range(SLOTS)]
        OC = [[KVC[s][g] for g in range(2)] for s in range(SLOTS)]
        DEN = [sb(f"DEN{s}", [P, 4, 16 * 2]) for s in range(SLOTS)]
        at_[0] = 0
        P7 = [[piece(IMGS * L2_W * L2_W, "p (b y x) -> p b y x", b=IMGS, y=L2_W) for _ in range(2)]
              for _ in range(SLOTS)]
        A7 = [piece(512, "p (b y x) -> p b y x", b=IMGS, y=SIDE) for _ in range(2)]
        AP7 = [piece(512) for _ in range(2)]
        PROD7 = [piece(512) for _ in range(RING)]
        PA = [piece(512) for _ in range(SLOTS)]
        D7 = [[piece(512) for _ in range(2)] for _ in range(SLOTS)]
        G0 = [piece(512) for _ in range(SLOTS)]
        G1 = [piece(512) for _ in range(SLOTS)]
        G2 = [piece(512) for _ in range(SLOTS)]
        at_[0] = 0
        XP = piece(512)
        Qc = [piece(512) for _ in range(SLOTS)]
        Kc = [piece(512) for _ in range(SLOTS)]
        Vh = [piece(TILES * HEADS * 32, "p (t h c) -> p t h c", t=TILES, h=HEADS) for _ in range(SLOTS)]
        QM = [piece(512) for _ in range(3)]
        LG = [piece(512) for _ in range(3)]
        REP = [piece(512) for _ in range(2)]
        E1 = [piece(512) for _ in range(2)]
        E2 = [piece(512) for _ in range(2)]
        PR = [piece(512) for _ in range(2)]
        PT = [piece(512) for _ in range(5)]
        PO = [piece(512) for _ in range(2)]
        OT = [XT[s][:].rearrange("p t (h d) -> p t h d", h=HEADS) for s in range(SLOTS)]
        OCf = [XN[s][:] for s in range(SLOTS)]
        UNITS = SLOTS * HEADS * IMGS
        top8 = [sb(f"top8_{i}", [P, 2, 16]) for i in range(4)]
        nmx = [sb(f"nmx{i}", [P, 2]) for i in range(4)]
        rdn = sb("rdn", [P, 2, TILES, 4])
        at_[0] = 0
        HS = [piece(512) for _ in range(SLOTS)]
        HQ = [piece(512) for _ in range(SLOTS)]
        H1 = [piece(512) for _ in range(SLOTS)]
        H2 = [piece(512) for _ in range(SLOTS)]
        H3 = [piece(512) for _ in range(SLOTS)]
        hst = [sb(f"hst{s}", [P, 9, IMGS]) for s in range(SLOTS)]
        at_[0] = 0
        SG = [piece(512) for _ in range(2)]
        GU = [[piece(512) for _ in range(5)] for _ in range(SLOTS)]
        CBP = [piece(4 * N, "p (i n) -> p i n", i=4) for _ in range(SLOTS)]
        comb_dram = [nc.dram_tensor(f"comb_rows{s}", (E, N), F32, kind="Internal").ap() for s in range(SLOTS)]

        first_in = S("first_in")
        beta_in = S("beta_in")
        stage1_in = S("stage1_in")
        later_in = S("later_in")
        consts = S("consts")
        dve_setup = S("dve_setup")
        pe_setup = S("pe_setup")
        act_setup = S("act_setup")
        taps_ready = S("taps_ready")
        pool_setup = S("pool_setup")
        setup_done = S("setup_done")
        dve_step = S("dve_step")
        act_step = S("act_step")
        pool_step = S("pool_step")
        pass_end = S("pass_end")
        pass_go = {n: S("go_" + n) for n in ("pe", "act", "dve", "pool")}
        borders5 = S("borders5")
        borders7 = S("borders7")
        tap_mats = S("tap_mats")
        v_ones = S("v_ones")
        lg_copied = S("lg_copied")
        x_loaded = [S(f"x_loaded{s}") for s in range(SLOTS)]
        x_turned = S("x_turned")
        x_in = S("x_in")
        ln_var = S("ln_var")
        ln_rstd = S("ln_rstd")
        xt_ready = S("xt_ready")
        xt_turned = S("xt_turned")
        xn_ready = S("xn_ready")
        up_done = S("up_done")
        up_biased = S("up_biased")
        up_leaky = S("up_leaky")
        up_gained = S("up_gained")
        up_clipped = S("up_clipped")
        down_done = S("down_done")
        x_after_conv = S("x_after_conv")
        logits_done = S("logits_done")
        router_shifted = S("router_shifted")
        router_exp = S("router_exp")
        comb_ready = S("comb_ready")
        comb_turned = S("comb_turned")
        combT_ready = S("combT_ready")
        ffn_up_done = S("ffn_up_done")
        ffn_gelu_done = S("ffn_gelu_done")
        ffn_down_done = S("ffn_down_done")
        ffn_scaled = S("ffn_scaled")
        ffn_turned = S("ffn_turned")
        x_after_ffn = S("x_after_ffn")
        comb_stored = [S(f"comb_stored{s}") for s in range(SLOTS)]
        comb_rows = [S(f"comb_rows{s}") for s in range(SLOTS)]
        ffn_added = S("ffn_added")
        qkv_done = S("qkv_done")
        qkv_padded = S("qkv_padded")
        kvpx_done = S("kvpx_done")
        kvpx_k = S("kvpx_k")
        kvpx_v = S("kvpx_v")
        dw5_first = S("dw5_first")
        dw5_prod = S("dw5_prod")
        dw5_padd = S("dw5_padd")
        dw7_first = S("dw7_first")
        dw7_prod = S("dw7_prod")
        dw7_padd = S("dw7_padd")
        dw5_acc = S("dw5_acc")
        dw5_done = S("dw5_done")
        dw5_out = S("dw5_out")
        agg_turned = S("agg_turned")
        agg_px = S("agg_px")
        kv_done = S("kv_done")
        kv_masked = S("kv_masked")
        num_done = S("num_done")
        num_scaled = S("num_scaled")
        o_turned = S("o_turned")
        o_ready = S("o_ready")
        proj_done = S("proj_done")
        x_shifted = S("x_shifted")
        x_added = S("x_added")
        eo_done = S("eo_done")
        eo_added = S("eo_added")
        eb_done = S("eb_done")
        fused_done = S("fused_done")
        fused_padded = S("fused_padded")
        dw7_acc = S("dw7_acc")
        dw7_done = S("dw7_done")
        dw7_out = S("dw7_out")
        g0_ready = S("g0_ready")
        pw0_done = S("pw0_done")
        g1_ready = S("g1_ready")
        pw1_done = S("pw1_done")
        g2_ready = S("g2_ready")
        out2_done = S("out2_done")
        x_after_l2 = S("x_after_l2")
        xp_ready = S("xp_ready")
        qk_done = S("qk_done")
        qk_ready = S("qk_ready")
        v_ready = S("v_ready")
        qm_ready = S("qm_ready")
        lg_done = S("lg_done")
        lg_max = S("lg_max")
        lg_exp = S("lg_exp")
        rep_ready = S("rep_ready")
        rep_exp = S("rep_exp")
        pr_ready = S("pr_ready")
        pt_done = S("pt_done")
        pt_ready = S("pt_ready")
        pv_done = S("pv_done")
        po_ready = S("po_ready")
        po_turned = S("po_turned")
        ot_ready = S("ot_ready")
        ot_turned = S("ot_turned")
        oc_ready = S("oc_ready")
        wo_done = S("wo_done")
        x_after_attn = S("x_after_attn")
        had_done = S("had_done")
        had_copied = S("had_copied")
        had_sq = S("had_sq")
        ss_done = S("ss_done")
        ms_ready = S("ms_ready")
        std_ready = S("std_ready")
        x_after_had = S("x_after_had")
        gate_done = S("gate_done")
        upp_done = S("upp_done")
        silu_done = S("silu_done")
        gu_ready = S("gu_ready")
        gus_pool = S("gus_pool")
        gus_ready = S("gus_ready")
        moe_done = S("moe_done")
        x_final = S("x_final")
        xf_turned = S("xf_turned")
        xf_ready = S("xf_ready")
        stored = S("stored")

        pass_sems = range(borders5.num, stored.num + 1)

        def next_pass(eng, name):
            eng.drain().then_inc(pass_end, 1)
            eng.wait_ge(pass_go[name], 1)
            eng.sem_clear(pass_go[name])
        block = ctx.enter_context(nc.Block())

        def ln_index(n, s):
            return 2 * n + s + 1

        @block.sync
        def _(sp):
            sp.dma_start(packs["first"][:], a["first"]).then_inc(first_in, 16)
            sp.dma_start(beta_w, a["beta_w"]).then_inc(beta_in, 16)
            with sp.Fori(0, PASSES) as p:
                for s in range(SLOTS):
                    src = a["x"][:, bass.ds((p * SLOTS + s) * IMGS, IMGS), :]
                    sp.dma_start(XC[s], src).then_inc(x_loaded[s], 16)
                if stop >= 1:
                    for s in range(SLOTS):
                        sp.wait_ge(combT_ready, s + 1)
                        sp.dma_start(comb_dram[s], combT[s][:]).then_inc(comb_stored[s], 16)
                        sp.wait_ge(comb_stored[s], 16)
                        sp.dma_start(CB[s], comb_dram[s].partition_broadcast(P)).then_inc(comb_rows[s], 16)
                if stop >= 7:
                    for s in range(SLOTS):
                        sp.wait_ge(combT_ready, 5 + s)
                        sp.dma_start(comb_dram[s], combT[s][:]).then_inc(comb_stored[s], 16)
                        sp.wait_ge(comb_stored[s], 32)
                        for d in range(2):
                            src = comb_dram[s].rearrange("(i d) n -> d i n", d=2)[d]
                            sp.dma_start(CBP[s][64 * d:64 * d + 64], src.partition_broadcast(64))\
                              .then_inc(comb_rows[s], 16)
                for s in range(SLOTS):
                    sp.wait_ge(xf_ready, s + 1)
                    dst = a["out"][:, bass.ds((p * SLOTS + s) * IMGS, IMGS), :]
                    sp.dma_start(dst, XC[s]).then_inc(stored, 16)
                sp.wait_ge(stored, 32)
                sp.wait_ge(pass_end, 4)
                sp.sem_clear(pass_sems)
                sp.sem_clear(pass_end)
                for g in pass_go.values():
                    sp.sem_inc(g, 1)

        @block.gpsimd
        def _(pool):
            def link(ins):
                steps[0] += 1
                ins.then_inc(pool_step, 1)
                pool.wait_ge(pool_step, steps[0])
            steps = [0]
            g = nc.gpsimd
            g.memset(ones[:], 1.0).then_inc(consts, 1)
            g.memset(mhalf[:], -0.5).then_inc(consts, 1)
            g.memset(phalf[:], 0.5).then_inc(consts, 1)
            g.memset(sixteenth[:], 1.0 / 16).then_inc(consts, 1)
            pool.wait_ge(first_in, 16)
            link(g.tensor_scalar(bncol[:, 0:1], bn[:, 3:4], 1e-5, None, ALU.add))
            pool.wait_ge(consts, 4)
            link(g.tensor_tensor(bncol[:, 1:2], bncol[:, 0:1], mhalf[:, 0:1], ALU.pow))
            g.tensor_tensor(bncol[:, 2:3], bncol[:, 1:2], bn[:, 0:1], ALU.mult).then_inc(pool_setup, 1)
            pool.wait_ge(dve_setup, 2)
            for i, (m, h) in enumerate(UP_PARTS):
                last = g.tensor_tensor(upw[:, i, :].rearrange("p (r x) -> p r x", r=ROWS_M),
                                       upA[:, h, ROWS_M * m:ROWS_M * m + ROWS_M].unsqueeze(2)
                                       .to_broadcast([P, ROWS_M, UP]),
                                       upB[:].unsqueeze(1).to_broadcast([P, ROWS_M, UP]), ALU.mult)
            last.then_inc(pool_setup, 1)

            def ln_pow(p, n, slots=range(SLOTS)):
                for s in slots:
                    pool.wait_ge(ln_var, ln_index(n, s))
                    g.tensor_tensor(lnrs[s][:], lnve[s][:], mhalf[:], ALU.pow).then_inc(ln_rstd, 1)

            def new_steps():
                if steps[0]:
                    pool.wait_ge(pool_step, steps[0])
                pool.sem_clear(pool_step)
                steps[0] = 0

            new_steps()
            with pool.Fori(0, PASSES) as p:
                ln_pow(p, 0)
                if stop >= 1:
                    ln_pow(p, 1)
                    for i in range(3):
                        for t in range(L1_PE):
                            o = L1_TAPS - L1_PE + t
                            last = g.tensor_scalar(w5[:, i, t, :], pw1T[:, i, :], dw1[:, i, o:o + 1],
                                                   None, ALU.mult)
                    last.then_inc(tap_mats, 1)
                    for i in range(2):
                        for t in range(L2_PE):
                            o = L2_TAPS - L2_PE + t
                            last = g.tensor_scalar(w7[:, i, t, :], ident[:], dw2[:, i, o:o + 1],
                                                   None, ALU.mult)
                    last.then_inc(tap_mats, 1)
                if stop >= 2:
                    for s in range(SLOTS):
                        for i in range(3):
                            g.memset(P5[s][i][:], 0.0)
                    ln_pow(p, 2, [0])
                    pool.wait_ge(ffn_added, 2)
                    for s in range(SLOTS):
                        for gg in range(2):
                            last = g.memset(KV[s][gg][:, :, 256:257], 1.0)
                    last.then_inc(borders5, 1)
                    ln_pow(p, 2, [1])
                    pool.wait_ge(later_in, 16)
                    pool.wait_ge(act_setup, 4)
                    for s in range(SLOTS):
                        pool.wait_ge(xt_ready, ln_index(2, s))
                        for t in range(TILES):
                            last = g.tensor_tensor(X[s][:, t, :], X[s][:, t, :], bnrow[:, 1, :], ALU.add)
                        last.then_inc(x_shifted, 1)
                    for k in range(6):
                        pool.wait_ge(dw5_first, k + 1)
                        for t in range(L1_POOL - 1):
                            n = (L1_POOL - 1) * k + t + 1
                            pool.wait_ge(dw5_prod, n)
                            if t > 0:
                                pool.wait_ge(dw5_padd, n - 1)
                            g.tensor_tensor(AP5[k % 2], AP5[k % 2], PROD5[n % RING], ALU.add)\
                             .then_inc(dw5_padd, 1)
                if stop >= 3:
                    ln_pow(p, 3)
                if stop >= 4:
                    ln_pow(p, 4)
                    pool.wait_ge(x_added, 2)
                    for s in range(SLOTS):
                        for i in range(2):
                            last = g.memset(P7[s][i][:], 0.0)
                    last.then_inc(borders7, 1)
                    for k in range(4):
                        pool.wait_ge(dw7_first, k + 1)
                        m = P if k % 2 == 1 else 96
                        for t in range(L2_POOL - 1):
                            n = (L2_POOL - 1) * k + t + 1
                            pool.wait_ge(dw7_prod, n)
                            if t > 0:
                                pool.wait_ge(dw7_padd, n - 1)
                            g.tensor_tensor(AP7[k % 2][0:m], AP7[k % 2][0:m], PROD7[n % RING][0:m], ALU.add)\
                             .then_inc(dw7_padd, 1)
                if stop >= 5:
                    ln_pow(p, 5)
                    for s in range(SLOTS):
                        pool.wait_ge(xt_ready, ln_index(5, s))
                        for t in range(TILES):
                            last = g.tensor_tensor(X[s][:, t, :], X[s][:, t, :], bo[:], ALU.add)
                        last.then_inc(x_shifted, 1)
                    pool.wait_ge(x_after_l2, 2)
                    for s in range(SLOTS):
                        link(g.memset(Vh[s], 0.0))
                        last = g.memset(Vh[s][:, :, :, HD:HD + 1], 1.0)
                    last.then_inc(v_ones, 1)

                    def mask_queries(hh):
                        s, h = divmod(hh, HEADS)
                        if h == 0:
                            pool.wait_ge(qk_ready, 2 * s + 1)
                        if hh >= 3:
                            pool.wait_ge(lg_done, 2 * (hh - 3) + 2)
                        g.tensor_scalar(QM[hh % 3], Qc[s], headmask2[:, h:h + 1], float(C) ** -0.5,
                                        ALU.mult, ALU.mult).then_inc(qm_ready, 1)
                    mask_queries(0)
                    mask_queries(1)
                    for c in range(UNITS):
                        if c % 2 == 0 and c // 2 + 2 < SLOTS * HEADS:
                            mask_queries(c // 2 + 2)
                        pool.wait_ge(rep_exp, c + 1)
                        if c >= 2:
                            pool.wait_ge(pt_done, c - 1)
                        g.tensor_tensor(PR[c % 2], E1[c % 2], E2[c % 2], ALU.subtract).then_inc(pr_ready, 1)
                        if c == 27 and stop >= 6:
                            ln_pow(p, 6, [0])
                    if stop >= 6:
                        ln_pow(p, 6, [1])
                if stop >= 6:
                    for s in range(SLOTS):
                        pool.wait_ge(ms_ready, s + 1)
                        g.tensor_tensor(hst[s][:, 2, :], hst[s][:, 1, :], phalf[:], ALU.pow)\
                         .then_inc(std_ready, 1)
                if stop >= 7:
                    ln_pow(p, 7)
                    for s in range(SLOTS):
                        pool.wait_ge(comb_rows[s], 48)
                        for i in range(2):
                            pool.wait_ge(gu_ready, 5 * s + i + 1)
                            g.tensor_tensor(GU[s][i], GU[s][i], CBP[s][:, i, :], ALU.mult).then_inc(gus_pool, 1)
                new_steps()
                next_pass(pool, "pool")

        @block.scalar
        def _(act):
            A = nc.scalar.activation
            pool_base = 0
            act.wait_ge(first_in, 16)
            nc.scalar.dma_start(packs["stage1"][:], a["stage1"]).then_inc(stage1_in, 16)
            nc.scalar.dma_start(packs["later"][:], a["later"]).then_inc(later_in, 16)
            act.wait_ge(pe_setup, 1)
            A(modr[:], TR[0][0:16, 0:16], ACT.Copy).then_inc(act_setup, 1)
            act.wait_ge(pe_setup, 2)
            A(modb[:], TR[1][:, 0:16], ACT.Copy).then_inc(act_setup, 1)
            act.wait_ge(pe_setup, 5)
            A(bnrow[:].rearrange("p g c -> p (g c)"), M[0][:, 0:256], ACT.Copy).then_inc(act_setup, 1)
            A(bt[:], M[1][0:E, 0:C], ACT.Copy).then_inc(act_setup, 1)
            def ln_copy(p, n, s):
                act.wait_ge(xt_turned, ln_index(n, s) - 2)
                A(XN[s][:], TR[s][:], ACT.Copy).then_inc(xn_ready, 1)

            def router_act(p, r, s):
                act.wait_ge(router_shifted, 2 * r + s + 1)
                A(rt[s][:, 1], rt[s][:, 0], ACT.Exp).then_inc(router_exp, 1)

            def comb_copy(p, r, s):
                act.wait_ge(comb_turned, 2 * r + s + 1)
                A(combT[s][:], TR[s][0:E, :], ACT.Copy).then_inc(combT_ready, 1)

            with act.Fori(0, PASSES) as p:
                for s in range(SLOTS):
                    act.wait_ge(x_turned, s + 1)
                    A(X[s][:].rearrange("p t c -> p (t c)"), TR[s][:], ACT.Copy).then_inc(x_in, 1)
                for s in range(SLOTS):
                    for m in range(7):
                        c = 7 * s + m
                        act.wait_ge(up_leaky, c + 1)
                        if c >= 3:
                            act.wait_ge(up_clipped, c - 2)
                        A(Zb[c % 3][0:PM, :], Z[c % 3][0:PM, :], ACT.Copy, scale=float(np.sqrt(2.0)))\
                            .then_inc(up_gained, 1)
                if stop >= 1:
                    act.wait_ge(stage1_in, 16)
                    for s in range(SLOTS):
                        ln_copy(p, 1, s)
                    for s in range(SLOTS):
                        router_act(p, 0, s)
                    for c in range(SLOTS * E * 4):
                        d = c // 4
                        act.wait_ge(ffn_up_done, c + 1)
                        if d >= 2:
                            act.wait_ge(ffn_down_done, d - 1)
                        A(H[d % 2][c % 4], M[c % 3][:], ACT.Gelu, bias=b1[:, c % 32:c % 32 + 1])\
                            .then_inc(ffn_gelu_done, 1)
                        if c == 7:
                            for s in range(SLOTS):
                                comb_copy(p, 0, s)
                if stop >= 2:
                    act.wait_ge(later_in, 16)
                    act.wait_ge(borders5, 1)
                    for s in range(SLOTS):
                        ln_copy(p, 2, s)
                    for s in range(SLOTS):
                        for i in range(3):
                            k = 3 * s + i + 1
                            act.wait_ge(qkv_done, k)
                            if i == 0:
                                A(Q1[s], M[0][:], ACT.Relu)
                            A(P5[s][i][:, :, L1_PAD:L1_PAD + SIDE, L1_PAD:L1_PAD + SIDE],
                              M[i][:].rearrange("p (b y x) -> p b y x", b=IMGS, y=SIDE),
                              ACT.Copy).then_inc(qkv_padded, 1)
                        for h in range(2):
                            act.wait_ge(kvpx_done, 2 * s + h + 1)
                            src = M[3 + h][:].rearrange("p (t c) -> p t c", t=2)
                            A(KV[s][0][:, 2 * h:2 * h + 2, 0:128], src[:, :, 0:128], ACT.Relu)\
                                .then_inc(kvpx_k, 1)
                            A(KV[s][0][:, 2 * h:2 * h + 2, 128:256], src[:, :, 128:256], ACT.Copy)\
                                .then_inc(kvpx_v, 1)
                    def products5(k):
                        s, i = divmod(k, 3)
                        for t in range(L1_POOL):
                            dy, dx = divmod(L1_DVE + t, 5)
                            win = P5[s][i][:, :, dy:dy + SIDE, dx:dx + SIDE]
                            col = dw1[:, i, L1_DVE + t:L1_DVE + t + 1]
                            if t == 0:
                                if k >= 2:
                                    act.wait_ge(dw5_acc, k - 1)
                                A(AP5[k % 2].rearrange("p (b y x) -> p b y x", b=IMGS, y=SIDE), win,
                                  ACT.Copy, scale=col).then_inc(dw5_first, 1)
                            else:
                                n = (L1_POOL - 1) * k + t
                                if n > RING:
                                    act.wait_ge(dw5_padd, n - RING)
                                A(PROD5[n % RING].rearrange("p (b y x) -> p b y x", b=IMGS, y=SIDE), win,
                                  ACT.Copy, scale=col).then_inc(dw5_prod, 1)
                    act.wait_ge(qkv_padded, 6)
                    for k in range(7):
                        if k < 6:
                            products5(k)
                        if k > 0:
                            act.wait_ge(dw5_done, k)
                            s, i = divmod(k - 1, 3)
                            dst = [Q2[s], KVC[s][0], KVC[s][1]][i]
                            A(dst, M[[5, 0, 1][i]][:], ACT.Copy if i == 2 else ACT.Relu).then_inc(dw5_out, 1)
                    for s in range(SLOTS):
                        for g in range(2):
                            act.wait_ge(agg_turned, 2 * s + g + 1)
                            A(KV[s][1][:, :, 128 * g:128 * g + 128],
                              M[2 + g][:].rearrange("p (t c) -> p t c", t=TILES), ACT.Copy)\
                                .then_inc(agg_px, 1)
                    for s in range(SLOTS):
                        for g in range(2):
                            act.wait_ge(o_turned, 2 * s + g + 1)
                            A(OC[s][g], M[4 + g][:], ACT.Copy).then_inc(o_ready, 1)
                if stop >= 3:
                    for s in range(SLOTS):
                        ln_copy(p, 3, s)
                    for s in range(SLOTS):
                        router_act(p, 1, s)
                    for s in range(SLOTS):
                        comb_copy(p, 1, s)
                if stop >= 4:
                    act.wait_ge(borders7, 1)
                    for s in range(SLOTS):
                        ln_copy(p, 4, s)
                    for s in range(SLOTS):
                        for i in range(2):
                            act.wait_ge(fused_done, 3 * s + i + 1)
                            n = P if i == 0 else 96
                            A(P7[s][i][0:n, :, L2_PAD:L2_PAD + SIDE, L2_PAD:L2_PAD + SIDE],
                              M[4 + i][0:n, :].rearrange("p (b y x) -> p b y x", b=IMGS, y=SIDE),
                              ACT.Identity, bias=bin_[0:n, i:i + 1]).then_inc(fused_padded, 1)
                        act.wait_ge(fused_done, 3 * s + 3)
                        A(PA[s][64:96, :], M[3][64:96, :], ACT.Identity, bias=bpa[64:96, :])\
                            .then_inc(fused_padded, 1)
                    def products7(k):
                        s, i = divmod(k, 2)
                        m = P if i == 1 else 96
                        for t in range(L2_POOL):
                            dy, dx = divmod(L2_DVE + t, 7)
                            win = P7[s][1 - i][0:m, :, dy:dy + SIDE, dx:dx + SIDE]
                            col = dw2[0:m, 1 - i, L2_DVE + t:L2_DVE + t + 1]
                            if t == 0:
                                if k >= 2:
                                    act.wait_ge(dw7_acc, k - 1)
                                A(AP7[k % 2][0:m].rearrange("p (b y x) -> p b y x", b=IMGS, y=SIDE), win,
                                  ACT.Copy, scale=col).then_inc(dw7_first, 1)
                            else:
                                n = (L2_POOL - 1) * k + t
                                if n > RING:
                                    act.wait_ge(dw7_padd, n - RING)
                                A(PROD7[n % RING][0:m].rearrange("p (b y x) -> p b y x", b=IMGS, y=SIDE), win,
                                  ACT.Copy, scale=col).then_inc(dw7_prod, 1)
                    act.wait_ge(fused_padded, 6)
                    for k in range(5):
                        if k < 4:
                            products7(k)
                        if k > 0:
                            act.wait_ge(dw7_done, k)
                            s, i = divmod(k - 1, 2)
                            n = P if i == 1 else 96
                            A(D7[s][i][0:n, :], M[i][0:n, :], ACT.Identity, bias=dwb2[0:n, 1 - i:2 - i])\
                                .then_inc(dw7_out, 1)
                if stop >= 5:
                    for s in range(SLOTS):
                        ln_copy(p, 5, s)

                    def project_copy(s, i):
                        act.wait_ge(qk_done, 3 * s + i + 1)
                        A([Qc, Kc][i][s], M[2][:], ACT.Identity, bias=bqk[:, i:i + 1]).then_inc(qk_ready, 1)

                    def lg_copy(c):
                        act.wait_ge(lg_done, c + 1)
                        if c >= 3:
                            act.wait_ge(rep_ready, c - 2)
                        A(LG[c % 3], M[c % 2][:], ACT.Copy).then_inc(lg_copied, 1)

                    def pt_copy(c):
                        act.wait_ge(pt_done, c + 1)
                        if c >= 5:
                            act.wait_ge(pv_done, (c - 5) // 4 + 1)
                        A(PT[c % 5], M[3 + c % 2][:], ACT.Copy).then_inc(pt_ready, 1)

                    def po_copy(s, g):
                        act.wait_ge(pv_done, 4 * s + 2 * g + 2)
                        if s == 1:
                            act.wait_ge(po_turned, g + 1)
                        A(PO[g], [M[5], TR[s]][g][:], ACT.Copy).then_inc(po_ready, 1)

                    def oc_copy(s):
                        act.wait_ge(ot_turned, s + 1)
                        A(OCf[s], M[2][:], ACT.Copy).then_inc(oc_ready, 1)
                    project_copy(0, 0)
                    project_copy(0, 1)
                    lg_copy(0)
                    for c in range(UNITS):
                        if c + 1 < UNITS:
                            lg_copy(c + 1)
                        act.wait_ge(lg_max, c + 1)
                        if c >= 2:
                            act.wait_ge(pr_ready, c - 1)
                        for q in range(2):
                            A(E1[c % 2][:, q * 256:q * 256 + 256], LG[c % 3][:, q * 256:q * 256 + 256],
                              ACT.Exp, bias=nmx[c % 4][:, q:q + 1])
                        act.wait_ge(rep_ready, c + 1)
                        for q in range(2):
                            last = A(E2[c % 2][:, q * 256:q * 256 + 256], REP[c % 2][:, q * 256:q * 256 + 256],
                                     ACT.Exp, bias=nmx[c % 4][:, q:q + 1])
                        last.then_inc(rep_exp, 1)
                        if c >= 1:
                            pt_copy(c - 1)
                        if c in (8, 9):
                            project_copy(1, c - 8)
                        if c == 9:
                            po_copy(0, 0)
                        if c == 17:
                            po_copy(0, 1)
                        if c == 23:
                            oc_copy(0)
                        if c == 25:
                            po_copy(1, 0)
                    pt_copy(UNITS - 1)
                    po_copy(1, 1)
                    oc_copy(1)
                if stop >= 6:
                    for s in range(SLOTS):
                        ln_copy(p, 6, s)
                    for s in range(SLOTS):
                        act.wait_ge(had_done, s + 1)
                        A(HS[s], M[2 + s][:], ACT.Copy).then_inc(had_copied, 1)
                        for j in range(IMGS):
                            last = A(HQ[s][:, 256 * j:256 * j + 256], M[2 + s][:, 256 * j:256 * j + 256],
                                     ACT.Square, accum_out=hst[s][:, 0, j:j + 1])
                        last.then_inc(had_sq, 1)
                if stop >= 7:
                    for s in range(SLOTS):
                        ln_copy(p, 7, s)
                    for s in range(SLOTS):
                        router_act(p, 2, s)
                    for c in range(10):
                        n = P if c % 5 < 4 else 64
                        act.wait_ge(gate_done, c + 1)
                        if c >= 2:
                            act.wait_ge(gu_ready, c - 1)
                        A(SG[c % 2][0:n, :], M[c % 2][0:n, :], ACT.Silu).then_inc(silu_done, 1)
                        if c == 1:
                            for s in range(SLOTS):
                                comb_copy(p, 2, s)
                for s in range(SLOTS):
                    act.wait_ge(xf_turned, s + 1)
                    A(XC[s].rearrange("p b n -> p (b n)"), TR[s][:], ACT.Copy).then_inc(xf_ready, 1)
                next_pass(act, "act")

        @block.vector
        def _(dve):
            v = nc.vector
            steps = [0]

            def link(ins):
                steps[0] += 1
                ins.then_inc(dve_step, 1)
                dve.wait_ge(dve_step, steps[0])

            def mark(ins):
                steps[0] += 1
                ins.then_inc(dve_step, 1)
                return steps[0]

            def after(k):
                dve.wait_ge(dve_step, k)

            done = [0] * SLOTS

            def begin(s, ins):
                done[s] = mark(ins)

            def in_turn(op):
                for s in range(SLOTS):
                    after(done[s])
                    done[s] = mark(op(s))

            dve.wait_ge(first_in, 16)
            v.tensor_reduce(inssum[:], ins[:], AX.X, ALU.add).then_inc(dve_setup, 1)

            def filters(lo, n, f):
                for t in range(TAPS):
                    k = mark(v.tensor_scalar(picked[:, (lo * TAPS + t * n):(lo * TAPS + t * n + n)],
                                             W["tap_no"][:, lo:lo + n], float(t),
                                             taps[:, f * TAPS + t:f * TAPS + t + 1], ALU.is_equal, ALU.mult))
                after(k)
                dst = filt[:, lo:lo + n]
                return v.tensor_reduce(dst, picked[:, lo * TAPS:(lo + n) * TAPS].rearrange("p (t n) -> p n t", t=TAPS),
                                       AX.X, ALU.add)
            link(filters(0, N_UP, 0))
            v.tensor_scalar(upB, upB, 4.0, None, ALU.mult).then_inc(dve_setup, 1)
            dve.wait_ge(pool_setup, 1)
            link(v.tensor_tensor(bncol[:, 3:4], bn[:, 2:3], bncol[:, 2:3], ALU.mult))
            link(v.tensor_tensor(bncol[:, 0:1], bn[:, 1:2], bncol[:, 3:4], ALU.subtract))
            v.tensor_scalar(bndiag[:, 0, :], ident[:], bncol[:, 2:3], None, ALU.mult)
            v.tensor_scalar(bndiag[:, 1, :], ident[:], bncol[:, 0:1], None, ALU.mult).then_inc(dve_setup, 1)
            dve.wait_ge(pe_setup, 3)
            dve.wait_ge(act_setup, 2)
            link(v.tensor_scalar(btd[:], M[2][:, 0:E], 1.0 / 16, None, ALU.mult))
            link(v.tensor_tensor(exp_bT[:], exp_bT[:], modb[:, 8:16], ALU.mult))
            v.tensor_tensor(btd[:], btd[:], exp_bT[:], ALU.add).then_inc(dve_setup, 1)
            link(filters(N_UP, N_DN, 1))
            for i in range(len(DOWN_PARTS)):
                last = v.tensor_tensor(downw[:, i, :].rearrange("p (j x) -> p j x", j=8),
                                       dnA[:, i, :].unsqueeze(2).to_broadcast([P, 8, SIDE]),
                                       dnB.unsqueeze(1).to_broadcast([P, 8, SIDE]), ALU.mult)
            last.then_inc(dve_setup, 1)

            def ln_stats(n, s):
                for t in range(TILES):
                    k = mark(v.bn_stats(lnst[s][:, t, :], X[s][:, t, :]))
                for t in range(TILES):
                    after(k - TILES + 1 + t)
                    k2 = mark(v.bn_aggr(lnmv[s][:, t, :], lnst[s][:, t, :]))
                after(k2)
                v.tensor_scalar(lnve[s][:], lnmv[s][:, :, 1], LN_EPS[n], None, ALU.add).then_inc(ln_var, 1)

            def ln_apply(n, s):
                dve.wait_ge(ln_rstd, ln_index(n, s))
                for t in range(TILES):
                    last = v.tensor_scalar(XT[s][:, t, :], X[s][:, t, :], lnmv[s][:, t, 0:1], lnrs[s][:, t:t + 1],
                                           ALU.subtract, ALU.mult)
                last.then_inc(xt_ready, 1)

            def layernorm(p, n, s):
                ln_stats(n, s)
                ln_apply(n, s)

            def router(r, gamma=None, renorm=False):
                R = lambda s, i: rt[s][:, i]
                q = lambda s, i: rs1[s][:, i]
                wide = lambda t: t.unsqueeze(2).to_broadcast([P, TILES, E])
                pk = pick[:].unsqueeze(1).to_broadcast([P, TILES, E])
                lg = lambda s: TR[s][:, 0:TILES * E].rearrange("p (t e) -> p t e", t=TILES)
                for s in range(SLOTS):
                    dve.wait_ge(logits_done, 2 * r + s + 1)
                    if gamma is None:
                        first = v.tensor_copy(R(s, 2), lg(s))
                    else:
                        first = v.tensor_tensor(R(s, 2), lg(s), gamma.unsqueeze(1).to_broadcast([P, TILES, E]),
                                                ALU.add)
                    begin(s, first)
                in_turn(lambda s: v.tensor_reduce(q(s, 0), R(s, 2), AX.X, ALU.max))
                for s in range(SLOTS):
                    after(done[s])
                    v.tensor_tensor(R(s, 0), R(s, 2), wide(q(s, 0)), ALU.subtract).then_inc(router_shifted, 1)
                for s in range(SLOTS):
                    dve.wait_ge(router_exp, 2 * r + s + 1)
                    begin(s, v.tensor_reduce(q(s, 1), R(s, 1), AX.X, ALU.add))
                in_turn(lambda s: v.reciprocal(q(s, 2), q(s, 1)))
                in_turn(lambda s: v.tensor_tensor(R(s, 3), R(s, 1), wide(q(s, 2)), ALU.mult))
                for i in range(2):
                    src = 3 if i == 0 else 7
                    in_turn(lambda s: v.tensor_reduce(q(s, 3 + i), R(s, src), AX.X, ALU.max))
                    in_turn(lambda s: v.tensor_tensor(R(s, 4), R(s, src), wide(q(s, 3 + i)), ALU.is_equal))
                    in_turn(lambda s: v.tensor_tensor(R(s, 4), R(s, 4), pk, ALU.mult))
                    in_turn(lambda s: v.tensor_reduce(q(s, 5), R(s, 4), AX.X, ALU.max))
                    in_turn(lambda s: v.tensor_tensor(R(s, 5 + i), R(s, 4), wide(q(s, 5)), ALU.is_equal))
                    if i == 0:
                        in_turn(lambda s: v.scalar_tensor_tensor(R(s, 7), R(s, 5), -2.0, R(s, 3), ALU.mult, ALU.add))
                in_turn(lambda s: v.tensor_tensor(R(s, 5), R(s, 5), R(s, 6), ALU.add))
                if renorm:
                    in_turn(lambda s: v.tensor_tensor(q(s, 6), q(s, 3), q(s, 4), ALU.add))
                    in_turn(lambda s: v.tensor_scalar(q(s, 6), q(s, 6), 1e-6, None, ALU.add))
                    in_turn(lambda s: v.reciprocal(q(s, 7), q(s, 6)))
                    in_turn(lambda s: v.tensor_tensor(R(s, 3), R(s, 3), wide(q(s, 7)), ALU.mult))
                for s in range(SLOTS):
                    after(done[s])
                    v.tensor_tensor(comb[s][:], R(s, 3), R(s, 5), ALU.mult).then_inc(comb_ready, 1)

            def new_steps():
                if steps[0]:
                    after(steps[0])
                dve.sem_clear(dve_step)
                steps[0] = 0

            new_steps()
            with dve.Fori(0, PASSES) as p:
                for s in range(SLOTS):
                    dve.wait_ge(x_in, s + 1)
                    ln_stats(0, s)
                for s in range(SLOTS):
                    ln_apply(0, s)
                for c in range(14 + 2):
                    if c < 14:
                        dve.wait_ge(up_done, c + 1)
                        if c >= 3:
                            dve.wait_ge(up_gained, c - 2)
                        v.tensor_tensor(Z[c % 3][0:PM, :].rearrange("p (k c) -> p k c", k=4),
                                        M[c % 3][0:PM, :].rearrange("p (k c) -> p k c", k=4),
                                        conv_bias[0:PM, :].unsqueeze(1).to_broadcast([PM, 4, C]),
                                        ALU.add).then_inc(up_biased, 1)
                        dve.wait_ge(up_biased, c + 1)
                        v.scalar_tensor_tensor(Z[c % 3][0:PM, :], Z[c % 3][0:PM, :], 0.2, Z[c % 3][0:PM, :],
                                               ALU.mult, ALU.max).then_inc(up_leaky, 1)
                    if c >= 2:
                        s, m = divmod(c - 2, 7)
                        dve.wait_ge(up_gained, c - 1)
                        v.tensor_scalar(Y[s][0:PM, 2 * m:2 * m + 2, :],
                                        Zb[(c - 2) % 3][0:PM, :].rearrange("p (m n) -> p m n", m=2),
                                        256.0, -256.0, ALU.min, ALU.max).then_inc(up_clipped, 1)
                for s in range(SLOTS):
                    dve.wait_ge(down_done, s + 1)
                    xv = X[s][:].rearrange("p (j h) c -> p h j c", h=2)
                    v.tensor_tensor(xv, xv, M[3 + s][:].rearrange("p (h j c) -> p h j c", h=2, j=IMGS),
                                    ALU.add).then_inc(x_after_conv, 1)
                    dve.wait_ge(x_after_conv, s + 1)
                    if stop >= 1:
                        ln_stats(1, s)
                if stop >= 1:
                    for s in range(SLOTS):
                        ln_apply(1, s)
                    dve.wait_ge(stage1_in, 16)
                    router(0, renorm=True)
                    for s in range(SLOTS):
                        acc = XT[s][:].rearrange("p t c -> p (t c)")
                        dve.wait_ge(comb_rows[s], 16)
                        for e in range(E):
                            d = E * s + e
                            dve.wait_ge(ffn_down_done, d + 1)
                            k1 = mark(v.scalar_tensor_tensor(acc if e == 0 else YS[e % 2], M[[3, 5][d % 2]][:],
                                                             b2T[:, e:e + 1], CB[s][:, e, :], ALU.add, ALU.mult))
                            after(k1)
                            v.nop().then_inc(ffn_scaled, 1)
                            if e == E - 1:
                                v.tensor_tensor(acc, acc, YS[e % 2], ALU.add).then_inc(ffn_added, 1)
                            elif e > 0:
                                link(v.tensor_tensor(acc, acc, YS[e % 2], ALU.add))
                        dve.wait_ge(ffn_turned, s + 1)
                        xf = X[s][:].rearrange("p t c -> p (t c)")
                        v.tensor_tensor(xf, xf, TR[s][:], ALU.add).then_inc(x_after_ffn, 1)
                        if stop >= 2:
                            dve.wait_ge(x_after_ffn, s + 1)
                            ln_stats(2, s)
                    for s in range(SLOTS):
                        if stop >= 2:
                            ln_apply(2, s)
                if stop >= 2:
                    dve.wait_ge(later_in, 16)
                    dve.wait_ge(act_setup, 4)
                    for s in range(SLOTS):
                        for i in range(3):
                            k = 3 * s + i + 1
                            dve.wait_ge(qkv_padded, k)
                            if k > 2:
                                dve.wait_ge(dw5_done, k - 2)
                            for t in range(L1_DVE):
                                dy, dx = divmod(t, 5)
                                for b in range(IMGS):
                                    win = P5[s][i][:, b, dy:dy + SIDE, dx:dx + SIDE]
                                    acc = A5[k % 2][:, b]
                                    if t == 0:
                                        kk = mark(v.tensor_scalar(acc, win, dw1[:, i, 0:1], None, ALU.mult))
                                    else:
                                        after(kk - 1)
                                        ins_ = v.scalar_tensor_tensor(acc, win, dw1[:, i, t:t + 1], acc,
                                                                      ALU.mult, ALU.add)
                                        kk = mark(ins_)
                            after(kk)
                            dve.wait_ge(dw5_padd, (L1_POOL - 1) * k)
                            af = A5[k % 2].rearrange("p b y x -> p (b y x)")
                            v.tensor_tensor(af, af, AP5[(k - 1) % 2], ALU.add).then_inc(dw5_acc, 1)
                    for s in range(SLOTS):
                        for g in range(2):
                            dve.wait_ge(kv_done, 2 * s + g + 1)
                            for j in range(IMGS):
                                v.tensor_tensor(KM[s][:, g, j, 0:128], M[4 + g][:, 129 * j:129 * j + 128],
                                                headmask1[:], ALU.mult)
                                last = v.tensor_scalar(KM[s][:, g, j, 128:144],
                                                       headmask1[:, 0:128:8], M[4 + g][:, 129 * j + 128:129 * j + 129],
                                                       None, ALU.mult)
                            last.then_inc(kv_masked, 1)
                    for s in range(SLOTS):
                        for i in range(4):
                            g, h = divmod(i, 2)
                            dve.wait_ge(num_done, 4 * s + i + 1)
                            src = M[i][:, 0:288].rearrange("p (t c) -> p t c", t=2)
                            den = DEN[s][:, i, :].rearrange("p (t h) -> p t h", t=2)
                            link(v.tensor_scalar(den, src[:, :, 128:144], 1e-15, None, ALU.add))
                            link(v.reciprocal(den, den))
                            v.tensor_tensor(OTk[s][g][:, 256 * h:256 * h + 256].rearrange("p (t h d) -> p t h d", t=2, h=16),
                                            src[:, :, 0:128].rearrange("p t (h d) -> p t h d", h=16),
                                            den.unsqueeze(3).to_broadcast([P, 2, 16, 8]), ALU.mult)\
                             .then_inc(num_scaled, 1)
                    for s in range(SLOTS):
                        dve.wait_ge(proj_done, s + 1)
                        link(v.tensor_tensor(XT[s][:], TR[s][:].rearrange("p (t c) -> p t c", t=TILES),
                                             bnrow[:, 0, :].unsqueeze(1).to_broadcast([P, TILES, C]), ALU.mult))
                        dve.wait_ge(x_shifted, s + 1)
                        v.tensor_tensor(X[s][:], X[s][:], XT[s][:], ALU.add).then_inc(x_added, 1)
                        dve.wait_ge(x_added, s + 1)
                        if stop >= 3:
                            ln_stats(3, s)
                if stop >= 3:
                    for s in range(SLOTS):
                        ln_apply(3, s)
                    router(1, gamma=modb[:, 0:8])
                    for s in range(SLOTS):
                        dve.wait_ge(comb_ready, 3 + s)
                        link(v.tensor_tensor(rt[s][:, 0], comb[s][:],
                                             modb[:, 8:16].unsqueeze(1).to_broadcast([P, TILES, E]), ALU.mult))
                    for s in range(SLOTS):
                        for t2 in range(0, TILES, 2):
                            last2 = [0, 0]
                            for h in range(2):
                                c = 8 * s + 2 * t2 + 2 * h
                                dve.wait_ge(eo_done, c + 2)
                                for e in range(4):
                                    for d in range(2):
                                        t = t2 + d
                                        if last2[d]:
                                            after(last2[d])
                                        last2[d] = mark(v.scalar_tensor_tensor(
                                            X[s][:, t, :], M[(c + d) % 4][:, e * C:e * C + C],
                                            rt[s][:, 0, t, 4 * h + e:4 * h + e + 1],
                                            X[s][:, t, :], ALU.mult, ALU.add))
                                for d in range(2):
                                    after(last2[d])
                                v.nop().then_inc(eo_added, 2)
                        dve.wait_ge(eb_done, s + 1)
                        xf = X[s][:].rearrange("p t c -> p (t c)")
                        link(v.tensor_tensor(xf, xf, M[4][:], ALU.add))
                        if stop >= 4:
                            layernorm(p, 4, s)
                if stop >= 4:
                    for s in range(SLOTS):
                        for i in range(2):
                            n = P if i == 1 else 96
                            k = 2 * s + i + 1
                            dve.wait_ge(fused_padded, 3 * s + 2)
                            if k > 2:
                                dve.wait_ge(dw7_done, k - 2)
                            for t in range(L2_DVE):
                                dy, dx = divmod(t, 7)
                                for b in range(IMGS):
                                    win = P7[s][1 - i][0:n, b, dy:dy + SIDE, dx:dx + SIDE]
                                    acc = A7[k % 2][0:n, b]
                                    if t == 0:
                                        kk = mark(v.tensor_scalar(acc, win, dw2[0:n, 1 - i, 0:1], None, ALU.mult))
                                    else:
                                        after(kk - 1)
                                        ins_ = v.scalar_tensor_tensor(acc, win, dw2[0:n, 1 - i, t:t + 1], acc,
                                                                      ALU.mult, ALU.add)
                                        kk = mark(ins_)
                            after(kk)
                            dve.wait_ge(dw7_padd, (L2_POOL - 1) * k)
                            af = A7[k % 2][0:n].rearrange("p b y x -> p (b y x)")
                            v.tensor_tensor(af, af, AP7[(k - 1) % 2][0:n], ALU.add).then_inc(dw7_acc, 1)
                    for s in range(SLOTS):
                        dve.wait_ge(dw7_out, 2 * s + 1)
                        dve.wait_ge(fused_padded, 3 * s + 3)
                        v.tensor_tensor(G0[s][64:96, :], PA[s][64:96, :], D7[s][0][64:96, :], ALU.mult)\
                         .then_inc(g0_ready, 1)
                    for s in range(SLOTS):
                        dve.wait_ge(pw0_done, s + 1)
                        v.scalar_tensor_tensor(G1[s][0:64, :], M[4][0:64, :], pwb0[0:64, :], D7[s][0][0:64, :],
                                               ALU.add, ALU.mult).then_inc(g1_ready, 1)
                    for s in range(SLOTS):
                        dve.wait_ge(pw1_done, s + 1)
                        dve.wait_ge(dw7_out, 2 * s + 2)
                        v.scalar_tensor_tensor(G2[s], M[5][:], pwb1[:], D7[s][1], ALU.add, ALU.mult)\
                         .then_inc(g2_ready, 1)
                    for s in range(SLOTS):
                        dve.wait_ge(out2_done, s + 1)
                        link(v.tensor_tensor(X[s][:], X[s][:], TR[s][:].rearrange("p (t c) -> p t c", t=TILES), ALU.add))
                        v.tensor_tensor(X[s][:], X[s][:], bout[:].unsqueeze(1).to_broadcast([P, TILES, C]), ALU.add)\
                         .then_inc(x_after_l2, 1)
                        dve.wait_ge(x_after_l2, s + 1)
                        if stop >= 5:
                            ln_stats(5, s)
                if stop >= 5:
                    for s in range(SLOTS):
                        ln_apply(5, s)

                    def positions(s):
                        dve.wait_ge(xn_ready, ln_index(5, s) - 2)
                        if s == 1:
                            dve.wait_ge(qk_done, 3)
                        xn3 = XN[s][:].rearrange("p (b m) -> p b m", b=IMGS)
                        xq3 = XP.rearrange("p (b m) -> p b m", b=IMGS)
                        link(v.tensor_scalar(XP, XN[s][:], posw[:, 1:2], posw[:, 3:4], ALU.mult, ALU.add))
                        link(v.scalar_tensor_tensor(xq3[:, :, 1:HW], xn3[:, :, 0:HW - 1], posw[:, 0:1],
                                                    xq3[:, :, 1:HW], ALU.mult, ALU.add))
                        link(v.scalar_tensor_tensor(xq3[:, :, 0:HW - 1], xn3[:, :, 1:HW], posw[:, 2:3],
                                                    xq3[:, :, 0:HW - 1], ALU.mult, ALU.add))
                        v.tensor_tensor(XP, XP, XN[s][:], ALU.add).then_inc(xp_ready, 1)

                    def values(s):
                        dve.wait_ge(qk_done, 3 * s + 3)
                        dve.wait_ge(v_ones, 1)
                        v.tensor_tensor(Vh[s][:, :, :, 0:HD],
                                        M[2][:].rearrange("p (t h d) -> p t h d", t=TILES, h=HEADS),
                                        bv[:].rearrange("p (h d) -> p h d", h=HEADS).unsqueeze(1)
                                        .to_broadcast([P, TILES, HEADS, HD]), ALU.add).then_inc(v_ready, 1)

                    def divide(s, g):
                        dve.wait_ge(po_turned, 2 * s + g + 1)
                        src = M[2][:].rearrange("p (t h c) -> p t h c", t=TILES, h=4)
                        link(v.reciprocal(rdn[:, g], src[:, :, :, HD]))
                        v.tensor_tensor(OT[s][:, :, 4 * g:4 * g + 4, :], src[:, :, :, 0:HD],
                                        rdn[:, g].unsqueeze(3).to_broadcast([P, TILES, 4, HD]), ALU.mult)\
                         .then_inc(ot_ready, 1)

                    def add_attention(s):
                        dve.wait_ge(wo_done, s + 1)
                        dve.wait_ge(x_shifted, 3 + s)
                        xf = X[s][:].rearrange("p t c -> p (t c)")
                        v.tensor_tensor(xf, xf, M[2][:], ALU.add).then_inc(x_after_attn, 1)
                        dve.wait_ge(x_after_attn, s + 1)
                    positions(0)
                    values(0)
                    for c in range(UNITS):
                        if c == 6:
                            positions(1)
                        if c == 12:
                            values(1)
                        if c == 21:
                            divide(0, 0)
                        if c == 23:
                            divide(0, 1)
                        if c == 27:
                            add_attention(0)
                            if stop >= 6:
                                ln_stats(6, 0)
                        if c == 30 and stop >= 6:
                            ln_apply(6, 0)
                        lg = [LG[c % 3][:, q * 256:q * 256 + 256] for q in range(2)]
                        rp = [REP[c % 2][:, q * 256:q * 256 + 256] for q in range(2)]
                        t8 = top8[c % 4]
                        dve.wait_ge(lg_copied, c + 1)
                        k = [mark(v.max(t8[:, q, 0:8], lg[q])) for q in range(2)]
                        after(k[1])
                        v.tensor_scalar(nmx[c % 4][:], t8[:, :, 0], -1.0, None, ALU.mult).then_inc(lg_max, 1)
                        if c >= 2:
                            dve.wait_ge(rep_exp, c - 1)
                        k = [mark(v.match_replace(rp[q], t8[:, q, 0:8], lg[q], NEG)) for q in range(2)]
                        k2 = []
                        for q in range(2):
                            after(k[q])
                            k2.append(mark(v.max(t8[:, q, 8:16], rp[q])))
                        for q in range(2):
                            after(k2[q])
                            last = v.match_replace(rp[q], t8[:, q, 8:16], rp[q], NEG)
                        last.then_inc(rep_ready, 1)
                    divide(1, 0)
                    divide(1, 1)
                    add_attention(1)
                    if stop >= 6:
                        layernorm(p, 6, 1)
                if stop >= 6:
                    MAGIC = 1.5 * 2.0 ** 23
                    q = lambda s, i: hst[s][:, i, :]
                    half = lambda t, j: t[:, HW * j:HW * j + HW]

                    def by_image(dst, src, s1, s2, o1, o2=None):
                        for s in range(SLOTS):
                            after(done[s])
                            for j in range(IMGS):
                                done[s] = mark(v.tensor_scalar(half(dst[s], j), half(src[s], j),
                                                               hst[s][:, s1, j:j + 1],
                                                               None if s2 is None else hst[s][:, s2, j:j + 1],
                                                               *((o1,) if o2 is None else (o1, o2))))
                    for s in range(SLOTS):
                        dve.wait_ge(ss_done, s + 1)
                        v.tensor_scalar(q(s, 1), M[4][:, 2 * s:2 * s + 2], 1.0 / (C * HW), None, ALU.mult)\
                         .then_inc(ms_ready, 1)
                    for s in range(SLOTS):
                        dve.wait_ge(std_ready, s + 1)
                        begin(s, v.tensor_scalar(q(s, 3), q(s, 2), 2.513930578568423, 1e-8, ALU.mult, ALU.add))
                    in_turn(lambda s: v.tensor_scalar(q(s, 4), q(s, 3), 2.0 / 15.0, None, ALU.mult))
                    in_turn(lambda s: v.reciprocal(q(s, 5), q(s, 4)))
                    in_turn(lambda s: v.tensor_scalar(q(s, 6), q(s, 4), 0.5, None, ALU.mult))
                    in_turn(lambda s: v.tensor_scalar(q(s, 7), q(s, 3), -1.0, None, ALU.mult))
                    in_turn(lambda s: v.tensor_scalar(q(s, 8), q(s, 2), 2.513930578568423 / 15.0, None, ALU.mult))
                    dve.wait_ge(had_copied, 2)
                    by_image(H1, HS, 3, 7, ALU.min, ALU.max)
                    by_image(H1, H1, 5, None, ALU.mult)
                    in_turn(lambda s: v.tensor_scalar(H1[s], H1[s], 0.5, MAGIC, ALU.add, ALU.add))
                    in_turn(lambda s: v.tensor_scalar(H1[s], H1[s], -MAGIC, None, ALU.add))
                    by_image(H1, H1, 4, 6, ALU.mult, ALU.subtract)
                    in_turn(lambda s: v.tensor_tensor(H2[s], H1[s], HS[s], ALU.subtract))
                    in_turn(lambda s: v.scalar_tensor_tensor(H2[s], H2[s], -1.0, H2[s], ALU.mult, ALU.max))
                    by_image(H2, H2, 8, None, ALU.is_le)
                    in_turn(lambda s: v.tensor_tensor(H2[s], HS[s], H2[s], ALU.mult))
                    in_turn(lambda s: v.tensor_tensor(H3[s], H1[s], H2[s], ALU.subtract))
                    in_turn(lambda s: v.tensor_tensor(H3[s], H2[s], H3[s], ALU.add))
                    for s in range(SLOTS):
                        after(done[s])
                        xf = X[s][:].rearrange("p t c -> p (t c)")
                        v.tensor_tensor(xf, xf, H3[s], ALU.add).then_inc(x_after_had, 1)
                    for s in range(SLOTS):
                        dve.wait_ge(x_after_had, s + 1)
                        if stop >= 7:
                            ln_stats(7, s)
                    for s in range(SLOTS):
                        if stop >= 7:
                            ln_apply(7, s)
                if stop >= 7:
                    router(2)
                    for s in range(SLOTS):
                        for i in range(5):
                            c = 5 * s + i
                            n = P if i < 4 else 64
                            dve.wait_ge(silu_done, c + 1)
                            dve.wait_ge(upp_done, c + 1)
                            v.tensor_tensor(GU[s][i][0:n, :], SG[c % 2][0:n, :], M[2 + c % 2][0:n, :], ALU.mult)\
                             .then_inc(gu_ready, 1)
                    for s in range(SLOTS):
                        dve.wait_ge(comb_rows[s], 48)
                        for i in range(2, 4):
                            dve.wait_ge(gu_ready, 5 * s + i + 1)
                            v.tensor_tensor(GU[s][i], GU[s][i], CBP[s][:, i, :], ALU.mult).then_inc(gus_ready, 1)
                    for s in range(SLOTS):
                        dve.wait_ge(moe_done, s + 1)
                        xf = X[s][:].rearrange("p t c -> p (t c)")
                        v.tensor_tensor(xf, xf, M[4 + s][:], ALU.add).then_inc(x_final, 1)
                else:
                    for s in range(SLOTS):
                        dve.drain()
                        link(v.tensor_copy(hst[s][:, 0, :], X[s][:, 0, 0:2]))
                        v.tensor_copy(X[s][:, 0, 0:2], hst[s][:, 0, :]).then_inc(x_final, 1)
                new_steps()
                next_pass(dve, "dve")

        @block.tensor
        def _(pe):
            mm = nc.tensor.matmul
            tr = nc.tensor.transpose
            pe.wait_ge(first_in, 16)
            mm(TR[0][0:16, 0:16], ins[:], modw[:], start=True, stop=True).then_inc(pe_setup, 1)
            pe.wait_ge(act_setup, 1)
            pe.wait_ge(consts, 4)
            mm(TR[1][:, 0:16], sixteenth[:], modr[:], start=True, stop=True).then_inc(pe_setup, 1)
            pe.wait_ge(dve_setup, 1)
            pe.wait_ge(beta_in, 16)
            for e in range(E):
                last = mm(M[2][:, e:e + 1], beta_w[:, e, :], inssum[:], start=True, stop=True)
            last.then_inc(pe_setup, 1)
            pe.wait_ge(dve_setup, 3)
            mm(M[0][:, 0:256], ones[:], bndiag[:].rearrange("p g c -> p (g c)"), start=True, stop=True)\
                .then_inc(pe_setup, 1)
            pe.wait_ge(dve_setup, 4)
            tr(M[1][0:E, 0:C], btd[:], ident[:]).then_inc(pe_setup, 1)
            pe.wait_ge(act_setup, 2)

            def turn(bank, src4, sig):
                for t in range(TILES):
                    last = tr(bank[:, t * P:t * P + P], src4(t), ident[:])
                last.then_inc(sig, 1)

            def ln_turn(p, n, s):
                pe.wait_ge(xt_ready, ln_index(n, s))
                turn(TR[s], lambda t: XT[s][:, t, :], xt_turned)

            def logits(p, r, n, s, Wg):
                pe.wait_ge(xn_ready, ln_index(n, s) - 2)
                for t in range(TILES):
                    last = mm(TR[s][:, t * E:t * E + E], XN[s][:, t * P:t * P + P], Wg[:], start=True, stop=True)
                last.then_inc(logits_done, 1)

            def comb_turn(p, r, s):
                pe.wait_ge(comb_ready, 2 * r + s + 1)
                for t in range(TILES):
                    last = tr(TR[s][0:E, t * P:t * P + P], comb[s][:, t, :], ident[:])
                last.then_inc(comb_turned, 1)

            with pe.Fori(0, PASSES) as p:
                for s in range(SLOTS):
                    pe.wait_ge(x_loaded[s], 16)
                    turn(TR[s], lambda t: XC[s][:, t // 2, (t % 2) * P:(t % 2) * P + P], x_turned)
                for s in range(SLOTS):
                    pe.wait_ge(xt_ready, ln_index(0, s))
                    pe.wait_ge(pool_setup, 2)
                    pe.wait_ge(act_setup, 4)
                    xv = XT[s][:].rearrange("p (j h) c -> p h j c", h=2)
                    for m2 in range(7):
                        c = 7 * s + m2
                        if c >= 3:
                            pe.wait_ge(up_biased, c - 2)
                        for m in (2 * m2, 2 * m2 + 1):
                            parts = [i for i, (mm_, h) in enumerate(UP_PARTS) if mm_ == m]
                            for n_, i in enumerate(parts):
                                last = mm(M[c % 3][0:PM, (m % 2) * 256:(m % 2) * 256 + 256], upw[:, i, :],
                                          xv[:, UP_PARTS[i][1]], start=n_ == 0, stop=n_ == len(parts) - 1)
                        last.then_inc(up_done, 1)
                for s in range(SLOTS):
                    pe.wait_ge(up_clipped, 7 * s + 7)
                    pe.wait_ge(dve_setup, 5)
                    for h in range(2):
                        parts = [i for i, (h_, k) in enumerate(DOWN_PARTS) if h_ == h]
                        for n_, i in enumerate(parts):
                            last = mm(M[3 + s][:, h * 256:h * 256 + 256], downw[0:PM, i, :],
                                      Y[s][0:PM, DOWN_PARTS[i][1], :], start=n_ == 0, stop=n_ == len(parts) - 1)
                    last.then_inc(down_done, 1)
                if stop >= 1:
                    for s in range(SLOTS):
                        ln_turn(p, 1, s)
                    pe.wait_ge(stage1_in, 16)
                    for s in range(SLOTS):
                        logits(p, 0, 1, s, Wg0)
                    def ffn_up(d):
                        s, e = divmod(d, E)
                        for hc in range(4):
                            c = 4 * d + hc
                            if c >= 3:
                                pe.wait_ge(ffn_gelu_done, c - 2)
                            mm(M[c % 3][:], W1[:, e, hc * P:hc * P + P], XN[s][:], start=True, stop=True)\
                                .then_inc(ffn_up_done, 1)

                    def ffn_down(d):
                        pe.wait_ge(ffn_gelu_done, 4 * d + 4)
                        if d >= 2:
                            pe.wait_ge(ffn_scaled, d - 1)
                        for hc in range(4):
                            last = mm(M[[3, 5][d % 2]][:], W2[:, d % E, hc, :], H[d % 2][hc],
                                      start=hc == 0, stop=hc == 3)
                        last.then_inc(ffn_down_done, 1)

                    def ffn_turn(s):
                        pe.wait_ge(ffn_added, s + 1)
                        pe.wait_ge(combT_ready, s + 1)
                        turn(TR[s], lambda t: XT[s][:, t, :], ffn_turned)
                    ffn_up(0)
                    for d in range(SLOTS * E):
                        if d + 1 < SLOTS * E:
                            ffn_up(d + 1)
                        if d == 0:
                            for s in range(SLOTS):
                                comb_turn(p, 0, s)
                        ffn_down(d)
                        if d == E:
                            ffn_turn(0)
                    ffn_turn(1)
                if stop >= 2:
                    for s in range(SLOTS):
                        ln_turn(p, 2, s)
                    pe.wait_ge(later_in, 16)
                    pe.wait_ge(tap_mats, 2)
                    for s in range(SLOTS):
                        pe.wait_ge(xn_ready, ln_index(2, s) - 2)
                        for i in range(3):
                            if s == 1:
                                pe.wait_ge(qkv_padded, i + 1)
                            mm(M[i][:], Wqkv1[:, i, :], XN[s][:], start=True, stop=True).then_inc(qkv_done, 1)
                        for h in range(2):
                            if s == 1:
                                pe.wait_ge(kvpx_v, h + 1)
                            for t in range(2 * h, 2 * h + 2):
                                last = mm(M[3 + h][:, (t % 2) * 256:(t % 2) * 256 + 256],
                                          XN[s][:, t * P:t * P + P], Wqkv1[:, 1:3, :].rearrange("p i c -> p (i c)"),
                                          start=True, stop=True)
                            last.then_inc(kvpx_done, 1)
                    def taps5(k):
                        s, i = divmod(k, 3)
                        pe.wait_ge(qkv_padded, max(k + 1, min(6, 4 + i)))
                        if s == 1:
                            pe.wait_ge(dw5_out, i + 1)
                        for t in range(L1_TAPS - L1_PE, L1_TAPS):
                            dy, dx = divmod(t, 5)
                            mm(M[[5, 0, 1][i]][:].rearrange("p (b y x) -> p b y x", b=IMGS, y=SIDE),
                               w5[:, i, t - L1_TAPS + L1_PE, :], P5[s][i][:, :, dy:dy + SIDE, dx:dx + SIDE],
                               start=t == L1_TAPS - L1_PE, stop=False)

                    def close5(k):
                        i = k % 3
                        pe.wait_ge(dw5_acc, k + 1)
                        mm(M[[5, 0, 1][i]][:], pw1T[:, i, :], A5[(k + 1) % 2].rearrange("p b y x -> p (b y x)"),
                           start=False, stop=True).then_inc(dw5_done, 1)
                    taps5(0)
                    for k in range(6):
                        if k + 1 < 6:
                            taps5(k + 1)
                        close5(k)
                    for s in range(SLOTS):
                        for g in range(2):
                            pe.wait_ge(dw5_out, 3 * s + g + 2)
                            if g == 0:
                                pe.wait_ge(qkv_padded, 6)
                            pe.wait_ge(kvpx_v, 4)
                            if s == 1:
                                pe.wait_ge(agg_px, g + 1)
                            turn(M[2 + g], lambda t: KVC[s][g][:, t * P:t * P + P], agg_turned)
                    for s in range(SLOTS):
                        for g in range(2):
                            if g == 1:
                                pe.wait_ge(agg_px, 2 * s + 2)
                                pe.wait_ge(dw5_out, 6)
                            if s == 1:
                                pe.wait_ge(kv_masked, g + 1)
                            for j in range(IMGS):
                                for h in range(2):
                                    t = 2 * j + h
                                    last = mm(M[4 + g][:, 129 * j:129 * j + 129], KV[s][g][:, t, 0:128],
                                              KV[s][g][:, t, 128:257], start=h == 0, stop=h == 1)
                            last.then_inc(kv_done, 1)
                    for s in range(SLOTS):
                        for i in range(4):
                            g, h = divmod(i, 2)
                            pe.wait_ge(kv_masked, 2 * s + g + 1)
                            if s == 0:
                                pe.wait_ge(agg_px, 4)
                            if s == 1:
                                pe.wait_ge(num_scaled, i + 1)
                            for t in range(2):
                                last = mm(M[i][:, 144 * t:144 * t + 144],
                                          [Q1, Q2][g][s][:, (2 * h + t) * P:(2 * h + t) * P + P],
                                          KM[s][:, g, h, :], start=True, stop=True)
                            last.then_inc(num_done, 1)
                    for s in range(SLOTS):
                        for g in range(2):
                            pe.wait_ge(num_scaled, 4 * s + 2 * g + 2)
                            pe.wait_ge(kv_masked, 4)
                            if s == 1:
                                pe.wait_ge(o_ready, g + 1)
                            turn(M[4 + g], lambda t: OTk[s][g][:, t * P:t * P + P], o_turned)
                    for s in range(SLOTS):
                        pe.wait_ge(o_ready, 2 * s + 2)
                        for t in range(TILES):
                            for g in range(2):
                                last = mm(TR[s][:, t * C:t * C + C], OC[s][g][:, t * P:t * P + P], proj[:, g, :],
                                          start=g == 0, stop=g == 1)
                        last.then_inc(proj_done, 1)
                if stop >= 3:
                    for s in range(SLOTS):
                        ln_turn(p, 3, s)
                    for s in range(SLOTS):
                        logits(p, 1, 3, s, Wg1)
                    for s in range(SLOTS):
                        for t2 in range(0, TILES, 2):
                            for h in range(2):
                                for d in range(2):
                                    c = 8 * s + 2 * t2 + 2 * h + d
                                    if c >= 4:
                                        pe.wait_ge(eo_added, c - c % 2 - 2)
                                    mm(M[c % 4][:], XN[s][:, (t2 + d) * P:(t2 + d) * P + P],
                                       Wexp[:, 4 * h:4 * h + 4, :].rearrange("p e c -> p (e c)"),
                                       start=True, stop=True).then_inc(eo_done, 1)
                        comb_turn(p, 1, s)
                        pe.wait_ge(combT_ready, 3 + s)
                        if s == 1 and stop >= 4:
                            pe.wait_ge(xt_ready, ln_index(4, 0))
                        for t in range(TILES):
                            last = mm(M[4][:, t * C:t * C + C], combT[s][:, t * P:t * P + P], bt[:],
                                      start=True, stop=True)
                        last.then_inc(eb_done, 1)
                if stop >= 4:
                    for s in range(SLOTS):
                        ln_turn(p, 4, s)
                    for s in range(SLOTS):
                        pe.wait_ge(xn_ready, ln_index(4, s) - 2)
                        for i in range(3):
                            if s == 1:
                                pe.wait_ge(fused_padded, i + 1)
                            out = [M[4][:], M[5][0:96, :], M[3][64:96, :]][i]
                            mm(out, [Win[:, 0:128], Win[:, 128:224], Win[:, 224:256]][i], XN[s][:],
                               start=True, stop=True).then_inc(fused_done, 1)
                    def taps7(k):
                        s, i = divmod(k, 2)
                        n = P if i == 1 else 96
                        pe.wait_ge(fused_padded, 3 * s + 2)
                        if s == 1:
                            pe.wait_ge(dw7_out, i + 1)
                        for t in range(L2_TAPS - L2_PE, L2_TAPS):
                            dy, dx = divmod(t, 7)
                            mm(M[i][0:n, :].rearrange("p (b y x) -> p b y x", b=IMGS, y=SIDE),
                               w7[0:n, 1 - i, t - L2_TAPS + L2_PE, 0:n],
                               P7[s][1 - i][0:n, :, dy:dy + SIDE, dx:dx + SIDE],
                               start=t == L2_TAPS - L2_PE, stop=False)

                    def close7(k):
                        n = P if k % 2 == 1 else 96
                        pe.wait_ge(dw7_acc, k + 1)
                        mm(M[k % 2][0:n, :], ident[0:n, 0:n], A7[(k + 1) % 2][0:n].rearrange("p b y x -> p (b y x)"),
                           start=False, stop=True).then_inc(dw7_done, 1)
                    taps7(0)
                    for k in range(4):
                        if k == 3:
                            close7(k)
                        elif k == 1:
                            taps7(2)
                            close7(1)
                        else:
                            taps7(k + 1)
                            close7(k)
                    for s in range(SLOTS):
                        pe.wait_ge(g0_ready, s + 1)
                        if s == 0:
                            pe.wait_ge(fused_padded, 6)
                        else:
                            pe.wait_ge(g1_ready, 1)
                        mm(M[4][0:64, :], pwT0[64:96, :], G0[s][64:96, :], start=True, stop=True)\
                            .then_inc(pw0_done, 1)
                    for s in range(SLOTS):
                        pe.wait_ge(g1_ready, s + 1)
                        if s == 1:
                            pe.wait_ge(g2_ready, 1)
                        mm(M[5][:], pwT1[0:64, :], G1[s][0:64, :], start=True, stop=True).then_inc(pw1_done, 1)
                    for s in range(SLOTS):
                        pe.wait_ge(g2_ready, s + 1)
                        for t in range(TILES):
                            last = mm(TR[s][:, t * C:t * C + C], G2[s][:, t * P:t * P + P], Wout[:],
                                      start=True, stop=True)
                        last.then_inc(out2_done, 1)
                if stop >= 5:
                    for s in range(SLOTS):
                        ln_turn(p, 5, s)
                    def project(s, i):
                        if i == 0:
                            pe.wait_ge(xp_ready, s + 1)
                            if s == 1:
                                pe.wait_ge(v_ready, 1)
                        else:
                            pe.wait_ge(qk_ready, 2 * s + i)
                        if i < 2:
                            mm(M[2][:], Wqkv2[:, i, :], XP, start=True, stop=True).then_inc(qk_done, 1)
                        else:
                            for t in range(TILES):
                                last = mm(M[2][:, t * C:t * C + C], XP[:, t * P:t * P + P], Wqkv2[:, 2, :],
                                          start=True, stop=True)
                            last.then_inc(qk_done, 1)

                    def lg(c):
                        hh, j = divmod(c, 2)
                        s = hh // HEADS
                        pe.wait_ge(qm_ready, hh + 1)
                        pe.wait_ge(qk_ready, 2 * s + 2)
                        if c >= 2:
                            pe.wait_ge(lg_copied, c - 1)
                        for q in range(2):
                            t = 2 * j + q
                            last = mm(M[c % 2][:, q * 256:q * 256 + 256],
                                      QM[hh % 3][:, t * P:t * P + P], Kc[s][:, j * 256:j * 256 + 256],
                                      start=True, stop=True)
                        last.then_inc(lg_done, 1)

                    def pv(gr):
                        s, g = gr // 4, gr // 2 % 2
                        pe.wait_ge(pt_ready, 4 * gr + 4)
                        pe.wait_ge(v_ready, s + 1)
                        if gr in (4, 5):
                            pe.wait_ge(po_ready, 1)
                        bank = [M[5], TR[s]][g]
                        for j in range(IMGS):
                            for kt in range(2):
                                for x in range(2):
                                    c = 4 * gr + 2 * x + j
                                    h = c // 2 % HEADS
                                    hq = h % 4
                                    last = mm(bank[32 * hq:32 * hq + 32, j * 256:j * 256 + 256],
                                              Vh[s][:, 2 * j + kt, h, :], PT[c % 5][:, kt * 256:kt * 256 + 256],
                                              start=kt == 0, stop=kt == 1)
                        last.then_inc(pv_done, 1)

                    def post(s, i):
                        if i < 2:
                            pe.wait_ge(po_ready, 2 * s + i + 1)
                            if i == 1:
                                pe.wait_ge(ot_ready, 2 * s + 1)
                            elif s == 0:
                                pe.wait_ge(v_ready, 2)
                            else:
                                pe.wait_ge(x_after_attn, 1)
                            turn(M[2], lambda t: PO[i][:, t * P:t * P + P], po_turned)
                        elif i == 2:
                            pe.wait_ge(ot_ready, 2 * s + 2)
                            turn(M[2], lambda t: OT[s][:, t].rearrange("p h d -> p (h d)"), ot_turned)
                        else:
                            pe.wait_ge(oc_ready, s + 1)
                            for t in range(TILES):
                                last = mm(M[2][:, t * C:t * C + C], OCf[s][:, t * P:t * P + P], Wo[:],
                                          start=True, stop=True)
                            last.then_inc(wo_done, 1)
                    for i in range(3):
                        project(0, i)
                    lg(0)
                    lg(1)
                    for c in range(UNITS):
                        if c + 2 < UNITS:
                            lg(c + 2)
                        pe.wait_ge(pr_ready, c + 1)
                        if c >= 2:
                            pe.wait_ge(pt_ready, c - 1)
                        for kt in range(2):
                            for q in range(2):
                                last = tr(M[3 + c % 2][:, kt * 256 + q * P:kt * 256 + q * P + P],
                                          PR[c % 2][:, q * 256 + kt * P:q * 256 + kt * P + P], ident[:])
                        last.then_inc(pt_done, 1)
                        if c % 4 == 0 and c > 0:
                            pv(c // 4 - 1)
                        if c in (7, 8, 9):
                            project(1, c - 7)
                        if c in (18, 20, 22, 24):
                            post(0, (c - 18) // 2)
                    pv(UNITS // 4 - 1)
                    for i in range(4):
                        post(1, i)
                if stop >= 6:
                    for s in range(SLOTS):
                        ln_turn(p, 6, s)
                    for s in range(SLOTS):
                        pe.wait_ge(xn_ready, ln_index(6, s) - 2)
                        pe.wait_ge(x_after_attn, 2)
                        for t in range(TILES):
                            last = mm(M[2 + s][:, t * C:t * C + C], XN[s][:, t * P:t * P + P], Whad[:],
                                      start=True, stop=True)
                        last.then_inc(had_done, 1)
                    for s in range(SLOTS):
                        pe.wait_ge(had_sq, s + 1)
                        if s == 1:
                            pe.wait_ge(ms_ready, 1)
                        mm(M[4][:, 2 * s:2 * s + 2], ones[:], hst[s][:, 0, :], start=True, stop=True)\
                            .then_inc(ss_done, 1)
                if stop >= 7:
                    for s in range(SLOTS):
                        ln_turn(p, 7, s)
                    for s in range(SLOTS):
                        logits(p, 2, 7, s, Wg3)
                    for s in range(SLOTS):
                        for i in range(5):
                            c = 5 * s + i
                            n = P if i < 4 else 64
                            if c >= 2:
                                pe.wait_ge(gu_ready, c - 1)
                            mm(M[c % 2][0:n, :], Wgate[:, i, 0:n], XN[s][:], start=True, stop=True)\
                                .then_inc(gate_done, 1)
                            mm(M[2 + c % 2][0:n, :], Wup[:, i, 0:n], XN[s][:], start=True, stop=True)\
                                .then_inc(upp_done, 1)
                            if c == 1:
                                for j in range(SLOTS):
                                    comb_turn(p, 2, j)
                    for s in range(SLOTS):
                        pe.wait_ge(gus_pool, 2 * s + 2)
                        pe.wait_ge(gus_ready, 2 * s + 2)
                        for t in range(TILES):
                            for i in range(5):
                                n = P if i < 4 else 64
                                last = mm(M[4 + s][:, t * C:t * C + C], GU[s][i][0:n, t * P:t * P + P],
                                          Wdown[0:n, i, :], start=i == 0, stop=i == 4)
                        last.then_inc(moe_done, 1)
                for s in range(SLOTS):
                    pe.wait_ge(x_final, s + 1)
                    turn(TR[s], lambda t: X[s][:, t, :], xf_turned)
                next_pass(pe, "pe")


def layout(inputs):
    f = {k: np.asarray(v) for k, v in inputs.items()}
    T = np.ascontiguousarray
    rep = lambda v: T(np.broadcast_to(np.asarray(v).reshape(1, -1), (P, np.asarray(v).size)))
    o = {}
    o["x"] = T(f["x"].reshape(B, C, HW).transpose(1, 0, 2))
    o["ident"] = np.eye(P, dtype=np.float32)
    o["taps"] = rep(np.concatenate([f["L0_conv_up_filter"], f["L0_conv_down_filter"]]))
    hh, ww = np.divmod(np.arange(P), SIDE)
    y = np.arange(UP)
    mA = np.stack([y[None, :] - 2 * (hh[:, None] + 8 * h) for h in (0, 1)], 1)
    mB = y[None, :] - 2 * ww[:, None]
    r, xx = np.divmod(np.arange(P), UP)
    dA = np.stack([11 - (ROWS_M * k + r[:, None] - 2 * (8 * h + np.arange(8)[None, :])) for h, k in DOWN_PARTS], 1)
    dB = 11 - (xx[:, None] - 2 * np.arange(SIDE)[None, :])
    o["tap_no"] = T(np.concatenate([m.reshape(P, -1) for m in (mA, mB, dA, dB)], 1).astype(np.float32))
    o["conv_bias"] = rep(f["L0_conv_bias"])
    o["Wg0"] = f["L0_ffn_Wg"]
    o["pick"] = rep(np.arange(E, 0, -1).astype(np.float32))
    o["W1"] = T(f["L0_ffn_W1"].transpose(1, 0, 2))
    o["b1"] = T(f["L0_ffn_b1"].reshape(E * 4, P).T)
    o["W2"] = T(f["L0_ffn_W2"].reshape(E, 4, P, C).transpose(2, 0, 1, 3))
    o["b2T"] = T(f["L0_ffn_b2"].T)
    perm = (24 * np.arange(16)[None, :, None] + 8 * np.arange(3)[:, None, None] + np.arange(8)).reshape(3, P)
    o["Wqkv1"] = T(f["L1_conv_qkv_w"].reshape(384, C)[perm].transpose(2, 0, 1))
    o["dw1"] = T(f["L1_conv_agg_dw_w"].reshape(384, 25)[perm].transpose(1, 0, 2))
    pw = f["L1_conv_agg_pw_w"].reshape(384, 8)[perm]
    blk = np.zeros((P, 3, P), np.float32)
    co = np.arange(P)
    for ci in range(8):
        blk[8 * (co // 8) + ci, :, co] = pw[:, co, ci].T
    o["pw1T"] = blk
    o["proj"] = T(f["L1_conv_proj_w"].reshape(C, 2, P).transpose(2, 1, 0))
    o["headmask1"] = (co[:, None] // 8 == co[None, :] // 8).astype(np.float32)
    o["bn"] = T(np.stack([f["L1_conv_bn_gamma"], f["L1_conv_bn_beta"], f["L1_conv_bn_mean"], f["L1_conv_bn_var"]], 1))
    o["ins"] = T(f["L1_ffn_Ins_tk"][0].T)
    o["modw"] = T(np.concatenate([f["L1_ffn_rmod_w"], f["L1_ffn_gamma_w"].T], 1))
    o["beta_w"] = T(f["L1_ffn_beta_w"].transpose(1, 0, 2))
    o["exp_bT"] = T(f["L1_ffn_expert_b"].T)
    o["Wg1"] = f["L1_ffn_gate_w"]
    o["Wexp"] = T(f["L1_ffn_expert_w"].transpose(1, 0, 2))
    order = np.concatenate([np.arange(128, 256), np.arange(64, 128), np.arange(32, 64), np.arange(0, 32)])
    o["Win"] = T(f["L2_conv_w_in"][order].T)
    b = f["L2_conv_b_in"][order]
    pad = lambda v, lo=0: np.concatenate([np.zeros(lo, np.float32), v, np.zeros(P - lo - v.size, np.float32)])
    o["bin"] = T(np.stack([b[0:128], pad(b[128:224])], 1))
    o["bpa"] = pad(b[224:256], 64).reshape(P, 1)
    dorder = order[:224] - 32
    d = f["L2_conv_dw_w"].reshape(224, 49)[dorder]
    o["dw2"] = T(np.stack([d[0:128], np.concatenate([d[128:], np.zeros((32, 49), np.float32)])], 1))
    db = f["L2_conv_dw_b"][dorder]
    o["dwb2"] = T(np.stack([db[0:128], pad(db[128:])], 1))
    z = np.zeros((P, 64), np.float32)
    z[64:96] = f["L2_conv_pw0_w"].T
    o["pwT0"] = z
    o["pwb0"] = pad(f["L2_conv_pw0_b"]).reshape(P, 1)
    z = np.zeros((P, P), np.float32)
    z[0:64] = f["L2_conv_pw1_w"].T
    o["pwT1"] = z
    o["pwb1"] = f["L2_conv_pw1_b"].reshape(P, 1)
    o["Wout"] = T(f["L2_conv_w_out"].T)
    o["bout"] = rep(f["L2_conv_b_out"])
    o["posw"] = T(np.concatenate([f["L2_ffn_pos_w"].reshape(C, 3), f["L2_ffn_pos_b"].reshape(C, 1)], 1))
    o["Wqkv2"] = T(f["L2_ffn_qkv_w"].reshape(3, C, C).transpose(2, 0, 1))
    o["bqk"] = T(f["L2_ffn_qkv_b"][0:256].reshape(2, C).T)
    o["bv"] = rep(f["L2_ffn_qkv_b"][256:384])
    o["headmask2"] = (co[:, None] // HD == np.arange(HEADS)[None, :]).astype(np.float32)
    o["Wo"] = T(f["L2_ffn_wo_w"].T)
    o["bo"] = rep(f["L2_ffn_wo_b"])
    z = np.zeros((P, P), np.float32)
    z[0:64, 0:64] = f["L3_conv_aux_matrix"]
    z[64:, 64:] = f["L3_conv_aux_matrix"]
    o["Whad"] = z
    o["Wg3"] = f["L3_ffn_router"]

    def pairs(we, ws):
        z = np.zeros((P, 5, P), np.float32)
        z[:, 0:4] = we.reshape(4, 2, C, 64).transpose(2, 0, 1, 3).reshape(C, 4, P)
        z[:, 4, 0:64] = ws
        return z
    o["Wgate"] = pairs(f["L3_ffn_W_gate"], f["L3_ffn_shared_gate"])
    o["Wup"] = pairs(f["L3_ffn_W_up"], f["L3_ffn_shared_up"])
    z = np.zeros((P, 5, C), np.float32)
    z[:, 0:4] = f["L3_ffn_W_down"].reshape(4, P, C).transpose(1, 0, 2)
    z[0:64, 4] = f["L3_ffn_shared_down"]
    o["Wdown"] = z
    for pack, parts in PACKS.items():
        o[pack] = np.concatenate([o.pop(name).reshape(P, -1) for name, _ in parts], 1)
    return {k: np.ascontiguousarray(v) for k, v in o.items()}


def kernel(**inputs):
    import concourse.bacc as _bacc
    from concourse.bass_utils import run_bass_kernel_spmd as _run

    nc = _bacc.Bacc("TRN2", target_bir_lowering=False, num_devices=1)
    arrays, args = {}, {}
    for name, v in layout(inputs).items():
        arrays[f"in_{name}_dram"] = v
        args[name] = nc.dram_tensor(f"in_{name}_dram", v.shape, mybir.dt.from_np(v.dtype), kind="ExternalInput").ap()
    out = nc.dram_tensor("out_0_dram", (B, C, HW), mybir.dt.float32, kind="ExternalOutput").ap()
    args["out"] = out.rearrange("b c n -> c b n")
    metaformer(nc, args)
    r = _run(nc, [arrays], core_ids=[0])
    return r.results[0]["out_0_dram"].reshape(B, C, SIDE, SIDE)
```

```python
import numpy as np
import concourse.bass as bass
from concourse import mybir
from contextlib import ExitStack

B, C, HW = 8, 128, 256
SIDE = 16
P = 128
SLOTS = 2
IMGS = 2
PASSES = B // (SLOTS * IMGS)
TILES = IMGS * HW // P
N = IMGS * HW
E = 8
HID = 512
TAPS = 12
UP = 42
ROWS_M = 3
M_UP = UP // ROWS_M
PM = ROWS_M * UP

def _up_halves(m):
    lo, hi = max(0, -(-(ROWS_M * m - 11) // 2)), min(SIDE - 1, (ROWS_M * m + 2) // 2)
    return [h for h in (0, 1) if lo <= 8 * h + 7 and hi >= 8 * h]
UP_PARTS = [(m, h) for m in range(M_UP) for h in _up_halves(m)]
DOWN_PARTS = [(h, k) for h in (0, 1) for k in range(M_UP)
              if ROWS_M * k + 2 >= 16 * h and ROWS_M * k <= 16 * h + 14 + 11]

L1_TAPS, L1_PAD, L1_W = 25, 2, 20
L2_TAPS, L2_PAD, L2_W = 49, 3, 22
L1_DVE, L1_POOL = 10, 6
L2_DVE, L2_POOL = 19, 12
DOWN_LAG = 5
L1_PE, L2_PE = L1_TAPS - L1_DVE - L1_POOL, L2_TAPS - L2_DVE - L2_POOL
RING = 3
HEADS, HD = 8, 16
N_UP = 3 * UP
N_DN = 8 * len(DOWN_PARTS) + SIDE
PACKS = {
    "first": [("ident", (P,)), ("tap_no", (N_UP + N_DN,)), ("taps", (2 * TAPS,)), ("conv_bias", (C,)),
              ("bn", (4,)),
              ("ins", (16,)), ("modw", (16,)),
              ("exp_bT", (E,)), ("dw1", (3, L1_TAPS)),
              ("pw1T", (3, P)),
              ("dw2", (2, L2_TAPS))],
    "stage1": [("Wg0", (E,)), ("pick", (E,)),
               ("b1", (E * 4,)), ("b2T", (E,)), ("W1", (E, HID)), ("W2", (E, 4, C))],
    "later": [("Wqkv1", (3, P)),
              ("proj", (2, C)),
              ("headmask1", (P,)),
              ("Wg1", (E,)), ("Wexp", (E, C)),
              ("Win", (256,)),
              ("bin", (2,)), ("bpa", (1,)), ("dwb2", (2,)),
              ("pwT0", (64,)), ("pwb0", (1,)), ("pwT1", (P,)), ("pwb1", (1,)), ("Wout", (C,)), ("bout", (C,)),
              ("posw", (4,)),
              ("Wqkv2", (3, C)), ("bqk", (2,)), ("bv", (C,)), ("headmask2", (HEADS,)), ("Wo", (C,)), ("bo", (C,)),
              ("Whad", (P,)), ("Wg3", (E,)), ("Wgate", (5, P)), ("Wup", (5, P)), ("Wdown", (5, C))],
}
LN_EPS = [1e-6, 1e-5] * 4
NEG = -3.0e38


def metaformer(nc, a):
    F32 = mybir.dt.float32
    ALU = mybir.AluOpType
    ACT = mybir.ActivationFunctionType
    AX = mybir.AxisListType

    ctx = ExitStack()
    with ctx:
        def sb(name, shape, dt=F32):
            return ctx.enter_context(nc.sbuf_tensor(name, shape, dt))

        def S(name):
            return ctx.enter_context(nc.semaphore(name))

        M = [ctx.enter_context(nc.psum_tensor(f"M{i}", [P, 512], F32)) for i in range(6)]
        TR = [ctx.enter_context(nc.psum_tensor(f"TR{i}", [P, 512], F32)) for i in range(2)]

        BANK5 = [5, 0, 1]

        W = {}
        packs = {}
        for pack, parts in PACKS.items():
            packs[pack] = sb("w_" + pack, [P, sum(int(np.prod(shape)) for _, shape in parts)])
            o = 0
            for name, shape in parts:
                n = int(np.prod(shape))
                W[name] = packs[pack][:, o:o + n]
                if len(shape) == 2:
                    W[name] = W[name].rearrange("p (a b) -> p a b", a=shape[0])
                if len(shape) == 3:
                    W[name] = W[name].rearrange("p (a b c) -> p a b c", a=shape[0], b=shape[1])
                o += n
        ident, taps, conv_bias = W["ident"], W["taps"], W["conv_bias"]
        pick, Wg0, b1, W1, W2 = W["pick"], W["Wg0"], W["b1"], W["W1"], W["W2"]
        Wqkv1, dw1, pw1T, proj, headmask1 = W["Wqkv1"], W["dw1"], W["pw1T"], W["proj"], W["headmask1"]
        bn, ins, modw, exp_bT = W["bn"], W["ins"], W["modw"], W["exp_bT"]
        Wg1, Wexp = W["Wg1"], W["Wexp"]
        Win, bin_, bpa, dw2, dwb2 = W["Win"], W["bin"], W["bpa"], W["dw2"], W["dwb2"]
        pwT0, pwb0, pwT1, pwb1, Wout, bout = (W[n] for n in ("pwT0", "pwb0", "pwT1", "pwb1", "Wout", "bout"))
        posw, Wqkv2, bqk, bv, headmask2 = W["posw"], W["Wqkv2"], W["bqk"], W["bv"], W["headmask2"]
        Wo, bo, Whad, Wg3 = W["Wo"], W["bo"], W["Whad"], W["Wg3"]
        Wgate, Wup, Wdown = W["Wgate"], W["Wup"], W["Wdown"]
        b2T = W["b2T"]

        ones = sb("ones", [P, P])
        mhalf = sb("mhalf", [P, TILES])
        phalf = sb("phalf", [P, 2])
        upw = sb("upw", [P, len(UP_PARTS), PM])
        downw = sb("downw", [P, len(DOWN_PARTS), P])
        filt = sb("filt", [P, N_UP + N_DN])
        upA = filt[:, 0:2 * UP].rearrange("p (h y) -> p h y", h=2)
        upB = filt[:, 2 * UP:N_UP]
        dnA = filt[:, N_UP:N_UP + 8 * len(DOWN_PARTS)].rearrange("p (k j) -> p k j", j=8)
        dnB = filt[:, N_UP + 8 * len(DOWN_PARTS):N_UP + N_DN]
        w5 = sb("w5", [P, 3, L1_PE, P])
        w7 = sb("w7", [P, 2, L2_PE, P])
        bncol = sb("bncol", [P, 4])
        bndiag = sb("bndiag", [P, 2, P])
        bnrow = sb("bnrow", [P, 2, C])
        inssum = sb("inssum", [P, 1])
        modr = sb("modr", [16, 16])
        sixteenth = sb("sixteenth", [16, P])
        modb = sb("modb", [P, 16])
        btd = sb("btd", [P, E])
        bt = sb("bt", [E, C])

        X = [sb(f"X{s}", [P, TILES, C]) for s in range(SLOTS)]
        XT = [sb(f"XT{s}", [P, TILES, C]) for s in range(SLOTS)]
        XN = [sb(f"XN{s}", [P, N]) for s in range(SLOTS)]
        XC = [XN[s][:].rearrange("p (b n) -> p b n", b=IMGS) for s in range(SLOTS)]
        lnst = [sb(f"lnst{s}", [P, TILES, 6]) for s in range(SLOTS)]
        lnmv = [sb(f"lnmv{s}", [P, TILES, 2]) for s in range(SLOTS)]
        lnve = [sb(f"lnve{s}", [P, TILES]) for s in range(SLOTS)]
        lnrs = [sb(f"lnrs{s}", [P, TILES]) for s in range(SLOTS)]
        rt = [sb(f"rt{s}", [P, 8, TILES, E]) for s in range(SLOTS)]
        rs1 = [sb(f"rs1{s}", [P, 8, TILES]) for s in range(SLOTS)]
        comb = [sb(f"comb{s}", [P, TILES, E]) for s in range(SLOTS)]
        combT = [sb(f"combT{s}", [E, N]) for s in range(SLOTS)]

        ARENA = 70 * 256 + 192
        arena = sb("arena", [P, ARENA])
        at_ = [0]
        def piece(n, shape_str=None, **kw):
            o = at_[0]
            at_[0] += n
            assert at_[0] <= ARENA, at_[0]
            v = arena[:, o:o + n]
            return v.rearrange(shape_str, **kw) if shape_str else v
        Y = [piece(M_UP * 256, "p (m n) -> p m n", m=M_UP) for s in range(SLOTS)]
        Z = [piece(512) for _ in range(3)]
        Zb = [piece(512) for _ in range(3)]
        picked = arena[:, 0:TAPS * (N_UP + N_DN)]
        beta_w = arena[:, 12288:12288 + E * C].rearrange("p (e c) -> p e c", e=E)
        at_[0] = 0
        H = [[piece(512) for _ in range(4)] for _ in range(2)]
        CB = [piece(E * N, "p (e n) -> p e n", e=E) for _ in range(SLOTS)]
        YS = [piece(512) for _ in range(2)]
        at_[0] = 0
        at_[0] = ARENA - SLOTS * 3 * IMGS * L1_W * L1_W
        P5 = [[piece(IMGS * L1_W * L1_W, "p (b y x) -> p b y x", b=IMGS, y=L1_W) for _ in range(3)]
              for _ in range(SLOTS)]
        at_[0] = 0
        A5 = [piece(512, "p (b y x) -> p b y x", b=IMGS, y=SIDE) for _ in range(2)]
        AP5 = [piece(512) for _ in range(2)]
        PROD5 = [piece(512) for _ in range(RING)]
        Q1 = [piece(512) for _ in range(SLOTS)]
        Q2 = [piece(512) for _ in range(SLOTS)]
        KVC = [[piece(512) for _ in range(2)] for _ in range(SLOTS)]
        KV = [[piece(TILES * 260, "p (t c) -> p t c", t=TILES) for _ in range(2)] for _ in range(SLOTS)]
        KM = [piece(2 * IMGS * 144, "p (g j c) -> p g j c", g=2, j=IMGS) for _ in range(SLOTS)]
        OTk = [[P5[s][g].rearrange("p b y x -> p (b y x)")[:, 0:512] for g in range(2)] for s in range(SLOTS)]
        OC = [[KVC[s][g] for g in range(2)] for s in range(SLOTS)]
        DEN = [sb(f"DEN{s}", [P, 4, 16 * 2]) for s in range(SLOTS)]
        at_[0] = 0
        P7 = [[piece(IMGS * L2_W * L2_W, "p (b y x) -> p b y x", b=IMGS, y=L2_W) for _ in range(2)]
              for _ in range(SLOTS)]
        A7 = [piece(512, "p (b y x) -> p b y x", b=IMGS, y=SIDE) for _ in range(2)]
        AP7 = [piece(512) for _ in range(2)]
        PROD7 = [piece(512) for _ in range(RING)]
        PA = [piece(512) for _ in range(SLOTS)]
        D7 = [[piece(512) for _ in range(2)] for _ in range(SLOTS)]
        G0 = [piece(512) for _ in range(SLOTS)]
        G1 = [piece(512) for _ in range(SLOTS)]
        G2 = [piece(512) for _ in range(SLOTS)]
        at_[0] = 0
        XP = piece(512)
        Qc = [piece(512) for _ in range(SLOTS)]
        Kc = [piece(512) for _ in range(SLOTS)]
        Vh = [piece(TILES * HEADS * 32, "p (t h c) -> p t h c", t=TILES, h=HEADS) for _ in range(SLOTS)]
        QM = [piece(512) for _ in range(3)]
        LG = [piece(512) for _ in range(3)]
        REP = [piece(512) for _ in range(2)]
        E1 = [piece(512) for _ in range(2)]
        E2 = [piece(512) for _ in range(2)]
        PR = [piece(512) for _ in range(2)]
        PT = [piece(512) for _ in range(5)]
        PO = [piece(512) for _ in range(2)]
        OT = [XT[s][:].rearrange("p t (h d) -> p t h d", h=HEADS) for s in range(SLOTS)]
        OCf = [XN[s][:] for s in range(SLOTS)]
        UNITS = SLOTS * HEADS * IMGS
        top8 = [sb(f"top8_{i}", [P, 2, 16]) for i in range(4)]
        nmx = [sb(f"nmx{i}", [P, 2]) for i in range(4)]
        rdn = sb("rdn", [P, 2, TILES, 4])
        at_[0] = 0
        HS, HQ, H1, H2, H3 = ([None] * SLOTS for _ in range(5))
        for s, start in ((0, 60 * 256), (1, 0)):
            at_[0] = start
            for bufs in (HS, HQ, H1, H2, H3):
                bufs[s] = piece(512)
        hst = [sb(f"hst{s}", [P, 9, IMGS]) for s in range(SLOTS)]
        at_[0] = 0
        SG = [piece(512) for _ in range(2)]
        GU = [[piece(512) for _ in range(5)] for _ in range(SLOTS)]
        CBP = [piece(4 * N, "p (i n) -> p i n", i=4) for _ in range(SLOTS)]
        comb_dram = [nc.dram_tensor(f"comb_rows{s}", (E, N), F32, kind="Internal").ap() for s in range(SLOTS)]

        first_in = S("first_in")
        beta_in = S("beta_in")
        stage1_in = S("stage1_in")
        later_in = S("later_in")
        consts = S("consts")
        dve_setup = S("dve_setup")
        pe_setup = S("pe_setup")
        act_setup = S("act_setup")
        pool_setup = S("pool_setup")
        dve_step = S("dve_step")
        pool_step = S("pool_step")
        pass_end = S("pass_end")
        pass_go = {n: S("go_" + n) for n in ("pe", "act", "dve", "pool")}
        borders5 = S("borders5")
        borders7 = S("borders7")
        tap_mats = S("tap_mats")
        v_ones = S("v_ones")
        lg_copied = S("lg_copied")
        x_loaded = [S(f"x_loaded{s}") for s in range(SLOTS)]
        x_turned = S("x_turned")
        x_in = S("x_in")
        ln_var = S("ln_var")
        ln_rstd = S("ln_rstd")
        xt_ready = S("xt_ready")
        xt_turned = S("xt_turned")
        xn_ready = S("xn_ready")
        up_done = S("up_done")
        up_biased = S("up_biased")
        up_leaky = S("up_leaky")
        up_gained = S("up_gained")
        up_clipped = S("up_clipped")
        down_done = S("down_done")
        x_after_conv = S("x_after_conv")
        logits_done = S("logits_done")
        router_shifted = S("router_shifted")
        router_exp = S("router_exp")
        comb_ready = S("comb_ready")
        comb_turned = S("comb_turned")
        combT_ready = S("combT_ready")
        ffn_up_done = S("ffn_up_done")
        ffn_gelu_done = S("ffn_gelu_done")
        ffn_down_done = S("ffn_down_done")
        ffn_scaled = S("ffn_scaled")
        ffn_turned = S("ffn_turned")
        x_after_ffn = S("x_after_ffn")
        comb_stored = [S(f"comb_stored{s}") for s in range(SLOTS)]
        comb_rows = [S(f"comb_rows{s}") for s in range(SLOTS)]
        ffn_added = S("ffn_added")
        qkv_done = S("qkv_done")
        qkv_padded = S("qkv_padded")
        kvpx_done = S("kvpx_done")
        kvpx_k = S("kvpx_k")
        kvpx_v = S("kvpx_v")
        dw5_first = S("dw5_first")
        dw5_prod = S("dw5_prod")
        dw5_padd = S("dw5_padd")
        dw7_first = S("dw7_first")
        dw7_prod = S("dw7_prod")
        dw7_padd = S("dw7_padd")
        dw5_acc = S("dw5_acc")
        dw5_done = S("dw5_done")
        dw5_out = S("dw5_out")
        agg_turned = S("agg_turned")
        agg_px = S("agg_px")
        kv_done = S("kv_done")
        kv_masked = S("kv_masked")
        num_done = S("num_done")
        num_scaled = S("num_scaled")
        o_turned = S("o_turned")
        o_ready = S("o_ready")
        proj_done = S("proj_done")
        x_shifted = S("x_shifted")
        x_added = S("x_added")
        eo_done = S("eo_done")
        eo_added = S("eo_added")
        eb_done = S("eb_done")
        fused_done = S("fused_done")
        fused_padded = S("fused_padded")
        dw7_acc = S("dw7_acc")
        dw7_done = S("dw7_done")
        dw7_out = S("dw7_out")
        g0_ready = S("g0_ready")
        pw0_done = S("pw0_done")
        g1_ready = S("g1_ready")
        pw1_done = S("pw1_done")
        g2_ready = S("g2_ready")
        out2_done = S("out2_done")
        x_after_l2 = S("x_after_l2")
        xp_ready = S("xp_ready")
        qk_done = S("qk_done")
        qk_ready = S("qk_ready")
        v_ready = S("v_ready")
        qm_ready = S("qm_ready")
        lg_done = S("lg_done")
        lg_max = S("lg_max")
        rep_ready = S("rep_ready")
        rep_exp = S("rep_exp")
        pr_ready = S("pr_ready")
        pt_done = S("pt_done")
        pt_ready = S("pt_ready")
        pv_done = S("pv_done")
        po_ready = S("po_ready")
        po_turned = S("po_turned")
        ot_ready = S("ot_ready")
        ot_turned = S("ot_turned")
        oc_ready = S("oc_ready")
        wo_done = S("wo_done")
        x_after_attn = S("x_after_attn")
        had_done = S("had_done")
        had_copied = S("had_copied")
        had_sq = S("had_sq")
        ss_done = S("ss_done")
        ms_ready = S("ms_ready")
        std_ready = S("std_ready")
        x_after_had = S("x_after_had")
        gate_done = S("gate_done")
        upp_done = S("upp_done")
        silu_done = S("silu_done")
        gu_ready = S("gu_ready")
        gus_pool = S("gus_pool")
        gus_ready = S("gus_ready")
        moe_done = S("moe_done")
        x_final = S("x_final")
        xf_turned = S("xf_turned")
        xf_ready = S("xf_ready")
        stored = S("stored")

        pass_sems = range(borders5.num, stored.num + 1)

        def next_pass(eng, name):
            eng.drain().then_inc(pass_end, 1)
            eng.wait_ge(pass_go[name], 1)
            eng.sem_clear(pass_go[name])
        block = ctx.enter_context(nc.Block())

        def ln_index(n, s):
            return 2 * n + s + 1

        @block.sync
        def _(sp):
            sp.dma_start(packs["first"][:], a["first"]).then_inc(first_in, 16)
            sp.dma_start(beta_w, a["beta_w"]).then_inc(beta_in, 16)
            with sp.Fori(0, PASSES) as p:
                for s in range(SLOTS):
                    src = a["x"][:, bass.ds((p * SLOTS + s) * IMGS, IMGS), :]
                    sp.dma_start(XC[s], src).then_inc(x_loaded[s], 16)
                for s in range(SLOTS):
                    sp.wait_ge(combT_ready, s + 1)
                    sp.dma_start(comb_dram[s], combT[s][:]).then_inc(comb_stored[s], 16)
                    sp.wait_ge(comb_stored[s], 16)
                    sp.dma_start(CB[s], comb_dram[s].partition_broadcast(P)).then_inc(comb_rows[s], 16)
                for s in range(SLOTS):
                    sp.wait_ge(combT_ready, 5 + s)
                    sp.dma_start(comb_dram[s], combT[s][:]).then_inc(comb_stored[s], 16)
                    sp.wait_ge(comb_stored[s], 32)
                    for d in range(2):
                        src = comb_dram[s].rearrange("(i d) n -> d i n", d=2)[d]
                        sp.dma_start(CBP[s][64 * d:64 * d + 64], src.partition_broadcast(64))\
                          .then_inc(comb_rows[s], 16)
                for s in range(SLOTS):
                    sp.wait_ge(xf_ready, s + 1)
                    dst = a["out"][:, bass.ds((p * SLOTS + s) * IMGS, IMGS), :]
                    sp.dma_start(dst, XC[s]).then_inc(stored, 16)
                sp.wait_ge(stored, 32)
                sp.wait_ge(pass_end, 4)
                sp.sem_clear(pass_sems)
                sp.sem_clear(pass_end)
                for g in pass_go.values():
                    sp.sem_inc(g, 1)

        @block.gpsimd
        def _(pool):
            def link(ins):
                steps[0] += 1
                ins.then_inc(pool_step, 1)
                pool.wait_ge(pool_step, steps[0])
            steps = [0]
            g = nc.gpsimd
            g.memset(ones[:], 1.0).then_inc(consts, 1)
            g.memset(mhalf[:], -0.5).then_inc(consts, 1)
            g.memset(phalf[:], 0.5).then_inc(consts, 1)
            g.memset(sixteenth[:], 1.0 / 16).then_inc(consts, 1)
            pool.wait_ge(first_in, 16)
            link(g.tensor_scalar(bncol[:, 0:1], bn[:, 3:4], 1e-5, None, ALU.add))
            pool.wait_ge(consts, 4)
            link(g.tensor_tensor(bncol[:, 1:2], bncol[:, 0:1], mhalf[:, 0:1], ALU.pow))
            g.tensor_tensor(bncol[:, 2:3], bncol[:, 1:2], bn[:, 0:1], ALU.mult).then_inc(pool_setup, 1)
            pool.wait_ge(dve_setup, 2)
            for i, (m, h) in enumerate(UP_PARTS):
                last = g.tensor_tensor(upw[:, i, :].rearrange("p (r x) -> p r x", r=ROWS_M),
                                       upA[:, h, ROWS_M * m:ROWS_M * m + ROWS_M].unsqueeze(2)
                                       .to_broadcast([P, ROWS_M, UP]),
                                       upB[:].unsqueeze(1).to_broadcast([P, ROWS_M, UP]), ALU.mult)
            last.then_inc(pool_setup, 1)

            def ln_pow(n, slots=range(SLOTS)):
                for s in slots:
                    pool.wait_ge(ln_var, ln_index(n, s))
                    g.tensor_tensor(lnrs[s][:], lnve[s][:], mhalf[:], ALU.pow).then_inc(ln_rstd, 1)

            def new_steps():
                if steps[0]:
                    pool.wait_ge(pool_step, steps[0])
                pool.sem_clear(pool_step)
                steps[0] = 0

            new_steps()
            with pool.Fori(0, PASSES) as p:
                ln_pow(0)
                ln_pow(1)
                for i in range(3):
                    for t in range(L1_PE):
                        o = L1_TAPS - L1_PE + t
                        last = g.tensor_scalar(w5[:, i, t, :], pw1T[:, i, :], dw1[:, i, o:o + 1],
                                               None, ALU.mult)
                last.then_inc(tap_mats, 1)
                for i in range(2):
                    for t in range(L2_PE):
                        o = L2_TAPS - L2_PE + t
                        last = g.tensor_scalar(w7[:, i, t, :], ident[:], dw2[:, i, o:o + 1],
                                               None, ALU.mult)
                last.then_inc(tap_mats, 1)
                for s in range(SLOTS):
                    for i in range(3):
                        last = g.memset(P5[s][i][:], 0.0)
                last.then_inc(borders5, 1)
                ln_pow(2, [0])
                pool.wait_ge(ffn_added, 2)
                for s in range(SLOTS):
                    for gg in range(2):
                        last = g.memset(KV[s][gg][:, :, 256:257], 1.0)
                last.then_inc(borders5, 1)
                ln_pow(2, [1])
                pool.wait_ge(later_in, 16)
                pool.wait_ge(act_setup, 4)
                for s in range(SLOTS):
                    pool.wait_ge(xt_ready, ln_index(2, s))
                    for t in range(TILES):
                        last = g.tensor_tensor(X[s][:, t, :], X[s][:, t, :], bnrow[:, 1, :], ALU.add)
                    last.then_inc(x_shifted, 1)
                for k in range(6):
                    pool.wait_ge(dw5_first, k + 1)
                    for t in range(L1_POOL - 1):
                        n = (L1_POOL - 1) * k + t + 1
                        pool.wait_ge(dw5_prod, n)
                        if t > 0:
                            pool.wait_ge(dw5_padd, n - 1)
                        g.tensor_tensor(AP5[k % 2], AP5[k % 2], PROD5[n % RING], ALU.add)\
                         .then_inc(dw5_padd, 1)
                ln_pow(3)
                pool.wait_ge(x_added, 2)
                for s in range(SLOTS):
                    for i in range(2):
                        last = g.memset(P7[s][i][:], 0.0)
                last.then_inc(borders7, 1)
                ln_pow(4)
                for k in range(4):
                    pool.wait_ge(dw7_first, k + 1)
                    m = P if k % 2 == 1 else 96
                    for t in range(L2_POOL - 1):
                        n = (L2_POOL - 1) * k + t + 1
                        pool.wait_ge(dw7_prod, n)
                        if t > 0:
                            pool.wait_ge(dw7_padd, n - 1)
                        g.tensor_tensor(AP7[k % 2][0:m], AP7[k % 2][0:m], PROD7[n % RING][0:m], ALU.add)\
                         .then_inc(dw7_padd, 1)
                ln_pow(5)
                for s in range(SLOTS):
                    pool.wait_ge(xt_ready, ln_index(5, s))
                    for t in range(TILES):
                        last = g.tensor_tensor(X[s][:, t, :], X[s][:, t, :], bo[:], ALU.add)
                    last.then_inc(x_shifted, 1)
                pool.wait_ge(x_after_l2, 2)
                for s in range(SLOTS):
                    link(g.memset(Vh[s], 0.0))
                    last = g.memset(Vh[s][:, :, :, HD:HD + 1], 1.0)
                last.then_inc(v_ones, 1)

                def mask_queries(hh):
                    s, h = divmod(hh, HEADS)
                    if h == 0:
                        pool.wait_ge(qk_ready, 2 * s + 1)
                    if hh >= 3:
                        pool.wait_ge(lg_done, 2 * (hh - 3) + 2)
                    g.tensor_scalar(QM[hh % 3], Qc[s], headmask2[:, h:h + 1], float(C) ** -0.5,
                                    ALU.mult, ALU.mult).then_inc(qm_ready, 1)
                mask_queries(0)
                mask_queries(1)
                for c in range(UNITS):
                    if c % 2 == 0 and c // 2 + 2 < SLOTS * HEADS:
                        mask_queries(c // 2 + 2)
                    pool.wait_ge(rep_exp, c + 1)
                    if c >= 2:
                        pool.wait_ge(pt_done, c - 1)
                    g.tensor_tensor(PR[c % 2], E1[c % 2], E2[c % 2], ALU.subtract).then_inc(pr_ready, 1)
                    if c == 27:
                        ln_pow(6, [0])

                def std(s):
                    pool.wait_ge(ms_ready, s + 1)
                    g.tensor_tensor(hst[s][:, 2, :], hst[s][:, 1, :], phalf[:], ALU.pow).then_inc(std_ready, 1)
                std(0)
                ln_pow(6, [1])
                ln_pow(7, [0])
                std(1)
                ln_pow(7, [1])
                for s in range(SLOTS):
                    pool.wait_ge(comb_rows[s], 48)
                    for i in range(2):
                        pool.wait_ge(gu_ready, 5 * s + i + 1)
                        g.tensor_tensor(GU[s][i], GU[s][i], CBP[s][:, i, :], ALU.mult).then_inc(gus_pool, 1)
                new_steps()
                next_pass(pool, "pool")

        @block.scalar
        def _(act):
            A = nc.scalar.activation
            act.wait_ge(first_in, 16)
            nc.scalar.dma_start(packs["stage1"][:], a["stage1"]).then_inc(stage1_in, 16)
            nc.scalar.dma_start(packs["later"][:], a["later"]).then_inc(later_in, 16)
            act.wait_ge(pe_setup, 1)
            A(modr[:], TR[0][0:16, 0:16], ACT.Copy).then_inc(act_setup, 1)
            act.wait_ge(pe_setup, 2)
            A(modb[:], TR[1][:, 0:16], ACT.Copy).then_inc(act_setup, 1)
            act.wait_ge(pe_setup, 5)
            A(bnrow[:].rearrange("p g c -> p (g c)"), M[0][:, 0:256], ACT.Copy).then_inc(act_setup, 1)
            A(bt[:], M[1][0:E, 0:C], ACT.Copy).then_inc(act_setup, 1)
            def ln_copy(n, s):
                act.wait_ge(xt_turned, ln_index(n, s) - 2)
                A(XN[s][:], TR[s][:], ACT.Copy).then_inc(xn_ready, 1)

            def router_act(r, s):
                act.wait_ge(router_shifted, 2 * r + s + 1)
                A(rt[s][:, 1], rt[s][:, 0], ACT.Exp).then_inc(router_exp, 1)

            def comb_copy(r, s):
                act.wait_ge(comb_turned, 2 * r + s + 1)
                A(combT[s][:], TR[s][0:E, :], ACT.Copy).then_inc(combT_ready, 1)

            with act.Fori(0, PASSES) as p:
                for s in range(SLOTS):
                    act.wait_ge(x_turned, s + 1)
                    A(X[s][:].rearrange("p t c -> p (t c)"), TR[s][:], ACT.Copy).then_inc(x_in, 1)
                for s in range(SLOTS):
                    for m in range(7):
                        c = 7 * s + m
                        act.wait_ge(up_leaky, c + 1)
                        if c >= 3:
                            act.wait_ge(up_clipped, c - 2)
                        A(Zb[c % 3][0:PM, :], Z[c % 3][0:PM, :], ACT.Copy, scale=float(np.sqrt(2.0)))\
                            .then_inc(up_gained, 1)
                act.wait_ge(stage1_in, 16)
                for s in range(SLOTS):
                    ln_copy(1, s)
                for s in range(SLOTS):
                    router_act(0, s)
                for c in range(SLOTS * E * 4):
                    d = c // 4
                    if c == 4 * (E + 4):
                        ln_copy(2, 0)
                    act.wait_ge(ffn_up_done, c + 1)
                    if d >= 2:
                        act.wait_ge(ffn_down_done, d - 1)
                    A(H[d % 2][c % 4], M[c % 3][:], ACT.Gelu, bias=b1[:, c % 32:c % 32 + 1])\
                        .then_inc(ffn_gelu_done, 1)
                    if c == 7:
                        for s in range(SLOTS):
                            comb_copy(0, s)
                act.wait_ge(later_in, 16)

                def pad5(s):
                    if s == 1:
                        ln_copy(2, 1)
                    act.wait_ge(borders5, 1 + s)
                    for i in range(3):
                        k = 3 * s + i + 1
                        act.wait_ge(qkv_done, k)
                        if i == 0:
                            A(Q1[s], M[0][:], ACT.Relu)
                        A(P5[s][i][:, :, L1_PAD:L1_PAD + SIDE, L1_PAD:L1_PAD + SIDE],
                          M[i][:].rearrange("p (b y x) -> p b y x", b=IMGS, y=SIDE),
                          ACT.Copy).then_inc(qkv_padded, 1)
                    act.wait_ge(borders5, 2)
                    for h in range(2):
                        act.wait_ge(kvpx_done, 2 * s + h + 1)
                        src = M[3 + h][:].rearrange("p (t c) -> p t c", t=2)
                        A(KV[s][0][:, 2 * h:2 * h + 2, 0:128], src[:, :, 0:128], ACT.Relu)\
                            .then_inc(kvpx_k, 1)
                        A(KV[s][0][:, 2 * h:2 * h + 2, 128:256], src[:, :, 128:256], ACT.Copy)\
                            .then_inc(kvpx_v, 1)

                def products5(k):
                    s, i = divmod(k, 3)
                    for t in range(L1_POOL):
                        dy, dx = divmod(L1_DVE + t, 5)
                        win = P5[s][i][:, :, dy:dy + SIDE, dx:dx + SIDE]
                        col = dw1[:, i, L1_DVE + t:L1_DVE + t + 1]
                        if t == 0:
                            if k >= 2:
                                act.wait_ge(dw5_acc, k - 1)
                            A(AP5[k % 2].rearrange("p (b y x) -> p b y x", b=IMGS, y=SIDE), win,
                              ACT.Copy, scale=col).then_inc(dw5_first, 1)
                        else:
                            n = (L1_POOL - 1) * k + t
                            if n > RING:
                                act.wait_ge(dw5_padd, n - RING)
                            A(PROD5[n % RING].rearrange("p (b y x) -> p b y x", b=IMGS, y=SIDE), win,
                              ACT.Copy, scale=col).then_inc(dw5_prod, 1)
                for s in range(SLOTS):
                    pad5(s)
                    act.wait_ge(qkv_padded, 3 * s + 3)
                    if s == 0:
                        products5(0)
                for k in range(7):
                    if 0 < k < 6:
                        products5(k)
                    if k > 0:
                        act.wait_ge(dw5_done, k)
                        s, i = divmod(k - 1, 3)
                        dst = [Q2[s], KVC[s][0], KVC[s][1]][i]
                        A(dst, M[BANK5[i]][:], ACT.Copy if i == 2 else ACT.Relu).then_inc(dw5_out, 1)
                    if k in (4, 6):
                        s = k // 2 - 2
                        for g in range(2):
                            act.wait_ge(agg_turned, 2 * s + g + 1)
                            A(KV[s][1][:, :, 128 * g:128 * g + 128],
                              M[2 + g][:].rearrange("p (t c) -> p t c", t=TILES), ACT.Copy)\
                                .then_inc(agg_px, 1)
                            if s == 1:
                                act.wait_ge(o_turned, g + 1)
                                A(OC[0][g], [M[4], TR[0]][g][:], ACT.Copy).then_inc(o_ready, 1)
                for g in range(2):
                    act.wait_ge(o_turned, 2 + g + 1)
                    A(OC[1][g], [M[5], TR[1]][g][:], ACT.Copy).then_inc(o_ready, 1)
                for s in range(SLOTS):
                    ln_copy(3, s)
                for s in range(SLOTS):
                    router_act(1, s)
                for s in range(SLOTS):
                    comb_copy(1, s)
                act.wait_ge(borders7, 1)

                def pad7(s):
                    ln_copy(4, s)
                    for i in range(2):
                        act.wait_ge(fused_done, 3 * s + i + 1)
                        n = P if i == 0 else 96
                        A(P7[s][i][0:n, :, L2_PAD:L2_PAD + SIDE, L2_PAD:L2_PAD + SIDE],
                          M[4 + i][0:n, :].rearrange("p (b y x) -> p b y x", b=IMGS, y=SIDE),
                          ACT.Identity, bias=bin_[0:n, i:i + 1]).then_inc(fused_padded, 1)
                    act.wait_ge(fused_done, 3 * s + 3)
                    A(PA[s][64:96, :], M[3][64:96, :], ACT.Identity, bias=bpa[64:96, :])\
                        .then_inc(fused_padded, 1)

                def products7(k):
                    s, i = divmod(k, 2)
                    m = P if i == 1 else 96
                    for t in range(L2_POOL):
                        dy, dx = divmod(L2_DVE + t, 7)
                        win = P7[s][1 - i][0:m, :, dy:dy + SIDE, dx:dx + SIDE]
                        col = dw2[0:m, 1 - i, L2_DVE + t:L2_DVE + t + 1]
                        if t == 0:
                            if k >= 2:
                                act.wait_ge(dw7_acc, k - 1)
                            A(AP7[k % 2][0:m].rearrange("p (b y x) -> p b y x", b=IMGS, y=SIDE), win,
                              ACT.Copy, scale=col).then_inc(dw7_first, 1)
                        else:
                            n = (L2_POOL - 1) * k + t
                            if n > RING:
                                act.wait_ge(dw7_padd, n - RING)
                            A(PROD7[n % RING][0:m].rearrange("p (b y x) -> p b y x", b=IMGS, y=SIDE), win,
                              ACT.Copy, scale=col).then_inc(dw7_prod, 1)
                for s in range(SLOTS):
                    pad7(s)
                    act.wait_ge(fused_padded, 3 * s + 3)
                    if s == 0:
                        products7(0)
                for k in range(5):
                    if 0 < k < 4:
                        products7(k)
                    if k > 0:
                        act.wait_ge(dw7_done, k)
                        s, i = divmod(k - 1, 2)
                        n = P if i == 1 else 96
                        A(D7[s][i][0:n, :], M[i][0:n, :], ACT.Identity, bias=dwb2[0:n, 1 - i:2 - i])\
                            .then_inc(dw7_out, 1)
                for s in range(SLOTS):
                    ln_copy(5, s)

                def project_copy(s, i):
                    act.wait_ge(qk_done, 3 * s + i + 1)
                    A([Qc, Kc][i][s], M[2][:], ACT.Identity, bias=bqk[:, i:i + 1]).then_inc(qk_ready, 1)

                def lg_copy(c):
                    act.wait_ge(lg_done, c + 1)
                    if c >= 3:
                        act.wait_ge(rep_ready, c - 2)
                    A(LG[c % 3], M[c % 2][:], ACT.Copy).then_inc(lg_copied, 1)

                def pt_copy(c):
                    act.wait_ge(pt_done, c + 1)
                    if c >= 5:
                        act.wait_ge(pv_done, (c - 5) // 4 + 1)
                    A(PT[c % 5], M[3 + c % 2][:], ACT.Copy).then_inc(pt_ready, 1)

                def po_copy(s, g):
                    act.wait_ge(pv_done, 4 * s + 2 * g + 2)
                    if s == 1:
                        act.wait_ge(po_turned, g + 1)
                    A(PO[g], [M[5], TR[s]][g][:], ACT.Copy).then_inc(po_ready, 1)

                def oc_copy(s):
                    act.wait_ge(ot_turned, s + 1)
                    A(OCf[s], M[2][:], ACT.Copy).then_inc(oc_ready, 1)

                def had_copy(s):
                    act.wait_ge(had_done, s + 1)
                    A(HS[s], M[3 * s][:], ACT.Copy).then_inc(had_copied, 1)
                    for j in range(IMGS):
                        last = A(HQ[s][:, HW * j:HW * j + HW], M[3 * s][:, HW * j:HW * j + HW],
                                 ACT.Square, accum_out=hst[s][:, 0, j:j + 1])
                    last.then_inc(had_sq, 1)
                project_copy(0, 0)
                project_copy(0, 1)
                lg_copy(0)
                for c in range(UNITS):
                    if c + 1 < UNITS:
                        lg_copy(c + 1)
                    act.wait_ge(lg_max, c + 1)
                    if c >= 2:
                        act.wait_ge(pr_ready, c - 1)
                    for q in range(2):
                        A(E1[c % 2][:, q * 256:q * 256 + 256], LG[c % 3][:, q * 256:q * 256 + 256],
                          ACT.Exp, bias=nmx[c % 4][:, q:q + 1])
                    act.wait_ge(rep_ready, c + 1)
                    for q in range(2):
                        last = A(E2[c % 2][:, q * 256:q * 256 + 256], REP[c % 2][:, q * 256:q * 256 + 256],
                                 ACT.Exp, bias=nmx[c % 4][:, q:q + 1])
                    last.then_inc(rep_exp, 1)
                    if c >= 1:
                        pt_copy(c - 1)
                    if c in (8, 9):
                        project_copy(1, c - 8)
                    if c == 9:
                        po_copy(0, 0)
                    if c == 17:
                        po_copy(0, 1)
                    if c == 23:
                        oc_copy(0)
                    if c == 25:
                        po_copy(1, 0)
                    if c == 30:
                        ln_copy(6, 0)
                    if c == 31:
                        had_copy(0)
                pt_copy(UNITS - 1)
                po_copy(1, 1)
                oc_copy(1)
                ln_copy(6, 1)
                had_copy(1)
                for s in range(SLOTS):
                    ln_copy(7, s)
                for s in range(SLOTS):
                    router_act(2, s)
                for c in range(10):
                    n = P if c % 5 < 4 else 64
                    act.wait_ge(gate_done, c + 1)
                    if c >= 2:
                        act.wait_ge(gu_ready, c - 1)
                    A(SG[c % 2][0:n, :], M[c % 2][0:n, :], ACT.Silu).then_inc(silu_done, 1)
                    if c == 1:
                        for s in range(SLOTS):
                            comb_copy(2, s)
                for s in range(SLOTS):
                    act.wait_ge(xf_turned, s + 1)
                    A(XC[s].rearrange("p b n -> p (b n)"), TR[s][:], ACT.Copy).then_inc(xf_ready, 1)
                next_pass(act, "act")

        @block.vector
        def _(dve):
            v = nc.vector
            steps = [0]

            def link(ins):
                steps[0] += 1
                ins.then_inc(dve_step, 1)
                dve.wait_ge(dve_step, steps[0])

            def mark(ins):
                steps[0] += 1
                ins.then_inc(dve_step, 1)
                return steps[0]

            def after(k):
                dve.wait_ge(dve_step, k)

            done = [0] * SLOTS

            def begin(s, ins):
                done[s] = mark(ins)

            def in_turn(op, slots=range(SLOTS)):
                for s in slots:
                    after(done[s])
                    done[s] = mark(op(s))

            dve.wait_ge(first_in, 16)
            v.tensor_reduce(inssum[:], ins[:], AX.X, ALU.add).then_inc(dve_setup, 1)

            def filters(lo, n, f):
                for t in range(TAPS):
                    k = mark(v.tensor_scalar(picked[:, (lo * TAPS + t * n):(lo * TAPS + t * n + n)],
                                             W["tap_no"][:, lo:lo + n], float(t),
                                             taps[:, f * TAPS + t:f * TAPS + t + 1], ALU.is_equal, ALU.mult))
                after(k)
                dst = filt[:, lo:lo + n]
                return v.tensor_reduce(dst, picked[:, lo * TAPS:(lo + n) * TAPS].rearrange("p (t n) -> p n t", t=TAPS),
                                       AX.X, ALU.add)
            link(filters(0, N_UP, 0))
            v.tensor_scalar(upB, upB, 4.0, None, ALU.mult).then_inc(dve_setup, 1)
            dve.wait_ge(pool_setup, 1)
            link(v.tensor_tensor(bncol[:, 3:4], bn[:, 2:3], bncol[:, 2:3], ALU.mult))
            link(v.tensor_tensor(bncol[:, 0:1], bn[:, 1:2], bncol[:, 3:4], ALU.subtract))
            v.tensor_scalar(bndiag[:, 0, :], ident[:], bncol[:, 2:3], None, ALU.mult)
            v.tensor_scalar(bndiag[:, 1, :], ident[:], bncol[:, 0:1], None, ALU.mult).then_inc(dve_setup, 1)
            dve.wait_ge(pe_setup, 3)
            dve.wait_ge(act_setup, 2)
            link(v.tensor_scalar(btd[:], M[2][:, 0:E], 1.0 / 16, None, ALU.mult))
            link(v.tensor_tensor(exp_bT[:], exp_bT[:], modb[:, 8:16], ALU.mult))
            v.tensor_tensor(btd[:], btd[:], exp_bT[:], ALU.add).then_inc(dve_setup, 1)
            link(filters(N_UP, N_DN, 1))
            for i in range(len(DOWN_PARTS)):
                last = v.tensor_tensor(downw[:, i, :].rearrange("p (j x) -> p j x", j=8),
                                       dnA[:, i, :].unsqueeze(2).to_broadcast([P, 8, SIDE]),
                                       dnB.unsqueeze(1).to_broadcast([P, 8, SIDE]), ALU.mult)
            last.then_inc(dve_setup, 1)

            def ln_stats(n, s):
                for t in range(TILES):
                    k = mark(v.bn_stats(lnst[s][:, t, :], X[s][:, t, :]))
                for t in range(TILES):
                    after(k - TILES + 1 + t)
                    k2 = mark(v.bn_aggr(lnmv[s][:, t, :], lnst[s][:, t, :]))
                after(k2)
                v.tensor_scalar(lnve[s][:], lnmv[s][:, :, 1], LN_EPS[n], None, ALU.add).then_inc(ln_var, 1)

            def ln_apply(n, s):
                dve.wait_ge(ln_rstd, ln_index(n, s))
                for t in range(TILES):
                    last = v.tensor_scalar(XT[s][:, t, :], X[s][:, t, :], lnmv[s][:, t, 0:1], lnrs[s][:, t:t + 1],
                                           ALU.subtract, ALU.mult)
                last.then_inc(xt_ready, 1)

            def router(r, gamma=None, renorm=False):
                R = lambda s, i: rt[s][:, i]
                q = lambda s, i: rs1[s][:, i]
                wide = lambda t: t.unsqueeze(2).to_broadcast([P, TILES, E])
                pk = pick[:].unsqueeze(1).to_broadcast([P, TILES, E])
                lg = lambda s: TR[s][:, 0:TILES * E].rearrange("p (t e) -> p t e", t=TILES)
                for s in range(SLOTS):
                    dve.wait_ge(logits_done, 2 * r + s + 1)
                    if gamma is None:
                        first = v.tensor_copy(R(s, 2), lg(s))
                    else:
                        first = v.tensor_tensor(R(s, 2), lg(s), gamma.unsqueeze(1).to_broadcast([P, TILES, E]),
                                                ALU.add)
                    begin(s, first)
                in_turn(lambda s: v.tensor_reduce(q(s, 0), R(s, 2), AX.X, ALU.max))
                for s in range(SLOTS):
                    after(done[s])
                    v.tensor_tensor(R(s, 0), R(s, 2), wide(q(s, 0)), ALU.subtract).then_inc(router_shifted, 1)
                for s in range(SLOTS):
                    dve.wait_ge(router_exp, 2 * r + s + 1)
                    begin(s, v.tensor_reduce(q(s, 1), R(s, 1), AX.X, ALU.add))
                in_turn(lambda s: v.reciprocal(q(s, 2), q(s, 1)))
                in_turn(lambda s: v.tensor_tensor(R(s, 3), R(s, 1), wide(q(s, 2)), ALU.mult))
                for i in range(2):
                    src = 3 if i == 0 else 7
                    in_turn(lambda s: v.tensor_reduce(q(s, 3 + i), R(s, src), AX.X, ALU.max))
                    in_turn(lambda s: v.tensor_tensor(R(s, 4), R(s, src), wide(q(s, 3 + i)), ALU.is_equal))
                    in_turn(lambda s: v.tensor_tensor(R(s, 4), R(s, 4), pk, ALU.mult))
                    in_turn(lambda s: v.tensor_reduce(q(s, 5), R(s, 4), AX.X, ALU.max))
                    in_turn(lambda s: v.tensor_tensor(R(s, 5 + i), R(s, 4), wide(q(s, 5)), ALU.is_equal))
                    if i == 0:
                        in_turn(lambda s: v.scalar_tensor_tensor(R(s, 7), R(s, 5), -2.0, R(s, 3), ALU.mult, ALU.add))
                in_turn(lambda s: v.tensor_tensor(R(s, 5), R(s, 5), R(s, 6), ALU.add))
                if renorm:
                    in_turn(lambda s: v.tensor_tensor(q(s, 6), q(s, 3), q(s, 4), ALU.add))
                    in_turn(lambda s: v.tensor_scalar(q(s, 6), q(s, 6), 1e-6, None, ALU.add))
                    in_turn(lambda s: v.reciprocal(q(s, 7), q(s, 6)))
                    in_turn(lambda s: v.tensor_tensor(R(s, 3), R(s, 3), wide(q(s, 7)), ALU.mult))
                for s in range(SLOTS):
                    after(done[s])
                    v.tensor_tensor(comb[s][:], R(s, 3), R(s, 5), ALU.mult).then_inc(comb_ready, 1)

            def new_steps():
                if steps[0]:
                    after(steps[0])
                dve.sem_clear(dve_step)
                steps[0] = 0

            new_steps()
            with dve.Fori(0, PASSES) as p:
                for s in range(SLOTS):
                    dve.wait_ge(x_in, s + 1)
                    ln_stats(0, s)
                for s in range(SLOTS):
                    ln_apply(0, s)
                for c in range(14 + 2):
                    if c < 14:
                        dve.wait_ge(up_done, c + 1)
                        if c >= 3:
                            dve.wait_ge(up_gained, c - 2)
                        v.tensor_tensor(Z[c % 3][0:PM, :].rearrange("p (k c) -> p k c", k=4),
                                        M[c % 3][0:PM, :].rearrange("p (k c) -> p k c", k=4),
                                        conv_bias[0:PM, :].unsqueeze(1).to_broadcast([PM, 4, C]),
                                        ALU.add).then_inc(up_biased, 1)
                        dve.wait_ge(up_biased, c + 1)
                        v.scalar_tensor_tensor(Z[c % 3][0:PM, :], Z[c % 3][0:PM, :], 0.2, Z[c % 3][0:PM, :],
                                               ALU.mult, ALU.max).then_inc(up_leaky, 1)
                    if c >= 2:
                        s, m = divmod(c - 2, 7)
                        dve.wait_ge(up_gained, c - 1)
                        v.tensor_scalar(Y[s][0:PM, 2 * m:2 * m + 2, :],
                                        Zb[(c - 2) % 3][0:PM, :].rearrange("p (m n) -> p m n", m=2),
                                        256.0, -256.0, ALU.min, ALU.max).then_inc(up_clipped, 1)
                for s in range(SLOTS):
                    dve.wait_ge(down_done, s + 1)
                    xv = X[s][:].rearrange("p (j h) c -> p h j c", h=2)
                    v.tensor_tensor(xv, xv, M[3 + s][:].rearrange("p (h j c) -> p h j c", h=2, j=IMGS),
                                    ALU.add).then_inc(x_after_conv, 1)
                    dve.wait_ge(x_after_conv, s + 1)
                    ln_stats(1, s)
                for s in range(SLOTS):
                    ln_apply(1, s)
                dve.wait_ge(stage1_in, 16)
                router(0, renorm=True)
                for s in range(SLOTS):
                    acc = XT[s][:].rearrange("p t c -> p (t c)")
                    dve.wait_ge(comb_rows[s], 16)
                    for e in range(E):
                        d = E * s + e
                        dve.wait_ge(ffn_down_done, d + 1)
                        k1 = mark(v.scalar_tensor_tensor(acc if e == 0 else YS[e % 2], M[[3, 5][d % 2]][:],
                                                         b2T[:, e:e + 1], CB[s][:, e, :], ALU.add, ALU.mult))
                        after(k1)
                        v.nop().then_inc(ffn_scaled, 1)
                        if e == E - 1:
                            v.tensor_tensor(acc, acc, YS[e % 2], ALU.add).then_inc(ffn_added, 1)
                        elif e > 0:
                            link(v.tensor_tensor(acc, acc, YS[e % 2], ALU.add))
                    dve.wait_ge(ffn_turned, s + 1)
                    xf = X[s][:].rearrange("p t c -> p (t c)")
                    v.tensor_tensor(xf, xf, TR[s][:], ALU.add).then_inc(x_after_ffn, 1)
                    dve.wait_ge(x_after_ffn, s + 1)
                    ln_stats(2, s)
                    ln_apply(2, s)
                dve.wait_ge(later_in, 16)
                dve.wait_ge(act_setup, 4)
                def taps5(k):
                    s, i = divmod(k, 3)
                    dve.wait_ge(qkv_padded, k + 1)
                    if k >= 2:
                        dve.wait_ge(dw5_done, k - 1)
                    for t in range(L1_DVE):
                        dy, dx = divmod(t, 5)
                        for b in range(IMGS):
                            win = P5[s][i][:, b, dy:dy + SIDE, dx:dx + SIDE]
                            acc = A5[k % 2][:, b]
                            if t == 0:
                                kk = mark(v.tensor_scalar(acc, win, dw1[:, i, 0:1], None, ALU.mult))
                            else:
                                after(kk - 1)
                                kk = mark(v.scalar_tensor_tensor(acc, win, dw1[:, i, t:t + 1], acc,
                                                                 ALU.mult, ALU.add))
                    after(kk)
                    dve.wait_ge(dw5_padd, (L1_POOL - 1) * (k + 1))
                    af = A5[k % 2].rearrange("p b y x -> p (b y x)")
                    v.tensor_tensor(af, af, AP5[k % 2], ALU.add).then_inc(dw5_acc, 1)

                def mask_kv(s):
                    for g in range(2):
                        dve.wait_ge(kv_done, 2 * s + g + 1)
                        bank = TR[s] if g == 1 else M[4 + s]
                        for j in range(IMGS):
                            v.tensor_tensor(KM[s][:, g, j, 0:128], bank[:, 129 * j:129 * j + 128],
                                            headmask1[:], ALU.mult)
                            last = v.tensor_scalar(KM[s][:, g, j, 128:144],
                                                   headmask1[:, 0:128:8], bank[:, 129 * j + 128:129 * j + 129],
                                                   None, ALU.mult)
                        last.then_inc(kv_masked, 1)

                def scale_num(s, i):
                    g, h = divmod(i, 2)
                    dve.wait_ge(num_done, 4 * s + i + 1)
                    src = M[2 + i % 2][:, 0:288].rearrange("p (t c) -> p t c", t=2)
                    den = DEN[s][:, i, :].rearrange("p (t h) -> p t h", t=2)
                    link(v.tensor_scalar(den, src[:, :, 128:144], 1e-15, None, ALU.add))
                    link(v.reciprocal(den, den))
                    v.tensor_tensor(OTk[s][g][:, 256 * h:256 * h + 256].rearrange("p (t h d) -> p t h d", t=2, h=16),
                                    src[:, :, 0:128].rearrange("p t (h d) -> p t h d", h=16),
                                    den.unsqueeze(3).to_broadcast([P, 2, 16, 8]), ALU.mult)\
                     .then_inc(num_scaled, 1)

                def add_l1(s):
                    dve.wait_ge(proj_done, s + 1)
                    link(v.tensor_tensor(XT[s][:], TR[s][:].rearrange("p (t c) -> p t c", t=TILES),
                                         bnrow[:, 0, :].unsqueeze(1).to_broadcast([P, TILES, C]), ALU.mult))
                    dve.wait_ge(x_shifted, s + 1)
                    v.tensor_tensor(X[s][:], X[s][:], XT[s][:], ALU.add).then_inc(x_added, 1)
                    dve.wait_ge(x_added, s + 1)
                    ln_stats(3, s)
                for k in range(6):
                    taps5(k)
                mask_kv(0)
                for i in range(4):
                    scale_num(0, i)
                mask_kv(1)
                add_l1(0)
                for i in range(4):
                    scale_num(1, i)
                add_l1(1)
                for s in range(SLOTS):
                    ln_apply(3, s)
                router(1, gamma=modb[:, 0:8])
                for s in range(SLOTS):
                    dve.wait_ge(comb_ready, 3 + s)
                    link(v.tensor_tensor(rt[s][:, 0], comb[s][:],
                                         modb[:, 8:16].unsqueeze(1).to_broadcast([P, TILES, E]), ALU.mult))
                def add_experts(s, t2):
                    last2 = [0, 0]
                    for h in range(2):
                        c = 8 * s + 2 * t2 + 2 * h
                        dve.wait_ge(eo_done, c + 2)
                        for e in range(4):
                            for d in range(2):
                                t = t2 + d
                                if last2[d]:
                                    after(last2[d])
                                last2[d] = mark(v.scalar_tensor_tensor(
                                    X[s][:, t, :], M[(c + d) % 4][:, e * C:e * C + C],
                                    rt[s][:, 0, t, 4 * h + e:4 * h + e + 1],
                                    X[s][:, t, :], ALU.mult, ALU.add))
                        for d in range(2):
                            after(last2[d])
                        v.nop().then_inc(eo_added, 2)

                def add_bias(s):
                    dve.wait_ge(eb_done, s + 1)
                    xf = X[s][:].rearrange("p t c -> p (t c)")
                    link(v.tensor_tensor(xf, xf, TR[s][:], ALU.add))
                    ln_stats(4, s)
                add_experts(0, 0)
                add_experts(0, 2)
                add_bias(0)
                add_experts(1, 0)
                ln_apply(4, 0)
                add_experts(1, 2)
                add_bias(1)
                ln_apply(4, 1)
                def taps7(k):
                    s, i = divmod(k, 2)
                    n = P if i == 1 else 96
                    dve.wait_ge(fused_padded, 3 * s + 2)
                    if k >= 2:
                        dve.wait_ge(dw7_done, k - 1)
                    for t in range(L2_DVE):
                        dy, dx = divmod(t, 7)
                        for b in range(IMGS):
                            win = P7[s][1 - i][0:n, b, dy:dy + SIDE, dx:dx + SIDE]
                            acc = A7[k % 2][0:n, b]
                            if t == 0:
                                kk = mark(v.tensor_scalar(acc, win, dw2[0:n, 1 - i, 0:1], None, ALU.mult))
                            else:
                                after(kk - 1)
                                kk = mark(v.scalar_tensor_tensor(acc, win, dw2[0:n, 1 - i, t:t + 1], acc,
                                                                 ALU.mult, ALU.add))
                    after(kk)
                    dve.wait_ge(dw7_padd, (L2_POOL - 1) * (k + 1))
                    af = A7[k % 2][0:n].rearrange("p b y x -> p (b y x)")
                    v.tensor_tensor(af, af, AP7[k % 2][0:n], ALU.add).then_inc(dw7_acc, 1)

                def gate0(s):
                    dve.wait_ge(dw7_out, 2 * s + 1)
                    dve.wait_ge(fused_padded, 3 * s + 3)
                    v.tensor_tensor(G0[s][64:96, :], PA[s][64:96, :], D7[s][0][64:96, :], ALU.mult)\
                     .then_inc(g0_ready, 1)

                def gate1(s):
                    dve.wait_ge(pw0_done, s + 1)
                    v.scalar_tensor_tensor(G1[s][0:64, :], M[4][0:64, :], pwb0[0:64, :], D7[s][0][0:64, :],
                                           ALU.add, ALU.mult).then_inc(g1_ready, 1)

                def gate2(s):
                    dve.wait_ge(pw1_done, s + 1)
                    dve.wait_ge(dw7_out, 2 * s + 2)
                    v.scalar_tensor_tensor(G2[s], M[5][:], pwb1[:], D7[s][1], ALU.add, ALU.mult)\
                     .then_inc(g2_ready, 1)

                def add_l2(s):
                    dve.wait_ge(out2_done, s + 1)
                    link(v.tensor_tensor(X[s][:], X[s][:], TR[s][:].rearrange("p (t c) -> p t c", t=TILES), ALU.add))
                    v.tensor_tensor(X[s][:], X[s][:], bout[:].unsqueeze(1).to_broadcast([P, TILES, C]), ALU.add)\
                     .then_inc(x_after_l2, 1)
                    dve.wait_ge(x_after_l2, s + 1)
                    ln_stats(5, s)
                taps7(0)
                taps7(1)
                gate0(0)
                taps7(2)
                gate1(0)
                taps7(3)
                gate2(0)
                gate0(1)
                gate1(1)
                add_l2(0)
                gate2(1)
                add_l2(1)
                for s in range(SLOTS):
                    ln_apply(5, s)

                def positions(s):
                    dve.wait_ge(xn_ready, ln_index(5, s) - 2)
                    if s == 1:
                        dve.wait_ge(qk_done, 3)
                    xn3 = XN[s][:].rearrange("p (b m) -> p b m", b=IMGS)
                    xq3 = XP.rearrange("p (b m) -> p b m", b=IMGS)
                    link(v.tensor_scalar(XP, XN[s][:], posw[:, 1:2], posw[:, 3:4], ALU.mult, ALU.add))
                    link(v.scalar_tensor_tensor(xq3[:, :, 1:HW], xn3[:, :, 0:HW - 1], posw[:, 0:1],
                                                xq3[:, :, 1:HW], ALU.mult, ALU.add))
                    link(v.scalar_tensor_tensor(xq3[:, :, 0:HW - 1], xn3[:, :, 1:HW], posw[:, 2:3],
                                                xq3[:, :, 0:HW - 1], ALU.mult, ALU.add))
                    v.tensor_tensor(XP, XP, XN[s][:], ALU.add).then_inc(xp_ready, 1)

                def values(s):
                    dve.wait_ge(qk_done, 3 * s + 3)
                    dve.wait_ge(v_ones, 1)
                    v.tensor_tensor(Vh[s][:, :, :, 0:HD],
                                    M[2][:].rearrange("p (t h d) -> p t h d", t=TILES, h=HEADS),
                                    bv[:].rearrange("p (h d) -> p h d", h=HEADS).unsqueeze(1)
                                    .to_broadcast([P, TILES, HEADS, HD]), ALU.add).then_inc(v_ready, 1)

                def divide(s, g):
                    dve.wait_ge(po_turned, 2 * s + g + 1)
                    src = M[2][:].rearrange("p (t h c) -> p t h c", t=TILES, h=4)
                    link(v.reciprocal(rdn[:, g], src[:, :, :, HD]))
                    v.tensor_tensor(OT[s][:, :, 4 * g:4 * g + 4, :], src[:, :, :, 0:HD],
                                    rdn[:, g].unsqueeze(3).to_broadcast([P, TILES, 4, HD]), ALU.mult)\
                     .then_inc(ot_ready, 1)

                def add_attention(s):
                    dve.wait_ge(wo_done, s + 1)
                    dve.wait_ge(x_shifted, 3 + s)
                    xf = X[s][:].rearrange("p t c -> p (t c)")
                    v.tensor_tensor(xf, xf, M[2][:], ALU.add).then_inc(x_after_attn, 1)
                    dve.wait_ge(x_after_attn, s + 1)
                positions(0)
                values(0)
                for c in range(UNITS):
                    if c == 6:
                        positions(1)
                    if c == 12:
                        values(1)
                    if c == 21:
                        divide(0, 0)
                    if c == 23:
                        divide(0, 1)
                    if c == 31:
                        divide(1, 0)
                    if c == 27:
                        add_attention(0)
                        ln_stats(6, 0)
                    if c == 30:
                        ln_apply(6, 0)
                    lg = [LG[c % 3][:, q * 256:q * 256 + 256] for q in range(2)]
                    rp = [REP[c % 2][:, q * 256:q * 256 + 256] for q in range(2)]
                    t8 = top8[c % 4]
                    dve.wait_ge(lg_copied, c + 1)
                    k0 = [mark(v.max(t8[:, q, 0:8], lg[q])) for q in range(2)]
                    k = []
                    for q in range(2):
                        after(k0[q])
                        if q == 0 and c >= 2:
                            dve.wait_ge(rep_exp, c - 1)
                        k.append(mark(v.match_replace(rp[q], t8[:, q, 0:8], lg[q], NEG)))
                    v.tensor_scalar(nmx[c % 4][:], t8[:, :, 0], -1.0, None, ALU.mult).then_inc(lg_max, 1)
                    k2 = []
                    for q in range(2):
                        after(k[q])
                        k2.append(mark(v.max(t8[:, q, 8:16], rp[q])))
                    for q in range(2):
                        after(k2[q])
                        last = v.match_replace(rp[q], t8[:, q, 8:16], rp[q], NEG)
                    last.then_inc(rep_ready, 1)
                MAGIC = 1.5 * 2.0 ** 23
                TRUST = 2.513930578568423 / 15.0
                q = lambda s, i: hst[s][:, i, :]
                half = lambda t, j: t[:, HW * j:HW * j + HW]

                def by_image(s, dst, src, s1, s2, o1, o2=None):
                    after(done[s])
                    for j in range(IMGS):
                        done[s] = mark(v.tensor_scalar(half(dst[s], j), half(src[s], j), hst[s][:, s1, j:j + 1],
                                                       None if s2 is None else hst[s][:, s2, j:j + 1],
                                                       *((o1,) if o2 is None else (o1, o2))))

                def round4(s):
                    one = [s]
                    dve.wait_ge(ss_done, s + 1)
                    v.tensor_scalar(q(s, 1), M[1][:, 2 * s:2 * s + 2], 1.0 / (C * HW), None, ALU.mult)\
                     .then_inc(ms_ready, 1)
                    dve.wait_ge(std_ready, s + 1)
                    begin(s, v.tensor_scalar(q(s, 3), q(s, 2), 2.513930578568423, 1e-8, ALU.mult, ALU.add))
                    in_turn(lambda s: v.tensor_scalar(q(s, 4), q(s, 3), 2.0 / 15.0, None, ALU.mult), one)
                    v.tensor_scalar(q(s, 7), q(s, 3), -1.0, None, ALU.mult)
                    v.tensor_scalar(q(s, 8), q(s, 2), TRUST, None, ALU.mult)
                    in_turn(lambda s: v.reciprocal(q(s, 5), q(s, 4)), one)
                    in_turn(lambda s: v.tensor_scalar(q(s, 6), q(s, 4), 0.5, None, ALU.mult), one)
                    dve.wait_ge(had_copied, s + 1)
                    by_image(s, H1, HS, 3, 7, ALU.min, ALU.max)
                    by_image(s, H1, H1, 5, None, ALU.mult)
                    in_turn(lambda s: v.tensor_scalar(H1[s], H1[s], 0.5, MAGIC, ALU.add, ALU.add), one)
                    in_turn(lambda s: v.tensor_scalar(H1[s], H1[s], -MAGIC, None, ALU.add), one)
                    by_image(s, H1, H1, 4, 6, ALU.mult, ALU.subtract)
                    in_turn(lambda s: v.tensor_tensor(H2[s], H1[s], HS[s], ALU.subtract), one)
                    in_turn(lambda s: v.scalar_tensor_tensor(H2[s], H2[s], -1.0, H2[s], ALU.mult, ALU.max), one)
                    by_image(s, H2, H2, 8, None, ALU.is_le)

                def add_rounded(s):
                    one = [s]
                    in_turn(lambda s: v.tensor_tensor(H2[s], HS[s], H2[s], ALU.mult), one)
                    in_turn(lambda s: v.tensor_tensor(H3[s], H1[s], H2[s], ALU.subtract), one)
                    in_turn(lambda s: v.tensor_tensor(H3[s], H2[s], H3[s], ALU.add), one)
                    after(done[s])
                    xf = X[s][:].rearrange("p t c -> p (t c)")
                    v.tensor_tensor(xf, xf, H3[s], ALU.add).then_inc(x_after_had, 1)
                round4(0)
                divide(1, 1)
                add_rounded(0)
                add_attention(1)
                ln_stats(6, 1)
                dve.wait_ge(x_after_had, 1)
                ln_stats(7, 0)
                ln_apply(6, 1)
                ln_apply(7, 0)
                round4(1)
                add_rounded(1)
                dve.wait_ge(x_after_had, 2)
                ln_stats(7, 1)
                ln_apply(7, 1)
                router(2)
                for s in range(SLOTS):
                    for i in range(5):
                        c = 5 * s + i
                        n = P if i < 4 else 64
                        dve.wait_ge(silu_done, c + 1)
                        dve.wait_ge(upp_done, c + 1)
                        v.tensor_tensor(GU[s][i][0:n, :], SG[c % 2][0:n, :], M[2 + c % 2][0:n, :], ALU.mult)\
                         .then_inc(gu_ready, 1)
                for s in range(SLOTS):
                    dve.wait_ge(comb_rows[s], 48)
                    for i in range(2, 4):
                        dve.wait_ge(gu_ready, 5 * s + i + 1)
                        v.tensor_tensor(GU[s][i], GU[s][i], CBP[s][:, i, :], ALU.mult).then_inc(gus_ready, 1)
                for s in range(SLOTS):
                    dve.wait_ge(moe_done, s + 1)
                    xf = X[s][:].rearrange("p t c -> p (t c)")
                    v.tensor_tensor(xf, xf, M[4 + s][:], ALU.add).then_inc(x_final, 1)
                new_steps()
                next_pass(dve, "dve")

        @block.tensor
        def _(pe):
            mm = nc.tensor.matmul
            tr = nc.tensor.transpose
            pe.wait_ge(first_in, 16)
            mm(TR[0][0:16, 0:16], ins[:], modw[:], start=True, stop=True).then_inc(pe_setup, 1)
            pe.wait_ge(act_setup, 1)
            pe.wait_ge(consts, 4)
            mm(TR[1][:, 0:16], sixteenth[:], modr[:], start=True, stop=True).then_inc(pe_setup, 1)
            pe.wait_ge(dve_setup, 1)
            pe.wait_ge(beta_in, 16)
            for e in range(E):
                last = mm(M[2][:, e:e + 1], beta_w[:, e, :], inssum[:], start=True, stop=True)
            last.then_inc(pe_setup, 1)
            pe.wait_ge(dve_setup, 3)
            mm(M[0][:, 0:256], ones[:], bndiag[:].rearrange("p g c -> p (g c)"), start=True, stop=True)\
                .then_inc(pe_setup, 1)
            pe.wait_ge(dve_setup, 4)
            tr(M[1][0:E, 0:C], btd[:], ident[:]).then_inc(pe_setup, 1)
            pe.wait_ge(act_setup, 2)

            def turn(bank, src4, sig):
                for t in range(TILES):
                    last = tr(bank[:, t * P:t * P + P], src4(t), ident[:])
                last.then_inc(sig, 1)

            def ln_turn(n, s):
                pe.wait_ge(xt_ready, ln_index(n, s))
                turn(TR[s], lambda t: XT[s][:, t, :], xt_turned)

            def logits(r, n, s, Wg):
                pe.wait_ge(xn_ready, ln_index(n, s) - 2)
                for t in range(TILES):
                    last = mm(TR[s][:, t * E:t * E + E], XN[s][:, t * P:t * P + P], Wg[:], start=True, stop=True)
                last.then_inc(logits_done, 1)

            def comb_turn(r, s):
                pe.wait_ge(comb_ready, 2 * r + s + 1)
                for t in range(TILES):
                    last = tr(TR[s][0:E, t * P:t * P + P], comb[s][:, t, :], ident[:])
                last.then_inc(comb_turned, 1)

            with pe.Fori(0, PASSES) as p:
                for s in range(SLOTS):
                    pe.wait_ge(x_loaded[s], 16)
                    turn(TR[s], lambda t: XC[s][:, t // 2, (t % 2) * P:(t % 2) * P + P], x_turned)
                def upsample(c):
                    s, m2 = divmod(c, 7)
                    xv = XT[s][:].rearrange("p (j h) c -> p h j c", h=2)
                    if m2 == 0:
                        pe.wait_ge(xt_ready, ln_index(0, s))
                    if c >= 3:
                        pe.wait_ge(up_biased, c - 2)
                    for m in (2 * m2, 2 * m2 + 1):
                        parts = [i for i, (mm_, h) in enumerate(UP_PARTS) if mm_ == m]
                        for n_, i in enumerate(parts):
                            last = mm(M[c % 3][0:PM, (m % 2) * 256:(m % 2) * 256 + 256], upw[:, i, :],
                                      xv[:, UP_PARTS[i][1]], start=n_ == 0, stop=n_ == len(parts) - 1)
                    last.then_inc(up_done, 1)

                def downsample(s, i):
                    h, k = DOWN_PARTS[i]
                    parts = [i_ for i_, (h_, k_) in enumerate(DOWN_PARTS) if h_ == h]
                    pe.wait_ge(up_clipped, 7 * s + k // 2 + 1)
                    last = mm(M[3 + s][:, h * 256:h * 256 + 256], downw[0:PM, i, :], Y[s][0:PM, k, :],
                              start=i == parts[0], stop=i == parts[-1])
                    if i == len(DOWN_PARTS) - 1:
                        last.then_inc(down_done, 1)
                pe.wait_ge(pool_setup, 2)
                pe.wait_ge(act_setup, 4)
                todo = [(s, i) for s in range(SLOTS) for i in range(len(DOWN_PARTS))]
                for c in range(14):
                    upsample(c)
                    if c == 4:
                        pe.wait_ge(dve_setup, 5)
                    while todo and c >= 4 and 7 * todo[0][0] + DOWN_PARTS[todo[0][1]][1] // 2 + DOWN_LAG <= c:
                        downsample(*todo.pop(0))
                for s, i in todo:
                    downsample(s, i)
                for s in range(SLOTS):
                    ln_turn(1, s)
                pe.wait_ge(stage1_in, 16)
                for s in range(SLOTS):
                    logits(0, 1, s, Wg0)
                def ffn_up(d):
                    s, e = divmod(d, E)
                    for hc in range(4):
                        c = 4 * d + hc
                        if c >= 3:
                            pe.wait_ge(ffn_gelu_done, c - 2)
                        mm(M[c % 3][:], W1[:, e, hc * P:hc * P + P], XN[s][:], start=True, stop=True)\
                            .then_inc(ffn_up_done, 1)

                def ffn_down(d):
                    pe.wait_ge(ffn_gelu_done, 4 * d + 4)
                    if d >= 2:
                        pe.wait_ge(ffn_scaled, d - 1)
                    for hc in range(4):
                        last = mm(M[[3, 5][d % 2]][:], W2[:, d % E, hc, :], H[d % 2][hc],
                                  start=hc == 0, stop=hc == 3)
                    last.then_inc(ffn_down_done, 1)

                def ffn_turn(s):
                    pe.wait_ge(ffn_added, s + 1)
                    pe.wait_ge(combT_ready, s + 1)
                    turn(TR[s], lambda t: XT[s][:, t, :], ffn_turned)
                ffn_up(0)
                for d in range(SLOTS * E):
                    if d + 1 < SLOTS * E:
                        ffn_up(d + 1)
                    if d == 0:
                        for s in range(SLOTS):
                            comb_turn(0, s)
                    ffn_down(d)
                    if d == E:
                        ffn_turn(0)
                    if d == E + 2:
                        ln_turn(2, 0)
                ffn_turn(1)
                pe.wait_ge(later_in, 16)
                pe.wait_ge(tap_mats, 2)
                def project5(s):
                    pe.wait_ge(xn_ready, ln_index(2, s) - 2)
                    for i in range(3):
                        if s == 1:
                            pe.wait_ge(qkv_padded, i + 1)
                        mm(M[i][:], Wqkv1[:, i, :], XN[s][:], start=True, stop=True).then_inc(qkv_done, 1)
                    for h in range(2):
                        if s == 0 and h == 0:
                            pe.wait_ge(ffn_scaled, 15)
                        if s == 1:
                            pe.wait_ge(kvpx_v, h + 1)
                        for t in range(2 * h, 2 * h + 2):
                            last = mm(M[3 + h][:, (t % 2) * 256:(t % 2) * 256 + 256],
                                      XN[s][:, t * P:t * P + P], Wqkv1[:, 1:3, :].rearrange("p i c -> p (i c)"),
                                      start=True, stop=True)
                        last.then_inc(kvpx_done, 1)

                def taps5(k):
                    s, i = divmod(k, 3)
                    if k == 0:
                        pe.wait_ge(qkv_padded, 1)
                        pe.wait_ge(ffn_scaled, 16)
                    else:
                        pe.wait_ge(qkv_padded, max(k + 1, 4 + i))
                    if s == 1:
                        pe.wait_ge(dw5_out, i + 1)
                    for t in range(L1_TAPS - L1_PE, L1_TAPS):
                        dy, dx = divmod(t, 5)
                        mm(M[BANK5[i]][:].rearrange("p (b y x) -> p b y x", b=IMGS, y=SIDE),
                           w5[:, i, t - L1_TAPS + L1_PE, :], P5[s][i][:, :, dy:dy + SIDE, dx:dx + SIDE],
                           start=t == L1_TAPS - L1_PE, stop=False)

                def close5(k):
                    i = k % 3
                    pe.wait_ge(dw5_acc, k + 1)
                    mm(M[BANK5[i]][:], pw1T[:, i, :], A5[k % 2].rearrange("p b y x -> p (b y x)"),
                       start=False, stop=True).then_inc(dw5_done, 1)
                def turn_agg(s):
                    for g in range(2):
                        pe.wait_ge(dw5_out, 3 * s + g + 2)
                        if s == 0:
                            pe.wait_ge(qkv_padded, 6)
                            pe.wait_ge(kvpx_v, 4)
                        else:
                            pe.wait_ge(num_scaled, 4)
                        turn(M[2 + g], lambda t: KVC[s][g][:, t * P:t * P + P], agg_turned)

                def kv(s):
                    for g in range(2):
                        if g == 1:
                            pe.wait_ge(agg_px, 2 * s + 2)
                        elif s == 1:
                            pe.wait_ge(dw5_out, 4)
                        bank = TR[s] if g == 1 else M[4 + s]
                        for j in range(IMGS):
                            for h in range(2):
                                t = 2 * j + h
                                last = mm(bank[:, 129 * j:129 * j + 129], KV[s][g][:, t, 0:128],
                                          KV[s][g][:, t, 128:257], start=h == 0, stop=h == 1)
                        last.then_inc(kv_done, 1)

                def num(s, i):
                    g, h = divmod(i, 2)
                    pe.wait_ge(kv_masked, 2 * s + g + 1)
                    if i < 2:
                        pe.wait_ge(agg_px, 2 * s + 2)
                    else:
                        pe.wait_ge(num_scaled, 4 * s + i - 1)
                    for t in range(2):
                        last = mm(M[2 + i % 2][:, 144 * t:144 * t + 144],
                                  [Q1, Q2][g][s][:, (2 * h + t) * P:(2 * h + t) * P + P],
                                  KM[s][:, g, h, :], start=True, stop=True)
                    last.then_inc(num_done, 1)

                def turn_o(s):
                    for g in range(2):
                        pe.wait_ge(num_scaled, 4 * s + 2 * g + 2)
                        pe.wait_ge(kv_masked, 2 * s + 2)
                        turn(TR[s] if g == 1 else M[4 + s], lambda t: OTk[s][g][:, t * P:t * P + P], o_turned)

                def project_o(s):
                    pe.wait_ge(o_ready, 2 * s + 2)
                    for t in range(TILES):
                        for g in range(2):
                            last = mm(TR[s][:, t * C:t * C + C], OC[s][g][:, t * P:t * P + P], proj[:, g, :],
                                      start=g == 0, stop=g == 1)
                    last.then_inc(proj_done, 1)
                project5(0)
                taps5(0)
                ln_turn(2, 1)
                project5(1)
                for k in range(4):
                    taps5(k + 1)
                    close5(k)
                turn_agg(0)
                taps5(5)
                kv(0)
                close5(4)
                close5(5)
                for i in range(4):
                    num(0, i)
                turn_agg(1)
                turn_o(0)
                kv(1)
                project_o(0)
                for i in range(4):
                    num(1, i)
                turn_o(1)
                project_o(1)
                for s in range(SLOTS):
                    ln_turn(3, s)
                for s in range(SLOTS):
                    logits(1, 3, s, Wg1)
                def experts(s, t2):
                    for h in range(2):
                        for d in range(2):
                            c = 8 * s + 2 * t2 + 2 * h + d
                            if c >= 4:
                                pe.wait_ge(eo_added, c - c % 2 - 2)
                            mm(M[c % 4][:], XN[s][:, (t2 + d) * P:(t2 + d) * P + P],
                               Wexp[:, 4 * h:4 * h + 4, :].rearrange("p e c -> p (e c)"),
                               start=True, stop=True).then_inc(eo_done, 1)

                def experts_bias(s):
                    comb_turn(1, s)
                    pe.wait_ge(combT_ready, 3 + s)
                    for t in range(TILES):
                        last = mm(TR[s][:, t * C:t * C + C], combT[s][:, t * P:t * P + P], bt[:],
                                  start=True, stop=True)
                    last.then_inc(eb_done, 1)

                def fuse(s):
                    pe.wait_ge(xn_ready, ln_index(4, s) - 2)
                    for i in range(3):
                        if s == 1:
                            pe.wait_ge(fused_padded, i + 1)
                        elif i == 2:
                            pe.wait_ge(eo_added, 16)
                        out = [M[4][:], M[5][0:96, :], M[3][64:96, :]][i]
                        mm(out, [Win[:, 0:128], Win[:, 128:224], Win[:, 224:256]][i], XN[s][:],
                           start=True, stop=True).then_inc(fused_done, 1)
                experts(0, 0)
                experts(0, 2)
                experts_bias(0)
                experts(1, 0)
                ln_turn(4, 0)
                experts(1, 2)
                experts_bias(1)
                fuse(0)
                def taps7(k):
                    s, i = divmod(k, 2)
                    n = P if i == 1 else 96
                    pe.wait_ge(fused_padded, 3 * s + 2)
                    if s == 1:
                        pe.wait_ge(dw7_out, i + 1)
                    for t in range(L2_TAPS - L2_PE, L2_TAPS):
                        dy, dx = divmod(t, 7)
                        mm(M[i][0:n, :].rearrange("p (b y x) -> p b y x", b=IMGS, y=SIDE),
                           w7[0:n, 1 - i, t - L2_TAPS + L2_PE, 0:n],
                           P7[s][1 - i][0:n, :, dy:dy + SIDE, dx:dx + SIDE],
                           start=t == L2_TAPS - L2_PE, stop=False)

                def close7(k):
                    n = P if k % 2 == 1 else 96
                    pe.wait_ge(dw7_acc, k + 1)
                    mm(M[k % 2][0:n, :], ident[0:n, 0:n], A7[k % 2][0:n].rearrange("p b y x -> p (b y x)"),
                       start=False, stop=True).then_inc(dw7_done, 1)
                def pw0(s):
                    pe.wait_ge(g0_ready, s + 1)
                    if s == 0:
                        pe.wait_ge(fused_padded, 6)
                    else:
                        pe.wait_ge(g1_ready, 1)
                    mm(M[4][0:64, :], pwT0[64:96, :], G0[s][64:96, :], start=True, stop=True)\
                        .then_inc(pw0_done, 1)

                def pw1(s):
                    pe.wait_ge(g1_ready, s + 1)
                    if s == 1:
                        pe.wait_ge(g2_ready, 1)
                    mm(M[5][:], pwT1[0:64, :], G1[s][0:64, :], start=True, stop=True).then_inc(pw1_done, 1)

                def out2(s):
                    pe.wait_ge(g2_ready, s + 1)
                    for t in range(TILES):
                        last = mm(TR[s][:, t * C:t * C + C], G2[s][:, t * P:t * P + P], Wout[:],
                                  start=True, stop=True)
                    last.then_inc(out2_done, 1)
                taps7(0)
                ln_turn(4, 1)
                fuse(1)
                taps7(1)
                close7(0)
                taps7(2)
                close7(1)
                pw0(0)
                taps7(3)
                pw1(0)
                close7(2)
                close7(3)
                pw0(1)
                out2(0)
                pw1(1)
                out2(1)
                for s in range(SLOTS):
                    ln_turn(5, s)
                def project(s, i):
                    if i == 0:
                        pe.wait_ge(xp_ready, s + 1)
                        if s == 1:
                            pe.wait_ge(v_ready, 1)
                    else:
                        pe.wait_ge(qk_ready, 2 * s + i)
                    if i < 2:
                        mm(M[2][:], Wqkv2[:, i, :], XP, start=True, stop=True).then_inc(qk_done, 1)
                    else:
                        for t in range(TILES):
                            last = mm(M[2][:, t * C:t * C + C], XP[:, t * P:t * P + P], Wqkv2[:, 2, :],
                                      start=True, stop=True)
                        last.then_inc(qk_done, 1)

                def lg(c):
                    hh, j = divmod(c, 2)
                    s = hh // HEADS
                    pe.wait_ge(qm_ready, hh + 1)
                    pe.wait_ge(qk_ready, 2 * s + 2)
                    if c >= 2:
                        pe.wait_ge(lg_copied, c - 1)
                    for q in range(2):
                        t = 2 * j + q
                        last = mm(M[c % 2][:, q * 256:q * 256 + 256],
                                  QM[hh % 3][:, t * P:t * P + P], Kc[s][:, j * 256:j * 256 + 256],
                                  start=True, stop=True)
                    last.then_inc(lg_done, 1)

                def pv(gr):
                    s, g = gr // 4, gr // 2 % 2
                    pe.wait_ge(pt_ready, 4 * gr + 4)
                    pe.wait_ge(v_ready, s + 1)
                    if gr in (4, 5):
                        pe.wait_ge(po_ready, 1)
                    bank = [M[5], TR[s]][g]
                    for j in range(IMGS):
                        for kt in range(2):
                            for x in range(2):
                                c = 4 * gr + 2 * x + j
                                h = c // 2 % HEADS
                                hq = h % 4
                                last = mm(bank[32 * hq:32 * hq + 32, j * 256:j * 256 + 256],
                                          Vh[s][:, 2 * j + kt, h, :], PT[c % 5][:, kt * 256:kt * 256 + 256],
                                          start=kt == 0, stop=kt == 1)
                    last.then_inc(pv_done, 1)

                def post(s, i):
                    if i < 2:
                        pe.wait_ge(po_ready, 2 * s + i + 1)
                        if i == 1:
                            pe.wait_ge(ot_ready, 2 * s + 1)
                        elif s == 0:
                            pe.wait_ge(v_ready, 2)
                        else:
                            pe.wait_ge(x_after_attn, 1)
                        turn(M[2], lambda t: PO[i][:, t * P:t * P + P], po_turned)
                    elif i == 2:
                        pe.wait_ge(ot_ready, 2 * s + 2)
                        turn(M[2], lambda t: OT[s][:, t].rearrange("p h d -> p (h d)"), ot_turned)
                    else:
                        pe.wait_ge(oc_ready, s + 1)
                        for t in range(TILES):
                            last = mm(M[2][:, t * C:t * C + C], OCf[s][:, t * P:t * P + P], Wo[:],
                                      start=True, stop=True)
                        last.then_inc(wo_done, 1)
                def rotate(s):
                    pe.wait_ge(xn_ready, ln_index(6, s) - 2)
                    if s == 0:
                        pe.wait_ge(lg_copied, UNITS - 1)
                    for t in range(TILES):
                        last = mm(M[3 * s][:, t * C:t * C + C], XN[s][:, t * P:t * P + P], Whad[:],
                                  start=True, stop=True)
                    last.then_inc(had_done, 1)

                def square_sums(s):
                    pe.wait_ge(had_sq, s + 1)
                    pe.wait_ge(lg_copied, UNITS)
                    if s == 1:
                        pe.wait_ge(ms_ready, 1)
                    mm(M[1][:, 2 * s:2 * s + 2], ones[:], hst[s][:, 0, :], start=True, stop=True)\
                        .then_inc(ss_done, 1)
                for i in range(3):
                    project(0, i)
                lg(0)
                lg(1)
                for c in range(UNITS):
                    if c + 2 < UNITS:
                        lg(c + 2)
                    if c == 30:
                        ln_turn(6, 0)
                    if c == 31:
                        rotate(0)
                    pe.wait_ge(pr_ready, c + 1)
                    if c >= 2:
                        pe.wait_ge(pt_ready, c - 1)
                    for kt in range(2):
                        for q in range(2):
                            last = tr(M[3 + c % 2][:, kt * 256 + q * P:kt * 256 + q * P + P],
                                      PR[c % 2][:, q * 256 + kt * P:q * 256 + kt * P + P], ident[:])
                    last.then_inc(pt_done, 1)
                    if c % 4 == 0 and c > 0:
                        pv(c // 4 - 1)
                    if c in (7, 8, 9):
                        project(1, c - 7)
                    if c in (18, 20, 22, 24):
                        post(0, (c - 18) // 2)
                    if c == 28:
                        post(1, 0)
                square_sums(0)
                pv(UNITS // 4 - 1)
                for i in range(1, 4):
                    post(1, i)
                ln_turn(6, 1)
                rotate(1)
                ln_turn(7, 0)
                square_sums(1)
                ln_turn(7, 1)
                for s in range(SLOTS):
                    logits(2, 7, s, Wg3)
                for s in range(SLOTS):
                    for i in range(5):
                        c = 5 * s + i
                        n = P if i < 4 else 64
                        if c >= 2:
                            pe.wait_ge(gu_ready, c - 1)
                        mm(M[c % 2][0:n, :], Wgate[:, i, 0:n], XN[s][:], start=True, stop=True)\
                            .then_inc(gate_done, 1)
                        mm(M[2 + c % 2][0:n, :], Wup[:, i, 0:n], XN[s][:], start=True, stop=True)\
                            .then_inc(upp_done, 1)
                        if c == 1:
                            for j in range(SLOTS):
                                comb_turn(2, j)
                for s in range(SLOTS):
                    pe.wait_ge(gus_pool, 2 * s + 2)
                    pe.wait_ge(gus_ready, 2 * s + 2)
                    for t in range(TILES):
                        for i in range(5):
                            n = P if i < 4 else 64
                            last = mm(M[4 + s][:, t * C:t * C + C], GU[s][i][0:n, t * P:t * P + P],
                                      Wdown[0:n, i, :], start=i == 0, stop=i == 4)
                    last.then_inc(moe_done, 1)
                for s in range(SLOTS):
                    pe.wait_ge(x_final, s + 1)
                    turn(TR[s], lambda t: X[s][:, t, :], xf_turned)
                next_pass(pe, "pe")


def layout(inputs):
    f = {k: np.asarray(v) for k, v in inputs.items()}
    T = np.ascontiguousarray
    rep = lambda v: T(np.broadcast_to(np.asarray(v).reshape(1, -1), (P, np.asarray(v).size)))
    o = {}
    o["x"] = T(f["x"].reshape(B, C, HW).transpose(1, 0, 2))
    o["ident"] = np.eye(P, dtype=np.float32)
    o["taps"] = rep(np.concatenate([f["L0_conv_up_filter"], f["L0_conv_down_filter"]]))
    hh, ww = np.divmod(np.arange(P), SIDE)
    y = np.arange(UP)
    mA = np.stack([y[None, :] - 2 * (hh[:, None] + 8 * h) for h in (0, 1)], 1)
    mB = y[None, :] - 2 * ww[:, None]
    r, xx = np.divmod(np.arange(P), UP)
    dA = np.stack([11 - (ROWS_M * k + r[:, None] - 2 * (8 * h + np.arange(8)[None, :])) for h, k in DOWN_PARTS], 1)
    dB = 11 - (xx[:, None] - 2 * np.arange(SIDE)[None, :])
    o["tap_no"] = T(np.concatenate([m.reshape(P, -1) for m in (mA, mB, dA, dB)], 1).astype(np.float32))
    o["conv_bias"] = rep(f["L0_conv_bias"])
    o["Wg0"] = f["L0_ffn_Wg"]
    o["pick"] = rep(np.arange(E, 0, -1).astype(np.float32))
    o["W1"] = T(f["L0_ffn_W1"].transpose(1, 0, 2))
    o["b1"] = T(f["L0_ffn_b1"].reshape(E * 4, P).T)
    o["W2"] = T(f["L0_ffn_W2"].reshape(E, 4, P, C).transpose(2, 0, 1, 3))
    o["b2T"] = T(f["L0_ffn_b2"].T)
    perm = (24 * np.arange(16)[None, :, None] + 8 * np.arange(3)[:, None, None] + np.arange(8)).reshape(3, P)
    o["Wqkv1"] = T(f["L1_conv_qkv_w"].reshape(384, C)[perm].transpose(2, 0, 1))
    o["dw1"] = T(f["L1_conv_agg_dw_w"].reshape(384, 25)[perm].transpose(1, 0, 2))
    pw = f["L1_conv_agg_pw_w"].reshape(384, 8)[perm]
    blk = np.zeros((P, 3, P), np.float32)
    co = np.arange(P)
    for ci in range(8):
        blk[8 * (co // 8) + ci, :, co] = pw[:, co, ci].T
    o["pw1T"] = blk
    o["proj"] = T(f["L1_conv_proj_w"].reshape(C, 2, P).transpose(2, 1, 0))
    o["headmask1"] = (co[:, None] // 8 == co[None, :] // 8).astype(np.float32)
    o["bn"] = T(np.stack([f["L1_conv_bn_gamma"], f["L1_conv_bn_beta"], f["L1_conv_bn_mean"], f["L1_conv_bn_var"]], 1))
    o["ins"] = T(f["L1_ffn_Ins_tk"][0].T)
    o["modw"] = T(np.concatenate([f["L1_ffn_rmod_w"], f["L1_ffn_gamma_w"].T], 1))
    o["beta_w"] = T(f["L1_ffn_beta_w"].transpose(1, 0, 2))
    o["exp_bT"] = T(f["L1_ffn_expert_b"].T)
    o["Wg1"] = f["L1_ffn_gate_w"]
    o["Wexp"] = T(f["L1_ffn_expert_w"].transpose(1, 0, 2))
    order = np.concatenate([np.arange(128, 256), np.arange(64, 128), np.arange(32, 64), np.arange(0, 32)])
    o["Win"] = T(f["L2_conv_w_in"][order].T)
    b = f["L2_conv_b_in"][order]
    pad = lambda v, lo=0: np.concatenate([np.zeros(lo, np.float32), v, np.zeros(P - lo - v.size, np.float32)])
    o["bin"] = T(np.stack([b[0:128], pad(b[128:224])], 1))
    o["bpa"] = pad(b[224:256], 64).reshape(P, 1)
    dorder = order[:224] - 32
    d = f["L2_conv_dw_w"].reshape(224, 49)[dorder]
    o["dw2"] = T(np.stack([d[0:128], np.concatenate([d[128:], np.zeros((32, 49), np.float32)])], 1))
    db = f["L2_conv_dw_b"][dorder]
    o["dwb2"] = T(np.stack([db[0:128], pad(db[128:])], 1))
    z = np.zeros((P, 64), np.float32)
    z[64:96] = f["L2_conv_pw0_w"].T
    o["pwT0"] = z
    o["pwb0"] = pad(f["L2_conv_pw0_b"]).reshape(P, 1)
    z = np.zeros((P, P), np.float32)
    z[0:64] = f["L2_conv_pw1_w"].T
    o["pwT1"] = z
    o["pwb1"] = f["L2_conv_pw1_b"].reshape(P, 1)
    o["Wout"] = T(f["L2_conv_w_out"].T)
    o["bout"] = rep(f["L2_conv_b_out"])
    o["posw"] = T(np.concatenate([f["L2_ffn_pos_w"].reshape(C, 3), f["L2_ffn_pos_b"].reshape(C, 1)], 1))
    o["Wqkv2"] = T(f["L2_ffn_qkv_w"].reshape(3, C, C).transpose(2, 0, 1))
    o["bqk"] = T(f["L2_ffn_qkv_b"][0:256].reshape(2, C).T)
    o["bv"] = rep(f["L2_ffn_qkv_b"][256:384])
    o["headmask2"] = (co[:, None] // HD == np.arange(HEADS)[None, :]).astype(np.float32)
    o["Wo"] = T(f["L2_ffn_wo_w"].T)
    o["bo"] = rep(f["L2_ffn_wo_b"])
    z = np.zeros((P, P), np.float32)
    z[0:64, 0:64] = f["L3_conv_aux_matrix"]
    z[64:, 64:] = f["L3_conv_aux_matrix"]
    o["Whad"] = z
    o["Wg3"] = f["L3_ffn_router"]

    def pairs(we, ws):
        z = np.zeros((P, 5, P), np.float32)
        z[:, 0:4] = we.reshape(4, 2, C, 64).transpose(2, 0, 1, 3).reshape(C, 4, P)
        z[:, 4, 0:64] = ws
        return z
    o["Wgate"] = pairs(f["L3_ffn_W_gate"], f["L3_ffn_shared_gate"])
    o["Wup"] = pairs(f["L3_ffn_W_up"], f["L3_ffn_shared_up"])
    z = np.zeros((P, 5, C), np.float32)
    z[:, 0:4] = f["L3_ffn_W_down"].reshape(4, P, C).transpose(1, 0, 2)
    z[0:64, 4] = f["L3_ffn_shared_down"]
    o["Wdown"] = z
    for pack, parts in PACKS.items():
        o[pack] = np.concatenate([o.pop(name).reshape(P, -1) for name, _ in parts], 1)
    return {k: np.ascontiguousarray(v) for k, v in o.items()}


def kernel(**inputs):
    import concourse.bacc as _bacc
    from concourse.bass_utils import run_bass_kernel_spmd as _run

    nc = _bacc.Bacc("TRN2", target_bir_lowering=False, num_devices=1)
    arrays, args = {}, {}
    for name, v in layout(inputs).items():
        arrays[f"in_{name}_dram"] = v
        args[name] = nc.dram_tensor(f"in_{name}_dram", v.shape, mybir.dt.from_np(v.dtype), kind="ExternalInput").ap()
    out = nc.dram_tensor("out_0_dram", (B, C, HW), mybir.dt.float32, kind="ExternalOutput").ap()
    args["out"] = out.rearrange("b c n -> c b n")
    metaformer(nc, args)
    r = _run(nc, [arrays], core_ids=[0])
    return r.results[0]["out_0_dram"].reshape(B, C, SIDE, SIDE)
```
